# Optimizing a Trainium2 kernel written in Bass

```python
import numpy as np
import jax
import jax.numpy as jnp

def _softmax(x, axis=-1):
    return jax.nn.softmax(x, axis=axis)

def _gelu(x):
    return jax.nn.gelu(x, approximate=True)

def _silu(x):
    return jax.nn.silu(x)

def _sigmoid(x):
    return jax.nn.sigmoid(x)

def _layernorm(x, axis=-1, eps=1e-05):
    m = jnp.mean(x, axis=axis, keepdims=True)
    v = jnp.var(x, axis=axis, keepdims=True)
    return (x - m) / jnp.sqrt(v + eps)

def _scatter_add(tgt, idx, src, axis=0):
    return tgt.at[idx].add(src)

def _segment_sum(src, seg, n):
    return jax.ops.segment_sum(src, seg, n)
kernel_name = 'mk_recurrent_d4_jaxref_r8_f28c00'

def setup_inputs(seed: int=0):
    np.random.seed(seed)
    _w = jnp.asarray

    def _L0_attn_setup():
        import jax, jax.numpy as jnp
        import numpy as np
        import math
        NUM_HEADS = 16
        D_MODEL = 128
        B, T = (1, 512)
        key = jax.random.key(seed)
        kx, kq, kk, kv, ko = jax.random.split(key, 5)
        s = 1.0 / math.sqrt(D_MODEL)
        return {'x': jax.random.normal(kx, (B, T, D_MODEL), dtype=jnp.float32), 'Wq': jax.random.normal(kq, (D_MODEL, D_MODEL), dtype=jnp.float32) * s, 'Wk': jax.random.normal(kk, (D_MODEL, D_MODEL), dtype=jnp.float32) * s, 'Wv': jax.random.normal(kv, (D_MODEL, D_MODEL), dtype=jnp.float32) * s, 'Wo': jax.random.normal(ko, (D_MODEL, D_MODEL), dtype=jnp.float32) * s}
    _L0_attn_in = _L0_attn_setup()

    def _L0_ffn_setup():
        import jax, jax.numpy as jnp
        import numpy as np
        import math
        B, S, H = (8, 512, 128)
        E, I, K = (8, 256, 2)
        CAP_FACTOR = 1.0

        def _router(x, expert_embeddings):
            dot = jnp.einsum('bsh,eh->bse', x, expert_embeddings)
            n = dot.shape[0] * dot.shape[1]
            dot2 = dot.reshape(n, E)
            vals, idx = jax.lax.top_k(dot2, K)
            rows = jnp.arange(n)[:, None]
            masked = jnp.full_like(dot2, -jnp.inf).at[rows, idx].set(vals)
            return jax.nn.softmax(masked, axis=-1)
        key = jax.random.key(seed)
        k1, k2, k3, k4 = jax.random.split(key, 4)

        def kaiming(k, shape):
            bound = math.sqrt(3.0 / shape[-1])
            return jax.random.uniform(k, shape, jnp.float32, -bound, bound)
        x = jax.random.normal(k1, (B, S, H), jnp.float32)
        expert_embeddings = kaiming(k2, (E, H))
        first_linear = kaiming(k3, (E, I, H))
        second_linear = kaiming(k4, (E, H, I))
        return {'x': x, 'expert_embeddings': expert_embeddings, 'first_linear': first_linear, 'second_linear': second_linear}
    _L0_ffn_in = _L0_ffn_setup()

    def _L1_attn_setup():
        import jax, jax.numpy as jnp
        import numpy as np
        HEADS = 8
        K_SIZE = 64
        key = jax.random.key(seed)
        k1, k2, k3, k4 = jax.random.split(key, 4)
        B, C, D = (4, 256, 128)
        return {'x': jax.random.normal(k1, (B, C, D), dtype=jnp.float32), 'Mq': jax.random.normal(k2, (D, HEADS * K_SIZE), dtype=jnp.float32) * 0.02, 'Mk': jax.random.normal(k3, (D, HEADS * K_SIZE), dtype=jnp.float32) * 0.02, 'Mv': jax.random.normal(k4, (D, 128), dtype=jnp.float32) * 0.02}
    _L1_attn_in = _L1_attn_setup()

    def _L1_ffn_setup():
        import jax, jax.numpy as jnp
        import numpy as np
        DIM = 128
        DEPTH = 2
        HEADS = 8
        DIM_HEAD = 64
        WINDOW = 64
        INNER = HEADS * DIM_HEAD
        HID = int(DIM * 4 * 2 / 3)
        B, N = (2, 1024)
        QK_SCALE = 8.0

        def shift_token(t):
            t1, t2 = jnp.split(t, 2, axis=-1)
            t2 = jnp.pad(t2, ((0, 0), (1, 0), (0, 0)))[:, :-1]
            return jnp.concatenate([t1, t2], axis=-1)

        def l2norm(t):
            return t / jnp.clip(jnp.linalg.norm(t, axis=-1, keepdims=True), 1e-12)

        def rotate_half(x):
            x1, x2 = jnp.split(x, 2, axis=-1)
            return jnp.concatenate([-x2, x1], axis=-1)

        def rotary_xpos(q, k):
            n = q.shape[-2]
            half_idx = jnp.arange(0, DIM_HEAD, 2, dtype=jnp.float32)
            inv_freq = 1.0 / 10000.0 ** (half_idx / DIM_HEAD)
            t = jnp.arange(n, dtype=jnp.float32)
            freqs = t[:, None] * inv_freq[None, :]
            freqs = jnp.concatenate([freqs, freqs], axis=-1)
            base = (half_idx + 0.4 * DIM_HEAD) / (1.4 * DIM_HEAD)
            power = (t - n // 2) / float(WINDOW // 2)
            scale = base[None, :] ** power[:, None]
            scale = jnp.concatenate([scale, scale], axis=-1)
            cos, sin = (jnp.cos(freqs), jnp.sin(freqs))
            q = q * cos * scale + rotate_half(q) * sin * scale
            k = k * cos / scale + rotate_half(k) * sin / scale
            return (q, k)

        def local_attention(q, k, v):
            b, h, n, d = q.shape
            w = n // WINDOW
            bq = q.reshape(b, h, w, WINDOW, d) * QK_SCALE
            bk = k.reshape(b, h, w, WINDOW, d)
            bv = v.reshape(b, h, w, WINDOW, d)

            def look_around(t):
                p = jnp.pad(t, ((0, 0), (0, 0), (1, 0), (0, 0), (0, 0)))
                return jnp.concatenate([p[:, :, :w], p[:, :, 1:]], axis=3)
            bk, bv = (look_around(bk), look_around(bv))
            bt = jnp.arange(n).reshape(w, WINDOW)
            btp = jnp.pad(bt, ((1, 0), (0, 0)), constant_values=-1)
            btk = jnp.concatenate([btp[:w], btp[1:]], axis=1)
            sim = jnp.einsum('bhwid,bhwjd->bhwij', bq, bk)
            i = bt[:, :, None]
            j = btk[:, None, :]
            mask = (i < j) | (i > j + WINDOW) | (j == -1)
            sim = jnp.where(mask, -jnp.finfo(sim.dtype).max, sim)
            attn = jax.nn.softmax(sim, axis=-1)
            out = jnp.einsum('bhwij,bhwjd->bhwid', attn, bv)
            return out.reshape(b, h, n, d)

        def _layer(x, wqkv, qs, ksc, wo, lg, lb, w1, b1, w2, b2):
            b, n, _ = x.shape
            h = shift_token(x)
            qkv = h @ wqkv
            q, k, v = jnp.split(qkv, 3, axis=-1)
            to_heads = lambda t: t.reshape(b, n, HEADS, DIM_HEAD).transpose(0, 2, 1, 3)
            q, k, v = (to_heads(q), to_heads(k), to_heads(v))
            q = l2norm(q) * qs
            k = l2norm(k) * ksc
            q, k = rotary_xpos(q, k)
            o = local_attention(q, k, v)
            o = o.transpose(0, 2, 1, 3).reshape(b, n, INNER)
            x = x + o @ wo
            h = shift_token(x)
            mu = h.mean(-1, keepdims=True)
            var = h.var(-1, keepdims=True)
            h = (h - mu) / jnp.sqrt(var + 1e-05) * lg + lb
            h = h @ w1 + b1
            a, g = jnp.split(h, 2, axis=-1)
            h = a * jax.nn.gelu(g, approximate=False)
            x = x + h @ w2 + b2
            return x
        key = jax.random.key(seed)
        ks = jax.random.split(key, 6)
        return {'x': jax.random.normal(ks[0], (B, N, DIM), jnp.float32), 'wqkv': jax.random.normal(ks[1], (DEPTH, DIM, 3 * INNER), jnp.float32) * 0.02, 'q_scale': jnp.ones((DEPTH, DIM_HEAD), jnp.float32), 'k_scale': jnp.ones((DEPTH, DIM_HEAD), jnp.float32), 'wo': jax.random.normal(ks[2], (DEPTH, INNER, DIM), jnp.float32) * 0.02, 'ln_g': jnp.ones((DEPTH, DIM), jnp.float32), 'ln_b': jnp.zeros((DEPTH, DIM), jnp.float32), 'w1': jax.random.normal(ks[3], (DEPTH, DIM, 2 * HID), jnp.float32) * 0.02, 'b1': jnp.zeros((DEPTH, 2 * HID), jnp.float32), 'w2': jax.random.normal(ks[4], (DEPTH, HID, DIM), jnp.float32) * 0.02, 'b2': jnp.zeros((DEPTH, DIM), jnp.float32)}
    _L1_ffn_in = _L1_ffn_setup()

    def _L2_attn_setup():
        import jax, jax.numpy as jnp
        import numpy as np
        DIM = 128
        HEADS = 16
        HEAD_DIM = DIM // HEADS
        SCALE = HEAD_DIM ** (-0.5)

        def apply_rope(x, theta=10000.0):
            n, d = (x.shape[2], x.shape[3])
            seq = jnp.arange(n, dtype=jnp.float32)
            inv = 1.0 / theta ** (jnp.arange(0, d, 2, dtype=jnp.float32) / d)
            freqs = seq[:, None] * inv[None, :]
            cos = jnp.cos(freqs)[None, None]
            sin = jnp.sin(freqs)[None, None]
            x1, x2 = jnp.split(x, 2, axis=-1)
            return jnp.concatenate([x1 * cos - x2 * sin, x1 * sin + x2 * cos], axis=-1)
        key = jax.random.key(seed)
        ks = jax.random.split(key, 7)
        s = DIM ** (-0.5)
        return {'x': jax.random.normal(ks[0], (2, 256, DIM), dtype=jnp.float32), 'Wqkv': jax.random.normal(ks[1], (3 * DIM, DIM), dtype=jnp.float32) * s, 'bqkv': jax.random.normal(ks[2], (3 * DIM,), dtype=jnp.float32) * 0.02, 'Wpre': jax.random.normal(ks[3], (HEADS, HEADS), dtype=jnp.float32) * HEADS ** (-0.5), 'Wpost': jax.random.normal(ks[4], (HEADS, HEADS), dtype=jnp.float32) * HEADS ** (-0.5), 'Wout': jax.random.normal(ks[5], (DIM, DIM), dtype=jnp.float32) * s, 'bout': jax.random.normal(ks[6], (DIM,), dtype=jnp.float32) * 0.02}
    _L2_attn_in = _L2_attn_setup()

    def _L2_ffn_setup():
        import jax, jax.numpy as jnp
        import numpy as np
        E = 8
        K = 2
        R = 64
        ALPHA = 128.0
        SCALING = ALPHA / R
        key = jax.random.key(seed)
        k0, k1, k2, k3 = jax.random.split(key, 4)
        B, S, D = (4, 512, 128)
        x = jax.random.normal(k0, (B, S, D), jnp.float32)
        Wg = jax.random.normal(k1, (E, D), jnp.float32) * 0.02
        bg = jnp.zeros((E,), jnp.float32)
        W1 = jax.random.normal(k2, (E, R, D), jnp.float32) * (1.0 / np.sqrt(D))
        W2 = jax.random.normal(k3, (E, D, R), jnp.float32) * 0.02
        return {'x': x, 'Wg': Wg, 'bg': bg, 'W1': W1, 'W2': W2}
    _L2_ffn_in = _L2_ffn_setup()

    def _L3_attn_setup():
        import jax, jax.numpy as jnp
        import numpy as np
        B, S, D_MODEL, D_K = (4, 256, 128, 1)
        D_QKV = D_MODEL * D_K
        MASK_NEG = -9000000000000000.0

        def _scaled_dot_product_attention(q, k, v):
            d_k = k.shape[-1]
            scores = jnp.einsum('bqd,bkd->bqk', q, k) / jnp.sqrt(jnp.float32(d_k))
            scores = jnp.triu(scores, k=0)
            scores = jnp.where(scores == 0, MASK_NEG, scores)
            attn = jax.nn.softmax(scores, axis=-1)
            return jnp.einsum('bqk,bkd->bqd', attn, v)
        key = jax.random.key(seed)
        kx, kw = jax.random.split(key)
        x = jax.random.normal(kx, (B, S, D_MODEL), dtype=jnp.float32)
        W = jax.random.normal(kw, (D_MODEL, 3 * D_QKV), dtype=jnp.float32) * (1.0 / np.sqrt(D_MODEL))
        return {'x': x, 'W': W}
    _L3_attn_in = _L3_attn_setup()

    def _L3_ffn_setup():
        import jax, jax.numpy as jnp
        import numpy as np
        NUM_EXPERTS = 8
        IN_FEATURES = 128
        HIDDEN_FEATURES = 512
        GATE_DIM = 16
        EPS = 0.0001
        key = jax.random.key(seed)
        ks = jax.random.split(key, 7)
        hidden_states = jax.random.normal(ks[0], (1, 256, IN_FEATURES), dtype=jnp.float32)
        wg_red = jax.random.normal(ks[1], (GATE_DIM, IN_FEATURES), dtype=jnp.float32) * 0.02
        wg = jax.random.normal(ks[2], (NUM_EXPERTS, GATE_DIM), dtype=jnp.float32)
        w1 = jax.random.uniform(ks[3], (NUM_EXPERTS, IN_FEATURES, HIDDEN_FEATURES), dtype=jnp.float32)
        b1 = jax.random.uniform(ks[4], (NUM_EXPERTS, HIDDEN_FEATURES), dtype=jnp.float32)
        w2 = jax.random.uniform(ks[5], (NUM_EXPERTS, HIDDEN_FEATURES, IN_FEATURES), dtype=jnp.float32)
        b2 = jax.random.uniform(ks[6], (NUM_EXPERTS, IN_FEATURES), dtype=jnp.float32)
        return {'hidden_states': hidden_states, 'wg_red': wg_red, 'wg': wg, 'w1': w1, 'b1': b1, 'w2': w2, 'b2': b2}
    _L3_ffn_in = _L3_ffn_setup()
    _d = {'L0_attn_x': _L0_attn_in['x'], 'L0_attn_Wq': _L0_attn_in['Wq'], 'L0_attn_Wk': _L0_attn_in['Wk'], 'L0_attn_Wv': _L0_attn_in['Wv'], 'L0_attn_Wo': _L0_attn_in['Wo'], 'L0_ffn_expert_embeddings': _L0_ffn_in['expert_embeddings'], 'L0_ffn_first_linear': _L0_ffn_in['first_linear'], 'L0_ffn_second_linear': _L0_ffn_in['second_linear'], 'L1_attn_Mq': _L1_attn_in['Mq'], 'L1_attn_Mk': _L1_attn_in['Mk'], 'L1_attn_Mv': _L1_attn_in['Mv'], 'L1_ffn_wqkv': _L1_ffn_in['wqkv'], 'L1_ffn_q_scale': _L1_ffn_in['q_scale'], 'L1_ffn_k_scale': _L1_ffn_in['k_scale'], 'L1_ffn_wo': _L1_ffn_in['wo'], 'L1_ffn_ln_g': _L1_ffn_in['ln_g'], 'L1_ffn_ln_b': _L1_ffn_in['ln_b'], 'L1_ffn_w1': _L1_ffn_in['w1'], 'L1_ffn_b1': _L1_ffn_in['b1'], 'L1_ffn_w2': _L1_ffn_in['w2'], 'L1_ffn_b2': _L1_ffn_in['b2'], 'L2_attn_Wqkv': _L2_attn_in['Wqkv'], 'L2_attn_bqkv': _L2_attn_in['bqkv'], 'L2_attn_Wpre': _L2_attn_in['Wpre'], 'L2_attn_Wpost': _L2_attn_in['Wpost'], 'L2_attn_Wout': _L2_attn_in['Wout'], 'L2_attn_bout': _L2_attn_in['bout'], 'L2_ffn_Wg': _L2_ffn_in['Wg'], 'L2_ffn_bg': _L2_ffn_in['bg'], 'L2_ffn_W1': _L2_ffn_in['W1'], 'L2_ffn_W2': _L2_ffn_in['W2'], 'L3_attn_W': _L3_attn_in['W'], 'L3_ffn_wg_red': _L3_ffn_in['wg_red'], 'L3_ffn_wg': _L3_ffn_in['wg'], 'L3_ffn_w1': _L3_ffn_in['w1'], 'L3_ffn_b1': _L3_ffn_in['b1'], 'L3_ffn_w2': _L3_ffn_in['w2'], 'L3_ffn_b2': _L3_ffn_in['b2']}
    _x0 = _d['L0_attn_x']
    _d['L0_attn_x'] = jax.random.normal(jax.random.fold_in(jax.random.key(seed), 1), (16, 512, 128), dtype=_x0.dtype)
    del _x0
    return _d

def reference(L0_attn_x, L0_attn_Wq, L0_attn_Wk, L0_attn_Wv, L0_attn_Wo, L0_ffn_expert_embeddings, L0_ffn_first_linear, L0_ffn_second_linear, L1_attn_Mq, L1_attn_Mk, L1_attn_Mv, L1_ffn_wqkv, L1_ffn_q_scale, L1_ffn_k_scale, L1_ffn_wo, L1_ffn_ln_g, L1_ffn_ln_b, L1_ffn_w1, L1_ffn_b1, L1_ffn_w2, L1_ffn_b2, L2_attn_Wqkv, L2_attn_bqkv, L2_attn_Wpre, L2_attn_Wpost, L2_attn_Wout, L2_attn_bout, L2_ffn_Wg, L2_ffn_bg, L2_ffn_W1, L2_ffn_W2, L3_attn_W, L3_ffn_wg_red, L3_ffn_wg, L3_ffn_w1, L3_ffn_b1, L3_ffn_w2, L3_ffn_b2):

    def _L0_attn_ref(x, Wq, Wk, Wv, Wo):
        import jax, jax.numpy as jnp
        import numpy as np
        import math
        NUM_HEADS = 16
        D_MODEL = 128
        B, T = (1, 512)
        Bx, Tx, D = x.shape
        H = NUM_HEADS
        dk = D // H
        q = (x @ Wq.T).reshape(Bx, Tx, H, dk)
        k = (x @ Wk.T).reshape(Bx, Tx, H, dk)
        v = (x @ Wv.T).reshape(Bx, Tx, H, dk)
        scores = jnp.einsum('bthd,bshd->bhts', q, k) / math.sqrt(dk)
        causal_mask = jnp.triu(jnp.ones((Tx, Tx), dtype=bool), k=1)
        scores = jnp.where(causal_mask, jnp.float32(-jnp.inf), scores).astype(jnp.float32)
        attn = jax.nn.softmax(scores, axis=-1)
        out = jnp.einsum('bhts,bshd->bthd', attn, v).reshape(Bx, Tx, D)
        return out @ Wo.T

    def _L0_ffn_ref(x, expert_embeddings, first_linear, second_linear):
        import jax, jax.numpy as jnp
        import numpy as np
        import math
        B, S, H = (8, 512, 128)
        E, I, K = (8, 256, 2)
        CAP_FACTOR = 1.0

        def _router(x, expert_embeddings):
            dot = jnp.einsum('bsh,eh->bse', x, expert_embeddings)
            n = dot.shape[0] * dot.shape[1]
            dot2 = dot.reshape(n, E)
            vals, idx = jax.lax.top_k(dot2, K)
            rows = jnp.arange(n)[:, None]
            masked = jnp.full_like(dot2, -jnp.inf).at[rows, idx].set(vals)
            return jax.nn.softmax(masked, axis=-1)
        batch, seq, hidden = x.shape
        n_tokens = batch * seq
        expert_capacity = math.ceil(n_tokens / E * CAP_FACTOR)
        weights = _router(x, expert_embeddings)
        ones = (weights > 0).astype(weights.dtype)
        cap_ones = jnp.where(jnp.cumsum(ones, axis=0) <= expert_capacity, ones, 0.0)
        caw = weights * cap_ones
        vals, idx = jax.lax.top_k(caw.T, expert_capacity)
        index = idx.reshape(-1)
        x_flat = x.reshape(n_tokens, hidden)
        tokens = x_flat[index].reshape(E, expert_capacity, hidden)
        inter = jax.nn.relu(jnp.einsum('ech,eih->eci', tokens, first_linear))
        out = jnp.einsum('eci,ehi->ech', inter, second_linear)
        out = out * vals[:, :, None]
        final = jnp.zeros((n_tokens, hidden), x.dtype).at[index].add(out.reshape(-1, hidden))
        return final.reshape(x.shape)

    def _L1_attn_ref(x, Mq, Mk, Mv):
        import jax, jax.numpy as jnp
        import numpy as np
        HEADS = 8
        K_SIZE = 64
        B, C, _ = x.shape
        H, K = (HEADS, K_SIZE)
        V = Mv.shape[1] // H
        q = (x @ Mq).reshape(B, H, C, K)
        k = (x @ Mk).reshape(B, H, C, K)
        v = (x @ Mv).reshape(B, H, C, V)
        scores = jnp.einsum('bhqk,bhck->bhqc', q, k).reshape(B * H, C, C)
        att = jax.nn.softmax(scores / jnp.sqrt(jnp.float32(K)), axis=1)
        att4 = att.reshape(B, C, H, C)
        out = jnp.einsum('bqhc,bhcd->bqhd', att4, v)
        return out.reshape(B, C, H * V)

    def _L1_ffn_ref(x, wqkv, q_scale, k_scale, wo, ln_g, ln_b, w1, b1, w2, b2):
        import jax, jax.numpy as jnp
        import numpy as np
        DIM = 128
        DEPTH = 2
        HEADS = 8
        DIM_HEAD = 64
        WINDOW = 64
        INNER = HEADS * DIM_HEAD
        HID = int(DIM * 4 * 2 / 3)
        B, N = (2, 1024)
        QK_SCALE = 8.0

        def shift_token(t):
            t1, t2 = jnp.split(t, 2, axis=-1)
            t2 = jnp.pad(t2, ((0, 0), (1, 0), (0, 0)))[:, :-1]
            return jnp.concatenate([t1, t2], axis=-1)

        def l2norm(t):
            return t / jnp.clip(jnp.linalg.norm(t, axis=-1, keepdims=True), 1e-12)

        def rotate_half(x):
            x1, x2 = jnp.split(x, 2, axis=-1)
            return jnp.concatenate([-x2, x1], axis=-1)

        def rotary_xpos(q, k):
            n = q.shape[-2]
            half_idx = jnp.arange(0, DIM_HEAD, 2, dtype=jnp.float32)
            inv_freq = 1.0 / 10000.0 ** (half_idx / DIM_HEAD)
            t = jnp.arange(n, dtype=jnp.float32)
            freqs = t[:, None] * inv_freq[None, :]
            freqs = jnp.concatenate([freqs, freqs], axis=-1)
            base = (half_idx + 0.4 * DIM_HEAD) / (1.4 * DIM_HEAD)
            power = (t - n // 2) / float(WINDOW // 2)
            scale = base[None, :] ** power[:, None]
            scale = jnp.concatenate([scale, scale], axis=-1)
            cos, sin = (jnp.cos(freqs), jnp.sin(freqs))
            q = q * cos * scale + rotate_half(q) * sin * scale
            k = k * cos / scale + rotate_half(k) * sin / scale
            return (q, k)

        def local_attention(q, k, v):
            b, h, n, d = q.shape
            w = n // WINDOW
            bq = q.reshape(b, h, w, WINDOW, d) * QK_SCALE
            bk = k.reshape(b, h, w, WINDOW, d)
            bv = v.reshape(b, h, w, WINDOW, d)

            def look_around(t):
                p = jnp.pad(t, ((0, 0), (0, 0), (1, 0), (0, 0), (0, 0)))
                return jnp.concatenate([p[:, :, :w], p[:, :, 1:]], axis=3)
            bk, bv = (look_around(bk), look_around(bv))
            bt = jnp.arange(n).reshape(w, WINDOW)
            btp = jnp.pad(bt, ((1, 0), (0, 0)), constant_values=-1)
            btk = jnp.concatenate([btp[:w], btp[1:]], axis=1)
            sim = jnp.einsum('bhwid,bhwjd->bhwij', bq, bk)
            i = bt[:, :, None]
            j = btk[:, None, :]
            mask = (i < j) | (i > j + WINDOW) | (j == -1)
            sim = jnp.where(mask, -jnp.finfo(sim.dtype).max, sim)
            attn = jax.nn.softmax(sim, axis=-1)
            out = jnp.einsum('bhwij,bhwjd->bhwid', attn, bv)
            return out.reshape(b, h, n, d)

        def _layer(x, wqkv, qs, ksc, wo, lg, lb, w1, b1, w2, b2):
            b, n, _ = x.shape
            h = shift_token(x)
            qkv = h @ wqkv
            q, k, v = jnp.split(qkv, 3, axis=-1)
            to_heads = lambda t: t.reshape(b, n, HEADS, DIM_HEAD).transpose(0, 2, 1, 3)
            q, k, v = (to_heads(q), to_heads(k), to_heads(v))
            q = l2norm(q) * qs
            k = l2norm(k) * ksc
            q, k = rotary_xpos(q, k)
            o = local_attention(q, k, v)
            o = o.transpose(0, 2, 1, 3).reshape(b, n, INNER)
            x = x + o @ wo
            h = shift_token(x)
            mu = h.mean(-1, keepdims=True)
            var = h.var(-1, keepdims=True)
            h = (h - mu) / jnp.sqrt(var + 1e-05) * lg + lb
            h = h @ w1 + b1
            a, g = jnp.split(h, 2, axis=-1)
            h = a * jax.nn.gelu(g, approximate=False)
            x = x + h @ w2 + b2
            return x
        for l in range(DEPTH):
            x = _layer(x, wqkv[l], q_scale[l], k_scale[l], wo[l], ln_g[l], ln_b[l], w1[l], b1[l], w2[l], b2[l])
        return x

    def _L2_attn_ref(x, Wqkv, bqkv, Wpre, Wpost, Wout, bout):
        import jax, jax.numpy as jnp
        import numpy as np
        DIM = 128
        HEADS = 16
        HEAD_DIM = DIM // HEADS
        SCALE = HEAD_DIM ** (-0.5)

        def apply_rope(x, theta=10000.0):
            n, d = (x.shape[2], x.shape[3])
            seq = jnp.arange(n, dtype=jnp.float32)
            inv = 1.0 / theta ** (jnp.arange(0, d, 2, dtype=jnp.float32) / d)
            freqs = seq[:, None] * inv[None, :]
            cos = jnp.cos(freqs)[None, None]
            sin = jnp.sin(freqs)[None, None]
            x1, x2 = jnp.split(x, 2, axis=-1)
            return jnp.concatenate([x1 * cos - x2 * sin, x1 * sin + x2 * cos], axis=-1)
        b, n, _ = x.shape
        qkv = x @ Wqkv.T + bqkv
        q, k, v = jnp.split(qkv, 3, axis=-1)
        reshape = lambda t: t.reshape(b, n, HEADS, HEAD_DIM).transpose(0, 2, 1, 3)
        q, k, v = (reshape(q), reshape(k), reshape(v))
        q = apply_rope(q)
        k = apply_rope(k)
        logits = jnp.einsum('bhid,bhjd->bhij', q, k) * SCALE
        logits = jnp.einsum('bhij,gh->bgij', logits, Wpre)
        attn = jax.nn.softmax(logits, axis=-1)
        attn = jnp.einsum('bhij,gh->bgij', attn, Wpost)
        out = jnp.einsum('bhij,bhjd->bhid', attn, v)
        out = out.transpose(0, 2, 1, 3).reshape(b, n, DIM)
        return out @ Wout.T + bout

    def _L2_ffn_ref(x, Wg, bg, W1, W2):
        import jax, jax.numpy as jnp
        import numpy as np
        E = 8
        K = 2
        R = 64
        ALPHA = 128.0
        SCALING = ALPHA / R
        orig_shape = x.shape
        D = orig_shape[-1]
        xf = x.reshape(-1, D)
        logits = xf @ Wg.T + bg
        top_gates, top_idx = jax.lax.top_k(logits, K)
        top_gates = jax.nn.softmax(top_gates, axis=-1)
        h = jax.nn.gelu(jnp.einsum('nd,erd->enr', xf, W1), approximate=False)
        eout = SCALING * jnp.einsum('enr,edr->ned', h, W2)
        sel = jnp.take_along_axis(eout, top_idx[:, :, None], axis=1)
        out = jnp.sum(top_gates[:, :, None] * sel, axis=1)
        return out.reshape(orig_shape)

    def _L3_attn_ref(x, W):
        import jax, jax.numpy as jnp
        import numpy as np
        B, S, D_MODEL, D_K = (4, 256, 128, 1)
        D_QKV = D_MODEL * D_K
        MASK_NEG = -9000000000000000.0

        def _scaled_dot_product_attention(q, k, v):
            d_k = k.shape[-1]
            scores = jnp.einsum('bqd,bkd->bqk', q, k) / jnp.sqrt(jnp.float32(d_k))
            scores = jnp.triu(scores, k=0)
            scores = jnp.where(scores == 0, MASK_NEG, scores)
            attn = jax.nn.softmax(scores, axis=-1)
            return jnp.einsum('bqk,bkd->bqd', attn, v)
        qkv = jnp.einsum('bsd,df->bsf', x, W)
        q, k, v = jnp.split(qkv, 3, axis=-1)
        return _scaled_dot_product_attention(q, k, v)

    def _L3_ffn_ref(hidden_states, wg_red, wg, w1, b1, w2, b2):
        import jax, jax.numpy as jnp
        import numpy as np
        NUM_EXPERTS = 8
        IN_FEATURES = 128
        HIDDEN_FEATURES = 512
        GATE_DIM = 16
        EPS = 0.0001
        b, t, c = hidden_states.shape
        x = hidden_states.reshape(-1, c)
        xr = x @ wg_red.T
        wg_unit = wg / jnp.maximum(jnp.linalg.norm(wg, axis=1, keepdims=True), EPS)
        logits = xr @ wg_unit.T
        gates = jax.nn.softmax(logits, axis=1)
        indices_s = jnp.argmax(gates, axis=1)
        scores = jnp.max(gates, axis=1)
        E = wg.shape[0]
        out = jnp.zeros_like(x)
        for e in range(E):
            mask = (indices_s == e).astype(x.dtype)[:, None]
            h = jax.nn.gelu(x @ w1[e] + b1[e], approximate=False)
            out = out + mask * (h @ w2[e] + b2[e])
        out = out * scores[:, None]
        return out.reshape(b, t, c)
    x = L0_attn_x
    xn = _layernorm(x, axis=-1)
    s = _L0_attn_ref(xn, L0_attn_Wq, L0_attn_Wk, L0_attn_Wv, L0_attn_Wo)
    g = _silu(_L0_ffn_ref(xn, L0_ffn_expert_embeddings, L0_ffn_first_linear, L0_ffn_second_linear))
    x = x + s * g
    xn = _layernorm(x, axis=-1)
    s = _L1_attn_ref(xn, L1_attn_Mq, L1_attn_Mk, L1_attn_Mv)
    g = _silu(_L1_ffn_ref(xn, L1_ffn_wqkv, L1_ffn_q_scale, L1_ffn_k_scale, L1_ffn_wo, L1_ffn_ln_g, L1_ffn_ln_b, L1_ffn_w1, L1_ffn_b1, L1_ffn_w2, L1_ffn_b2))
    x = x + s * g
    xn = _layernorm(x, axis=-1)
    s = _L2_attn_ref(xn, L2_attn_Wqkv, L2_attn_bqkv, L2_attn_Wpre, L2_attn_Wpost, L2_attn_Wout, L2_attn_bout)
    g = _silu(_L2_ffn_ref(xn, L2_ffn_Wg, L2_ffn_bg, L2_ffn_W1, L2_ffn_W2))
    x = x + s * g
    xn = _layernorm(x, axis=-1)
    s = _L3_attn_ref(xn, L3_attn_W)
    g = _silu(_L3_ffn_ref(xn, L3_ffn_wg_red, L3_ffn_wg, L3_ffn_w1, L3_ffn_b1, L3_ffn_w2, L3_ffn_b2))
    x = x + s * g
    return x

_drawn_inputs = setup_inputs


def setup_inputs(seed=0):
    import zlib

    import numpy as np

    out = dict(_drawn_inputs(seed))
    spreads = {'L1_ffn_q_scale': (1.0, 0.6),
     'L1_ffn_k_scale': (1.0, 0.6),
     'L1_ffn_ln_g': (1.0, 0.6),
     'L1_ffn_ln_b': (0.0, 0.8),
     'L1_ffn_b1': (0.0, 0.8),
     'L1_ffn_b2': (0.0, 0.8),
     'L2_ffn_bg': (0.0, 0.8)}
    factors = {'L1_attn_Mq': 8.0,
     'L1_attn_Mk': 8.0,
     'L1_attn_Mv': 3.372,
     'L1_ffn_wqkv': 8.0,
     'L1_ffn_wo': 8.0,
     'L1_ffn_w1': 8.0,
     'L1_ffn_w2': 8.0,
     'L2_attn_Wqkv': 5.839,
     'L2_attn_bqkv': 8.0,
     'L2_attn_Wpre': 5.745,
     'L2_attn_Wpost': 5.266,
     'L2_attn_Wout': 5.064,
     'L2_attn_bout': 64.0,
     'L2_ffn_Wg': 6.421,
     'L2_ffn_W1': 5.78,
     'L2_ffn_W2': 4.855,
     'L3_ffn_b1': 64.0,
     'L3_ffn_b2': 64.0,
     'L3_ffn_wg_red': 6.791,
     'L3_ffn_wg': 7.359,
     'L3_ffn_w1': 8.0,
     'L3_ffn_w2': 8.0}
    for name, (base, spread) in spreads.items():
        noise = np.random.default_rng([zlib.crc32(name.encode()), seed]).standard_normal(out[name].shape)
        drawn = base * np.exp(spread * noise) if base else spread * noise
        out[name] = jnp.asarray(drawn.astype(out[name].dtype))
    for name, factor in factors.items():
        out[name] = (out[name] * factor).astype(out[name].dtype)
    return out
```

```python
import math
from contextlib import ExitStack

import numpy as np

import concourse.bass as bass
from concourse import mybir

F32 = mybir.dt.float32
BF16 = mybir.dt.bfloat16
ALU = mybir.AluOpType
ACT = mybir.ActivationFunctionType
AX = mybir.AxisListType

P = 128
D = 128
T = 512
NC = T // P
NB = 16
EPS = 1e-5
NEG_BIG = -1.0e30
MASK_NEG = -9000000000000000.0


class Chain:

    def __init__(self, eng, sem):
        self.eng, self.sem, self.n = eng, sem, 0

    def restart(self):
        self.eng.sem_clear(self.sem)
        self.n = 0

    def __call__(self, ins):
        self.n += 1
        ins.then_inc(self.sem, 1)
        self.eng.wait_ge(self.sem, self.n)


class Rows:

    def __init__(self, nc, ctx, tag, x_dram):
        def sb(name, shape, dt=F32):
            return ctx.enter_context(nc.sbuf_tensor(f"{tag}_{name}", shape, dt))

        def sem(name):
            return nc.alloc_semaphore(f"{tag}_{name}")

        self.nc = nc
        self.x_dram = x_dram.rearrange("b (c p) d -> b p c d", p=P)
        self.x = sb("x", [P, NC, D])
        self.stats = sb("stats", [P, NC, 6])
        self.moments = sb("moments", [P, NC, 2])
        self.var_eps = sb("var_eps", [P, NC])
        self.rstd = sb("rstd", [P, NC])
        self.half = sb("half", [P, NC])
        self.xn = sb("xn", [P, NC, D])
        self.xT = sb("xT", [D, T])
        self.x_loaded = sem("x_loaded")
        self.x_free = sem("x_free")
        self.half_ready = sem("half_ready")
        self.var_ready = sem("var_ready")
        self.rstd_ready = sem("rstd_ready")
        self.xn_ready = sem("xn_ready")
        self.xn_turned = sem("xn_turned")
        self.xT_ready = sem("xT_ready")

    def load(self, sp, b):
        sp.wait_ge(self.x_free, b + 1)
        sp.dma_start(self.x[:], self.x_dram[b]).then_inc(self.x_loaded, 16)

    def before_loop(self, dve):
        dve.memset(self.half[:], -0.5).then_inc(self.half_ready, 1)
        dve.memset(self.stats[:], 0.0).then_inc(self.x_free, 1)

    def root(self, pool, b):
        pool.wait_ge(self.half_ready, 1)
        pool.wait_ge(self.var_ready, b + 1)
        pool.tensor_tensor(self.rstd[:], self.var_eps[:], self.half[:], ALU.pow).then_inc(self.rstd_ready, 1)

    def normalise(self, dve, chain, b):
        dve.wait_ge(self.x_loaded, b * 16 + 16)
        for c in range(NC):
            last = dve.bn_stats(self.stats[:, c, :], self.x[:, c, :])
        chain(last)
        for c in range(NC):
            last = dve.bn_aggr(self.moments[:, c, :], self.stats[:, c, :])
        chain(last)
        dve.tensor_scalar(self.var_eps[:], self.moments[:, :, 1], EPS, None, ALU.add).then_inc(self.var_ready, 1)
        dve.wait_ge(self.rstd_ready, b + 1)
        for c in range(NC):
            last = dve.tensor_scalar(self.xn[:, c, :], self.x[:, c, :], self.moments[:, c, 0:1],
                                     self.rstd[:, c:c + 1], ALU.subtract, ALU.mult)
            last.then_inc(self.xn_ready, 1)
        dve.wait_ge(self.xn_ready, b * NC + NC)
        dve.sem_inc(self.x_free, 1)

    def turn(self, pe, bank, ident, b):
        pe.wait_ge(self.xn_ready, b * NC + NC)
        for c in range(NC):
            last = pe.transpose(bank[:, c * P:(c + 1) * P], self.xn[:, c, :], ident[:])
        last.then_inc(self.xn_turned, 1)

    def keep_turned(self, act, bank, b):
        act.wait_ge(self.xn_turned, b + 1)
        act.activation(self.xT[:], bank[:], ACT.Copy).then_inc(self.xT_ready, 1)


def attention_phase(nc, dram, tag, kind, x_dram, s_dram, batches):
    H = 1 if kind == "triu" else 16
    DH = D // H
    U = NC * H
    causal, mixed, triu = kind == "causal", kind == "mixed", kind == "triu"

    with nc.cleanup_on_exit(), ExitStack() as ctx:
        def sb(name, shape, dt=F32):
            return ctx.enter_context(nc.sbuf_tensor(f"{tag}_{name}", shape, dt))

        def sem(name):
            return nc.alloc_semaphore(f"{tag}_{name}")

        def ps(name):
            return ctx.enter_context(nc.psum_tensor(f"{tag}_{name}_ps", [P, 512], F32))

        rows = Rows(nc, ctx, tag, x_dram)
        ident = sb("ident", [P, P])
        n_w = {"causal": 3, "mixed": 5, "triu": 3}[kind]
        w_in = sb("w_in", [D, n_w, D])
        qT, kT = sb("qT", [D, T]), sb("kT", [D, T])
        v = sb("v", [P, NC, D])
        probs = sb("probs", [P, 2, T])
        probsT = sb("probsT", [P, 2, T])
        neg_max = sb("neg_max", [P, 2])
        row_sum = sb("row_sum", [P, U])
        inv_sum = sb("inv_sum", [P, U])
        o = sb("o", [P, NC, D])
        s_out = sb("s_out", [P, NC, D])
        if not triu:
            w_out = sb("w_out", [D, D])
            oT = sb("oT", [D, T])
            head_scale = sb("head_scale", [D, H])
            q_head = sb("q_head", [D, 4, P])
        if causal:
            ident16 = sb("ident16", [P, P], BF16)
            mask16, mask = sb("mask16", [P, P], BF16), sb("mask", [P, P])
        if mixed:
            b_in = sb("b_in", [D, 4])
            b_v = sb("b_v", [P, D])
            b_out = sb("b_out", [P, D])
            cos, sin = sb("cos", [D, T]), sb("sin", [D, T])
            cos_part, sin_part = sb("cos_part", [D, T]), sb("sin_part", [D, T])
            post = sb("post", [P, H, D])
            v_post = sb("v_post", [P, H, NC, D])
        if triu:
            keep = sb("keep", [P, NC, T])
            masked = sb("masked", [P, 2, T])
            is_zero = sb("is_zero", [P, T])
        scores_ps = [ps("scores0"), ps("scores1")]
        turned_ps = [ps("turned0"), ps("turned1")]
        out_ps = [ps("out0"), ps("out1")]
        a_ps, b_ps = ps("a"), ps("b")

        weights = sem("weights")
        mask_ready = sem("mask_ready")
        projected = sem("projected")
        q_ready, k_ready, v_ready = sem("q_ready"), sem("k_ready"), sem("v_ready")
        v_post_ready = sem("v_post_ready")
        q_head_ready = sem("q_head_ready")
        scores_ready = sem("scores_ready")
        max_ready = sem("max_ready")
        probs_ready = sem("probs_ready")
        probs_turned = sem("probs_turned")
        probsT_ready = sem("probsT_ready")
        out_ready = sem("out_ready")
        o_taken = sem("o_taken")
        o_turned = sem("o_turned")
        oT_ready = sem("oT_ready")
        y_ready = sem("y_ready")
        s_ready = sem("s_ready")
        s_stored = sem("s_stored")
        s_free = sem("s_free")
        dve_chain = sem("dve_chain")

        loads = [(ident[:], dram["ident"])]
        if causal:
            loads += [(w_in[:], dram["L0_w_in"].rearrange("i n o -> i n o")), (w_out[:], dram["L0_WoT"]),
                      (head_scale[:], dram["L0_head_scale"]), (mask[:], dram["causal"])]
        if mixed:
            loads += [(w_in[:], dram["L2_w_in"]), (w_out[:], dram["L2_WoutT"]),
                      (head_scale[:], dram["L2_pre"]), (b_in[:], dram["L2_b_in"]),
                      (b_v[:], dram["L2_b_v"].partition_broadcast(P)),
                      (b_out[:], dram["L2_attn_bout"].partition_broadcast(P)),
                      (cos[:], dram["L2_cos"]), (sin[:], dram["L2_sin"]),
                      (post[:], dram["L2_post"].partition_broadcast(P))]
        if triu:
            loads += [(w_in[:], dram["L3_w_in"]), (keep[:], dram["keep_triu"])]
        SCORE_SCALE = 1.0 / math.sqrt(DH)
        s_rows = s_dram.rearrange("b (c p) d -> b p c d", p=P)
        used = (lambda c: (c + 1) * P) if causal else (lambda c: T)

        block = ctx.enter_context(nc.Block())

        @block.sync
        def _(sp):
            for dst, src in loads:
                sp.dma_start(dst, src).then_inc(weights, 16)
            with sp.Fori(0, batches) as b:
                rows.load(sp, b)

        @block.gpsimd
        def _(pool):
            pool.sem_inc(s_free, 1)
            pool.wait_ge(weights, 16 * len(loads))
            with pool.Fori(0, batches) as b:
                rows.root(pool, b)
                if not triu:
                    pool.wait_ge(q_ready, b + 1)
                    if mixed:
                        pool.wait_ge(v_ready, b + 1)
                    for u in range(U):
                        c, h = divmod(u, H)
                        if u >= 4:
                            pool.wait_ge(scores_ready, b * U + (u - 3))
                        pool.tensor_tensor(q_head[:, u % 4, :], qT[:, c * P:(c + 1) * P],
                                           head_scale[:, h:h + 1].to_broadcast([D, P]),
                                           ALU.mult).then_inc(q_head_ready, 1)
                        if mixed and c == 0:
                            pool.tensor_tensor(v_post[:, h, :, :], v[:],
                                               post[:, h:h + 1, :].to_broadcast([P, NC, D]),
                                               ALU.mult).then_inc(v_post_ready, 1)
                pool.wait_ge(s_ready, b + 1)
                pool.dma_start(s_rows[b], s_out[:]).then_inc(s_stored, 16)
                pool.wait_ge(s_stored, b * 16 + 16)
                pool.sem_inc(s_free, 1)

        @block.scalar
        def _(act):
            with act.Fori(0, batches) as b:
                rows.keep_turned(act, a_ps, b)
                n_p = 5 if mixed else 3
                if not mixed:
                    act.wait_ge(projected, b * n_p + 1)
                    act.activation(qT[:], b_ps[:], ACT.Copy,
                                   scale=(SCORE_SCALE if triu else 1.0)).then_inc(q_ready, 1)
                    act.wait_ge(projected, b * n_p + 2)
                    act.activation(kT[:], a_ps[:], ACT.Copy).then_inc(k_ready, 1)
                    act.wait_ge(projected, b * n_p + 3)
                    act.activation(v[:].rearrange("p c d -> p (c d)"), out_ps[0][:], ACT.Copy).then_inc(v_ready, 1)

                def exps(u):
                    c, h = divmod(u, H)
                    act.wait_ge(max_ready, b * U + (u + 1))
                    if u >= 2:
                        act.wait_ge(probs_turned, b * U + (u - 1))
                    src = masked[:, u % 2, :] if triu else scores_ps[u % 2][:, 0:used(c)]
                    act.activation(probs[:, u % 2, 0:used(c)], src, ACT.Exp, bias=neg_max[:, u % 2:u % 2 + 1],
                                   scale=1.0, accum_out=row_sum[:, u:u + 1]).then_inc(probs_ready, 1)

                def keep_probsT(u):
                    act.wait_ge(probs_turned, b * U + (u + 1))
                    if u >= 2:
                        act.wait_ge(out_ready, b * U + (u - 1))
                    act.activation(probsT[:, u % 2, :], turned_ps[u % 2][:], ACT.Copy).then_inc(probsT_ready, 1)

                for i in range(U + 1):
                    if i < U:
                        exps(i)
                    if i >= 1 and not causal:
                        keep_probsT(i - 1)
                if not triu:
                    act.wait_ge(o_turned, b + 1)
                    act.activation(oT[:], a_ps[:], ACT.Copy).then_inc(oT_ready, 1)
                if causal:
                    act.wait_ge(y_ready, b + 1)
                    act.wait_ge(s_free, b + 1)
                    act.activation(s_out[:].rearrange("p c d -> p (c d)"), b_ps[:], ACT.Copy).then_inc(s_ready, 1)

        @block.vector
        def _(dve):
            chain = Chain(dve, dve_chain)
            rows.before_loop(dve)
            dve.wait_ge(weights, 16 * len(loads))
            if causal:
                dve.tensor_copy(ident16[:], ident[:]).then_inc(mask_ready, 1)
                dve.tensor_copy(mask16[:], mask[:]).then_inc(mask_ready, 1)
            with dve.Fori(0, batches) as b:
                chain.restart()
                rows.normalise(dve, chain, b)
                if mixed:
                    for n, (plain, swapped, dst, ready) in enumerate(
                            [(b_ps, scores_ps[0], qT, q_ready), (a_ps, scores_ps[1], kT, k_ready)]):
                        dve.wait_ge(projected, b * 5 + 2 * n + 1)
                        dve.scalar_tensor_tensor(cos_part[:], plain[:], b_in[:, 2 * n:2 * n + 1], cos[:],
                                                 ALU.add, ALU.mult)
                        dve.wait_ge(projected, b * 5 + 2 * n + 2)
                        chain(dve.scalar_tensor_tensor(sin_part[:], swapped[:], b_in[:, 2 * n + 1:2 * n + 2],
                                                       sin[:], ALU.add, ALU.mult))
                        dve.tensor_tensor(dst[:], cos_part[:], sin_part[:], ALU.add).then_inc(ready, 1)
                        dve.wait_ge(ready, b + 1)
                    dve.wait_ge(projected, b * 5 + 5)
                    dve.tensor_tensor(v[:], out_ps[0][:].rearrange("p (c d) -> p c d", c=NC),
                                      b_v[:].unsqueeze(1).to_broadcast([P, NC, D]),
                                      ALU.add).then_inc(v_ready, 1)

                def row_max(u):
                    c, h = divmod(u, H)
                    dve.wait_ge(scores_ready, b * U + (u + 1))
                    if u >= 2:
                        dve.wait_ge(probs_ready, b * U + (u - 1))
                    src = scores_ps[u % 2][:, 0:used(c)]
                    if triu:
                        m = masked[:, u % 2, :]
                        chain(dve.tensor_tensor(m, src, keep[:, c, :], ALU.mult))
                        chain(dve.tensor_scalar(is_zero[:], m, 0.0, MASK_NEG, ALU.is_equal, ALU.mult))
                        chain(dve.tensor_tensor(m, m, is_zero[:], ALU.add))
                        src = m
                    dve.tensor_reduce(neg_max[:, u % 2:u % 2 + 1], src, AX.X, ALU.max,
                                      negate=True).then_inc(max_ready, 1)

                def keep_probsT(u):
                    c = u // H
                    dve.wait_ge(probs_turned, b * U + (u + 1))
                    if u >= 2:
                        dve.wait_ge(out_ready, b * U + (u - 1))
                    dve.tensor_copy(probsT[:, u % 2, 0:used(c)],
                                    turned_ps[u % 2][:, 0:used(c)]).then_inc(probsT_ready, 1)

                def take_heads(c):
                    dve.wait_ge(out_ready, b * U + (c + 1) * H)
                    chain(dve.reciprocal(inv_sum[:, c * H:(c + 1) * H], row_sum[:, c * H:(c + 1) * H]))
                    dve.tensor_tensor(o[:, c, :].rearrange("p (h d) -> p h d", h=H),
                                      out_ps[c % 2][:, 0:D].rearrange("p (h d) -> p h d", h=H),
                                      inv_sum[:, c * H:(c + 1) * H].unsqueeze(2).to_broadcast([P, H, DH]),
                                      ALU.mult).then_inc(o_taken, 1)

                def take_unit(u):
                    c, h = divmod(u, H)
                    dve.wait_ge(out_ready, b * U + (u + 1))
                    chain(dve.reciprocal(inv_sum[:, u:u + 1], row_sum[:, u:u + 1]))
                    dst = s_out if triu else o
                    if h == 0:
                        if triu and c == 0:
                            dve.wait_ge(s_free, b + 1)
                        dve.tensor_scalar(dst[:, c, :], out_ps[u % 2][:, 0:D], inv_sum[:, u:u + 1], None,
                                          ALU.mult).then_inc(o_taken, 1)
                    else:
                        dve.wait_ge(o_taken, b * U + u)
                        dve.scalar_tensor_tensor(o[:, c, :], out_ps[u % 2][:, 0:D], inv_sum[:, u:u + 1],
                                                 o[:, c, :], ALU.mult, ALU.add).then_inc(o_taken, 1)

                for i in range(U + 2):
                    if i < U:
                        row_max(i)
                    if causal and 1 <= i <= U:
                        keep_probsT(i - 1)
                    if causal and i >= 2 and (i - 1) % H == 0:
                        take_heads((i - 1) // H - 1)
                    if not causal and i >= 2:
                        take_unit(i - 2)
                if mixed:
                    dve.wait_ge(y_ready, b + 1)
                    dve.wait_ge(s_free, b + 1)
                    dve.tensor_tensor(s_out[:], b_ps[:].rearrange("p (c d) -> p c d", c=NC),
                                      b_out[:].unsqueeze(1).to_broadcast([P, NC, D]),
                                      ALU.add).then_inc(s_ready, 1)
                if triu:
                    dve.wait_ge(o_taken, b * U + U)
                    dve.sem_inc(s_ready, 1)

        @block.tensor
        def _(pe):
            pe.wait_ge(weights, 16 * len(loads))
            if causal:
                pe.wait_ge(mask_ready, 2)
            n_taken = NC if causal else U
            with pe.Fori(0, batches) as b:
                rows.turn(pe, a_ps, ident, b)
                pe.wait_ge(rows.xT_ready, b + 1)
                banks = [(0, b_ps), (3, scores_ps[0]), (1, a_ps), (4, scores_ps[1])] if mixed else \
                    [(0, b_ps), (1, a_ps)]
                for n, bank in banks:
                    pe.matmul(bank[:], w_in[:, n, :], rows.xT[:], start=True, stop=True).then_inc(projected, 1)
                for c in range(NC):
                    last = pe.matmul(out_ps[0][:, c * D:(c + 1) * D], rows.xT[:, c * P:(c + 1) * P], w_in[:, 2, :],
                                     start=True, stop=True)
                last.then_inc(projected, 1)
                pe.wait_ge(k_ready, b + 1)
                if triu:
                    pe.wait_ge(q_ready, b + 1)
                    pe.wait_ge(v_ready, b + 1)

                def scores(u):
                    c, h = divmod(u, H)
                    if not triu:
                        pe.wait_ge(q_head_ready, b * U + (u + 1))
                    if u >= 2:
                        pe.wait_ge(probs_ready, b * U + (u - 1))
                    q = qT[:, c * P:(c + 1) * P] if triu else q_head[:, u % 4, :]
                    if causal:
                        pe.matmul(scores_ps[u % 2][:, c * P:(c + 1) * P], ident16[:], mask16[:],
                                  start=True, stop=False, skip_group_check=True)
                    pe.matmul(scores_ps[u % 2][:, 0:used(c)], q, kT[:, 0:used(c)], start=not causal, stop=True,
                              skip_group_check=causal).then_inc(scores_ready, 1)

                def turn_probs(u):
                    c = u // H
                    pe.wait_ge(probs_ready, b * U + (u + 1))
                    if u >= 2:
                        pe.wait_ge(probsT_ready, b * U + (u - 1))
                    for j in range(used(c) // P):
                        last = pe.transpose(turned_ps[u % 2][:, j * P:(j + 1) * P],
                                            probs[:, u % 2, j * P:(j + 1) * P], ident[:])
                    last.then_inc(probs_turned, 1)

                def products(u):
                    c, h = divmod(u, H)
                    pe.wait_ge(probsT_ready, b * U + (u + 1))
                    if causal:
                        if u == 0:
                            pe.wait_ge(v_ready, b + 1)
                        if h == 0 and c >= 2:
                            pe.wait_ge(o_taken, b * NC + (c - 1))
                        dst = out_ps[c % 2][:, h * DH:(h + 1) * DH]
                    else:
                        if u == 0 and mixed:
                            pe.wait_ge(v_ready, b + 1)
                        if u >= 2:
                            pe.wait_ge(o_taken, b * U + (u - 1))
                        if mixed and c == 0:
                            pe.wait_ge(v_post_ready, b * H + (h + 1))
                        dst = out_ps[u % 2][:, 0:D]
                    n = used(c) // P
                    for j in range(n):
                        rhs = v_post[:, h, j, :] if mixed else v[:, j, h * DH:(h + 1) * DH]
                        last = pe.matmul(dst, probsT[:, u % 2, j * P:(j + 1) * P], rhs,
                                         start=(j == 0), stop=(j == n - 1))
                    last.then_inc(out_ready, 1)

                for i in range(U + 2):
                    if i < U:
                        scores(i)
                    if 1 <= i <= U:
                        turn_probs(i - 1)
                    if i >= 2:
                        products(i - 2)
                pe.wait_ge(o_taken, b * n_taken + n_taken)
                if not triu:
                    for c in range(NC):
                        last = pe.transpose(a_ps[:, c * P:(c + 1) * P], o[:, c, :], ident[:])
                    last.then_inc(o_turned, 1)
                    pe.wait_ge(oT_ready, b + 1)
                    for c in range(NC):
                        last = pe.matmul(b_ps[:, c * D:(c + 1) * D], oT[:, c * P:(c + 1) * P], w_out[:],
                                         start=True, stop=True)
                    last.then_inc(y_ready, 1)
                    pe.wait_ge(s_ready, b + 1)


class Gate:

    def __init__(self, nc, ctx, tag, x_dram, s_dram, out_dram):
        def sb(name):
            return ctx.enter_context(nc.sbuf_tensor(f"{tag}_{name}", [P, NC, D], F32))

        def sem(name):
            return nc.alloc_semaphore(f"{tag}_{name}")

        self.x_rows, self.s_rows, self.out_rows = (
            a.rearrange("b (c p) d -> b p c d", p=P) for a in (x_dram, s_dram, out_dram))
        self.x, self.s, self.y, self.e, self.out = sb("gx"), sb("gs"), sb("y"), sb("ge"), sb("gout")
        self.loaded = sem("gate_loaded")
        self.free = sem("gate_free")
        self.neg_abs_ready = sem("neg_abs_ready")
        self.exp_ready = sem("exp_ready")
        self.out_full = sem("out_full")
        self.stored = sem("stored")
        self.out_free = sem("out_free")

    def load(self, sp, b):
        sp.wait_ge(self.free, b + 1)
        sp.dma_start(self.x[:], self.x_rows[b]).then_inc(self.loaded, 16)
        sp.dma_start(self.s[:], self.s_rows[b]).then_inc(self.loaded, 16)

    def exp(self, act, b):
        act.wait_ge(self.neg_abs_ready, b + 1)
        act.activation(self.e[:], self.e[:], ACT.Exp).then_inc(self.exp_ready, 1)

    def finish(self, dve, chain, b):
        dve.scalar_tensor_tensor(self.e[:], self.y[:], -1.0, self.y[:], ALU.mult,
                                 ALU.min).then_inc(self.neg_abs_ready, 1)
        dve.wait_ge(self.loaded, b * 32 + 32)
        chain(dve.tensor_tensor(self.s[:], self.s[:], self.y[:], ALU.mult))
        dve.wait_ge(self.exp_ready, b + 1)
        chain(dve.scalar_tensor_tensor(self.y[:], self.y[:], 0.0, self.e[:], ALU.is_ge, ALU.max))
        dve.tensor_scalar(self.e[:], self.e[:], 1.0, None, ALU.add)
        chain(dve.tensor_tensor(self.s[:], self.s[:], self.y[:], ALU.mult))
        chain(dve.reciprocal(self.e[:], self.e[:]))
        chain(dve.tensor_tensor(self.s[:], self.s[:], self.e[:], ALU.mult))
        dve.wait_ge(self.out_free, b + 1)
        dve.tensor_tensor(self.out[:], self.s[:], self.x[:], ALU.add).then_inc(self.out_full, 1)
        dve.wait_ge(self.out_full, b + 1)
        dve.sem_inc(self.free, 1)

    def before_loop(self, pool):
        pool.sem_inc(self.free, 1)
        pool.sem_inc(self.out_free, 1)

    def store(self, pool, b):
        pool.wait_ge(self.out_full, b + 1)
        pool.dma_start(self.out_rows[b], self.out[:]).then_inc(self.stored, 16)
        pool.wait_ge(self.stored, b * 16 + 16)
        pool.sem_inc(self.out_free, 1)


def experts_phase(nc, dram, tag, kind, x_dram, s_dram, out_dram, batches):
    E = 8
    capacity, lora, top1 = kind == "capacity", kind == "lora", kind == "top1"
    I = {"capacity": 256, "lora": 64, "top1": 512}[kind]
    PAIR = max(1, P // I)
    K = max(1, I // P)
    G = E // PAIR
    CAPACITY = NB * T // E
    GR = 16

    with nc.cleanup_on_exit(), ExitStack() as ctx:
        def sb(name, shape, dt=F32):
            return ctx.enter_context(nc.sbuf_tensor(f"{tag}_{name}", shape, dt))

        def sem(name):
            return nc.alloc_semaphore(f"{tag}_{name}")

        def ps(name):
            return ctx.enter_context(nc.psum_tensor(f"{tag}_{name}_ps", [P, 512], F32))

        rows = Rows(nc, ctx, tag, x_dram)
        gate = Gate(nc, ctx, tag, x_dram, s_dram, out_dram)
        ident = sb("ident", [P, P])
        rank = sb("rank", [P, NC, E])
        w_gate = sb("w_gate", [D, GR if top1 else E])
        w1 = sb("w1", [D, G * K, P])
        w2 = sb("w2", [P, G * K, D])
        hidden = sb("hidden", [P, 2, K, T])
        logits = sb("logits", [P, NC, E])
        eq = sb("eq", [P, NC, E])
        first = sb("first", [P, NC, E])
        second = sb("second", [P, NC, E])
        top = sb("top", [P, NC])
        top_rank = sb("top_rank", [P, NC])
        top2 = sb("top2", [P, NC])
        diff = sb("diff", [P, NC, E] if top1 else [P, NC])
        weight = sb("weight", [P, NC])
        weight2 = sb("weight2", [P, NC])
        gates = sb("gates", [P, NC, E])
        gatesT = sb("gatesT", [E, T])
        if capacity:
            picked, zeros, count = sb("picked", [E, T]), sb("zeros", [E, T]), sb("count", [E, T])
            carry = sb("carry", [E, 1])
            capped = sb("capped", [P, NC, E])
        if lora:
            b_gate = sb("b_gate", [P, E])
        if top1:
            b1 = sb("b1", [P, E * K])
            b2 = sb("b2", [E, D])
            wg, wg_sq, wg_norm = sb("wg", [E, GR]), sb("wg_sq", [E, GR]), sb("wg_norm", [E, 1])
            wg_half = sb("wg_half", [E, 1])
            wg_unit = sb("wg_unit", [E, GR])
            wg_unitT = sb("wg_unitT", [GR, E])
            reducedT = sb("reducedT", [GR, T])
        hidden_ps = [ps("hidden0"), ps("hidden1")]
        y_ps = [ps("y0"), ps("y1")]
        a_ps, router_ps, gatesT_ps, extra_ps = ps("a"), ps("router"), ps("gatesT"), ps("extra")

        weights = sem("weights")
        gate_weights = sem("gate_weights")
        reduced_done, reduced_ready = sem("reduced_done"), sem("reduced_ready")
        logits_done = sem("logits_done")
        diff_ready, weight_ready = sem("diff_ready"), sem("weight_ready")
        gates_ready = sem("gates_ready")
        gates_turned, gatesT_ready = sem("gates_turned"), sem("gatesT_ready")
        back_turned = sem("back_turned")
        bias_done = sem("bias_done")
        hidden_done, hidden_ready = sem("hidden_done"), sem("hidden_ready")
        y_done, y_taken = sem("y_done"), sem("y_taken")
        dve_chain = sem("dve_chain")

        pre = {"capacity": "L0", "lora": "L2f", "top1": "L3f"}[kind]
        loads = [(ident[:], dram["ident"]), (rank[:], dram["rank"]), (w_gate[:], dram[f"{pre}_w_gate"]),
                 (w1[:], dram[f"{pre}_w1"]), (w2[:], dram[f"{pre}_w2"])]
        if lora:
            loads += [(b_gate[:], dram["L2_ffn_bg"].partition_broadcast(P))]
        if top1:
            loads += [(b1[:], dram["L3f_b1"]), (b2[:], dram["L3_ffn_b2"]), (wg[:], dram["L3_ffn_wg"])]
        act_fn = ACT.Relu if capacity else ACT.Gelu

        block = ctx.enter_context(nc.Block())

        @block.sync
        def _(sp):
            for dst, src in loads:
                sp.dma_start(dst, src).then_inc(weights, 16)
            with sp.Fori(0, batches) as b:
                rows.load(sp, b)
                gate.load(sp, b)

        @block.gpsimd
        def _(pool):
            gate.before_loop(pool)
            if top1:
                pool.wait_ge(gate_weights, 2)
                pool.tensor_tensor(wg_norm[:], wg_norm[:], wg_half[:], ALU.pow).then_inc(gate_weights, 1)
            with pool.Fori(0, batches) as b:
                rows.root(pool, b)
                gate.store(pool, b)

        @block.scalar
        def _(act):
            act.wait_ge(weights, 16 * len(loads))
            if top1:
                act.wait_ge(gate_weights, 5)
                act.activation(wg_unitT[:], a_ps[0:GR, 0:E], ACT.Copy).then_inc(gate_weights, 1)
            with act.Fori(0, batches) as b:
                rows.keep_turned(act, a_ps, b)
                if top1:
                    act.wait_ge(reduced_done, b + 1)
                    act.activation(reducedT[:], gatesT_ps[0:GR, :], ACT.Copy).then_inc(reduced_ready, 1)
                act.wait_ge(diff_ready, b + 1)
                if top1:
                    act.activation(diff[:], diff[:], ACT.Exp).then_inc(weight_ready, 1)
                else:
                    act.activation(diff[:], diff[:], ACT.Exp).then_inc(weight_ready, 1)
                for g in range(G):
                    if g >= 2:
                        act.wait_ge(y_done, b * E + (g - 1) * PAIR)
                    for k in range(K):
                        n = g * K + k
                        act.wait_ge(hidden_done, b * G * K + (n + 1))
                        bias = b1[:, n:n + 1] if top1 else 0.0
                        act.activation(hidden[:, g % 2, k, :], hidden_ps[n % 2][:], act_fn,
                                       bias=bias).then_inc(hidden_ready, 1)
                gate.exp(act, b)

        @block.vector
        def _(dve):
            chain = Chain(dve, dve_chain)
            rows.before_loop(dve)
            dve.wait_ge(weights, 16 * len(loads))
            if capacity:
                dve.memset(zeros[:], 0.0)
                chain(dve.memset(carry[:], 0.0))
            if top1:
                chain(dve.tensor_tensor(wg_sq[:], wg[:], wg[:], ALU.mult))
                dve.memset(wg_half[:], 0.5).then_inc(gate_weights, 1)
                dve.tensor_reduce(wg_norm[:], wg_sq[:], AX.X, ALU.add).then_inc(gate_weights, 1)
                dve.wait_ge(gate_weights, 3)
                chain(dve.tensor_scalar(wg_norm[:], wg_norm[:], 1e-4, None, ALU.max))
                chain(dve.reciprocal(wg_norm[:], wg_norm[:]))
                dve.tensor_scalar(wg_unit[:], wg[:], wg_norm[:], None, ALU.mult).then_inc(gate_weights, 1)

            def wide(a):
                return a[:].unsqueeze(2).to_broadcast([P, NC, E])

            def one_hot(dst, top_value):
                chain(dve.tensor_reduce(top_value[:], logits[:], AX.X, ALU.max))
                chain(dve.tensor_tensor(eq[:], logits[:], wide(top_value), ALU.is_equal))
                chain(dve.tensor_tensor(eq[:], eq[:], rank[:], ALU.mult))
                chain(dve.tensor_reduce(top_rank[:], eq[:], AX.X, ALU.max))
                chain(dve.tensor_tensor(dst[:], eq[:], wide(top_rank), ALU.is_equal))

            with dve.Fori(0, batches) as b:
                chain.restart()
                rows.normalise(dve, chain, b)
                dve.wait_ge(logits_done, b + 1)
                src = router_ps[:, 0:NC * E].rearrange("p (c e) -> p c e", c=NC)
                if lora:
                    chain(dve.tensor_tensor(logits[:], src, b_gate[:].unsqueeze(1).to_broadcast([P, NC, E]), ALU.add))
                else:
                    chain(dve.tensor_copy(logits[:], src))
                one_hot(first, top)
                if top1:
                    dve.tensor_tensor(diff[:], logits[:], wide(top), ALU.subtract).then_inc(diff_ready, 1)
                    dve.wait_ge(weight_ready, b + 1)
                    chain(dve.tensor_reduce(weight[:], diff[:], AX.X, ALU.add))
                    chain(dve.reciprocal(weight[:], weight[:]))
                    dve.tensor_tensor(gates[:], first[:], wide(weight), ALU.mult).then_inc(gates_ready, 1)
                    dve.wait_ge(gates_ready, b + 1)
                else:
                    chain(dve.scalar_tensor_tensor(logits[:], first[:], -3.0e38, logits[:], ALU.mult, ALU.add))
                    one_hot(second, top2)
                    dve.tensor_tensor(diff[:], top2[:], top[:], ALU.subtract).then_inc(diff_ready, 1)
                    dve.wait_ge(weight_ready, b + 1)
                    chain(dve.tensor_scalar(weight[:], diff[:], 1.0, None, ALU.add))
                    chain(dve.reciprocal(weight[:], weight[:]))
                    if lora:
                        chain(dve.tensor_scalar(weight[:], weight[:], 2.0, None, ALU.mult))
                    chain(dve.tensor_tensor(weight2[:], diff[:], weight[:], ALU.mult))
                    dve.tensor_tensor(first[:], first[:], wide(weight), ALU.mult)
                    chain(dve.tensor_tensor(second[:], second[:], wide(weight2), ALU.mult))
                    dve.tensor_tensor(gates[:], first[:], second[:], ALU.add).then_inc(gates_ready, 1)
                    dve.wait_ge(gates_ready, b + 1)
                if capacity:
                    dve.wait_ge(gates_turned, b + 1)
                    chain(dve.tensor_copy(gatesT[:], gatesT_ps[0:E, :]))
                    chain(dve.tensor_scalar(picked[:], gatesT[:], 0.0, None, ALU.is_gt))
                    chain(dve.tensor_tensor_scan(count[:], picked[:], zeros[:], carry[:], ALU.add, ALU.add))
                    dve.tensor_copy(carry[:], count[:, T - 1:T])
                    chain(dve.scalar_tensor_tensor(gatesT[:], count[:], float(CAPACITY), gatesT[:],
                                                   ALU.is_le, ALU.mult))
                    dve.sem_inc(gatesT_ready, 1)
                    dve.wait_ge(back_turned, b + 1)
                    chain(dve.tensor_copy(capped[:], router_ps[:, 64:64 + NC * E].rearrange("p (c e) -> p c e", c=NC)))
                if top1:
                    dve.wait_ge(gates_turned, b + 1)
                    dve.tensor_copy(gatesT[:], gatesT_ps[0:E, :]).then_inc(gatesT_ready, 1)
                    dve.wait_ge(bias_done, b + 1)
                    chain(dve.tensor_copy(gate.y[:], extra_ps[:].rearrange("p (c d) -> p c d", c=NC)))
                g_src = capped if capacity else gates
                for e in range(E):
                    dve.wait_ge(y_done, b * E + (e + 1))
                    for c in range(NC):
                        src = y_ps[e % 2][:, c * D:(c + 1) * D]
                        if e == 0 and not top1:
                            last = dve.tensor_scalar(gate.y[:, c, :], src, g_src[:, c, e:e + 1], None, ALU.mult)
                        else:
                            last = dve.scalar_tensor_tensor(gate.y[:, c, :], src, g_src[:, c, e:e + 1],
                                                            gate.y[:, c, :], ALU.mult, ALU.add)
                    last.then_inc(y_taken, 1)
                    dve.wait_ge(y_taken, b * E + (e + 1))
                gate.finish(dve, chain, b)

        @block.tensor
        def _(pe):
            pe.wait_ge(weights, 16 * len(loads))
            if top1:
                pe.wait_ge(gate_weights, 4)
                pe.transpose(a_ps[0:GR, 0:E], wg_unit[:], ident[0:E, 0:E]).then_inc(gate_weights, 1)
                pe.wait_ge(gate_weights, 6)
            with pe.Fori(0, batches) as b:
                rows.turn(pe, a_ps, ident, b)
                pe.wait_ge(rows.xT_ready, b + 1)
                if top1:
                    pe.matmul(gatesT_ps[0:GR, :], w_gate[:], rows.xT[:], start=True, stop=True).then_inc(reduced_done, 1)
                    pe.wait_ge(reduced_ready, b + 1)
                for c in range(NC):
                    lhsT = (reducedT if top1 else rows.xT)[:, c * P:(c + 1) * P]
                    last = pe.matmul(router_ps[:, c * E:(c + 1) * E], lhsT, (wg_unitT if top1 else w_gate)[:],
                                     start=True, stop=True)
                last.then_inc(logits_done, 1)

                def hidden_tiles(g):
                    for k in range(K):
                        n = g * K + k
                        if n >= 2:
                            pe.wait_ge(hidden_ready, b * G * K + (n - 1))
                        pe.matmul(hidden_ps[n % 2][:], w1[:, n, :], rows.xT[:], start=True,
                                  stop=True).then_inc(hidden_done, 1)

                def outputs(g):
                    pe.wait_ge(hidden_ready, b * G * K + (g + 1) * K)
                    for e in range(g * PAIR, (g + 1) * PAIR):
                        if e >= 2:
                            pe.wait_ge(y_taken, b * E + (e - 1))
                        lo = (e % PAIR) * I if PAIR > 1 else 0
                        hi = lo + I if PAIR > 1 else P
                        for c in range(NC):
                            for k in range(K):
                                last = pe.matmul(y_ps[e % 2][:, c * D:(c + 1) * D],
                                                 hidden[lo:hi, g % 2, k, c * P:(c + 1) * P],
                                                 w2[lo:hi, g * K + k, :], start=(k == 0), stop=(k == K - 1))
                        last.then_inc(y_done, 1)

                hidden_tiles(0)
                if not lora:
                    pe.wait_ge(gates_ready, b + 1)
                    for c in range(NC):
                        last = pe.transpose(gatesT_ps[0:E, c * P:(c + 1) * P], gates[:, c, :], ident[:])
                    last.then_inc(gates_turned, 1)
                    pe.wait_ge(gatesT_ready, b + 1)
                    hidden_tiles(1)
                    for c in range(NC):
                        if capacity:
                            last = pe.transpose(router_ps[:, 64 + c * E:64 + (c + 1) * E],
                                                gatesT[:, c * P:(c + 1) * P], ident[0:E, 0:E])
                        else:
                            last = pe.matmul(extra_ps[:, c * D:(c + 1) * D], gatesT[:, c * P:(c + 1) * P], b2[:],
                                             start=True, stop=True)
                    last.then_inc(back_turned if capacity else bias_done, 1)
                else:
                    hidden_tiles(1)
                outputs(0)
                for g in range(2, G):
                    hidden_tiles(g)
                    outputs(g - 1)
                outputs(G - 1)
                pe.wait_ge(y_taken, b * E + E)


def grouped_attention_phase(nc, dram, tag, x_dram, s_dram, batches):
    G, S, W = 8, 8, 64
    R2 = S // 2
    U = G * R2
    DV = D // S

    with nc.cleanup_on_exit(), ExitStack() as ctx:
        def sb(name, shape, dt=F32):
            return ctx.enter_context(nc.sbuf_tensor(f"{tag}_{name}", shape, dt))

        def sem(name):
            return nc.alloc_semaphore(f"{tag}_{name}")

        def ps(name):
            return ctx.enter_context(nc.psum_tensor(f"{tag}_{name}_ps", [P, 512], F32))

        rows = Rows(nc, ctx, tag, x_dram)
        ident = sb("ident", [P, P])
        wq, wk, wv = sb("wq", [D, S, W]), sb("wk", [D, S, W]), sb("wv", [D, D])
        qT = sb("qT", [W, G, S, T // G])
        kT = sb("kT", [W, G, S, T // G])
        xT_twice = sb("xT_twice", [D, G, 2, T // G])
        v = sb("v", [P, R2, G, DV])
        v_scaled = sb("v_scaled", [P, 3, G * DV])
        probs = sb("probs", [P, 3, T])
        neg_max = sb("neg_max", [P, 2])
        col_sum = sb("col_sum", [P, U])
        inv_sum = sb("inv_sum", [P, U])
        s_out = sb("s_out", [T // G, G, D])
        scores_ps = [ps("scores0"), ps("scores1")]
        out_ps = [ps("out0"), ps("out1")]
        a_ps = ps("a")
        v_ps = [ps("v0"), ps("v1")]

        weights = sem("weights")
        projected = sem("projected")
        q_kept, k_kept = sem("q_kept"), sem("k_kept")
        twice_ready = sem("twice_ready")
        v_projected, v_ready = sem("v_projected"), sem("v_ready")
        scores_ready, max_ready, probs_ready = sem("scores_ready"), sem("max_ready"), sem("probs_ready")
        v_scaled_ready = sem("v_scaled_ready")
        out_ready = sem("out_ready")
        o_taken = sem("o_taken")
        s_free, s_stored = sem("s_free"), sem("s_stored")
        dve_chain = sem("dve_chain")

        loads = [(ident[:], dram["ident"]), (wq[:].rearrange("p s w -> p (s w)"), dram["L1_Mq"]),
                 (wk[:].rearrange("p s w -> p (s w)"), dram["L1_Mk"]), (wv[:], dram["L1_Mv"])]
        s_rows = s_dram.rearrange("b (g t) d -> b t g d", g=G)
        banks = [scores_ps[0], out_ps[0], scores_ps[1], out_ps[1]]

        block = ctx.enter_context(nc.Block())

        @block.sync
        def _(sp):
            for dst, src in loads:
                sp.dma_start(dst, src).then_inc(weights, 16)
            with sp.Fori(0, batches) as b:
                rows.load(sp, b)

        @block.gpsimd
        def _(pool):
            pool.sem_inc(s_free, 1)
            with pool.Fori(0, batches) as b:
                rows.root(pool, b)
                pool.wait_ge(o_taken, b * G + G)
                pool.dma_start(s_rows[b], s_out[:]).then_inc(s_stored, 16)
                pool.wait_ge(s_stored, b * 16 + 16)
                pool.sem_inc(s_free, 1)

        @block.scalar
        def _(act):
            with act.Fori(0, batches) as b:
                rows.keep_turned(act, a_ps, b)
                act.activation(xT_twice[:], a_ps[:].rearrange("p (g t) -> p g t", g=G).unsqueeze(2)
                               .to_broadcast([D, G, 2, T // G]), ACT.Copy).then_inc(twice_ready, 1)
                for n in range(S):
                    act.wait_ge(projected, b * 2 * S + (2 * n + 1))
                    act.activation(qT[:, :, n, :], banks[2 * n % 4][0:W, :].rearrange("p (g t) -> p g t", g=G),
                                   ACT.Copy, scale=1.0 / math.sqrt(W)).then_inc(q_kept, 1)
                for u in range(U):
                    act.wait_ge(max_ready, b * U + (u + 1))
                    if u >= 3:
                        act.wait_ge(out_ready, b * U + (u - 2))
                    act.activation(probs[:, u % 3, :], scores_ps[u % 2][:], ACT.Exp, bias=neg_max[:, u % 2:u % 2 + 1],
                                   accum_out=col_sum[:, u:u + 1]).then_inc(probs_ready, 1)

        @block.vector
        def _(dve):
            chain = Chain(dve, dve_chain)
            rows.before_loop(dve)
            with dve.Fori(0, batches) as b:
                chain.restart()
                rows.normalise(dve, chain, b)
                for n in range(S):
                    dve.wait_ge(projected, b * 2 * S + (2 * n + 2))
                    dve.tensor_copy(kT[:, :, n, :], banks[(2 * n + 1) % 4][0:W, :]
                                    .rearrange("p (g t) -> p g t", g=G)).then_inc(k_kept, 1)
                dve.wait_ge(v_projected, b + 1)
                for half in range(2):
                    for n in range(2):
                        lo = half * 64
                        src = v_ps[n][lo:lo + 64, :].rearrange("p (g r two d) -> p r g two d", g=4, r=R2, two=2)
                        dve.tensor_copy(v[lo:lo + 64, :, n * 4:n * 4 + 4, :], src[:, :, :, half, :]).then_inc(v_ready, 1)
                dve.wait_ge(v_ready, b * 4 + 4)

                def col_max(u):
                    dve.wait_ge(scores_ready, b * U + (u + 1))
                    if u >= 2:
                        dve.wait_ge(probs_ready, b * U + (u - 1))
                    dve.tensor_reduce(neg_max[:, u % 2:u % 2 + 1], scores_ps[u % 2][:], AX.X, ALU.max,
                                      negate=True).then_inc(max_ready, 1)

                def scale_v(u):
                    dve.wait_ge(probs_ready, b * U + (u + 1))
                    chain(dve.reciprocal(inv_sum[:, u:u + 1], col_sum[:, u:u + 1]))
                    if u >= 3:
                        dve.wait_ge(out_ready, b * U + (u - 2))
                    dve.tensor_scalar(v_scaled[:, u % 3, :], v[:, u % R2, :, :].rearrange("p g d -> p (g d)"),
                                      inv_sum[:, u:u + 1], None, ALU.mult).then_inc(v_scaled_ready, 1)

                def take(g):
                    dve.wait_ge(out_ready, b * U + (g + 1) * R2)
                    if g == 0:
                        dve.wait_ge(s_free, b + 1)
                    dve.tensor_copy(s_out[:, g, :], out_ps[g % 2][0:T // G, 0:D]).then_inc(o_taken, 1)

                for i in range(U + 4):
                    if i < U:
                        col_max(i)
                    if 1 <= i <= U:
                        scale_v(i - 1)
                    if i >= 6 and (i - 3) % R2 == 0:
                        take((i - 3) // R2 - 1)

        @block.tensor
        def _(pe):
            pe.wait_ge(weights, 16 * len(loads))
            with pe.Fori(0, batches) as b:
                rows.turn(pe, a_ps, ident, b)
                pe.wait_ge(rows.xT_ready, b + 1)
                for n in range(2 * S):
                    if n >= 4:
                        pe.wait_ge(q_kept if n % 2 == 0 else k_kept, b * S + ((n - 4) // 2 + 1))
                    pe.matmul(banks[n % 4][0:W, :], (wq if n % 2 == 0 else wk)[:, n // 2, :], rows.xT[:],
                              start=True, stop=True).then_inc(projected, 1)
                pe.wait_ge(twice_ready, b + 1)
                for g in range(G):
                    last = pe.matmul(v_ps[g // 4][:, (g % 4) * D:(g % 4 + 1) * D],
                                     xT_twice[:, g, :, :].rearrange("p a t -> p (a t)"), wv[:],
                                     start=True, stop=True)
                last.then_inc(v_projected, 1)
                pe.wait_ge(q_kept, b * S + S)
                pe.wait_ge(k_kept, b * S + S)

                def scores(u):
                    g, r = divmod(u, R2)
                    if u >= 2:
                        pe.wait_ge(probs_ready, b * U + (u - 1))
                    pe.matmul(scores_ps[u % 2][:], kT[:, g, 2 * r:2 * r + 2, :].rearrange("p a t -> p (a t)"),
                              qT[:, g, :, :].rearrange("p s t -> p (s t)"), start=True,
                              stop=True).then_inc(scores_ready, 1)

                def products(u):
                    g, r = divmod(u, R2)
                    pe.wait_ge(v_scaled_ready, b * U + (u + 1))
                    if r == 0 and g >= 2:
                        pe.wait_ge(o_taken, b * G + (g - 1))
                    for n in range(S):
                        last = pe.matmul(out_ps[g % 2][0:T // G, n * DV:(n + 1) * DV],
                                         probs[:, u % 3, n * W:(n + 1) * W],
                                         v_scaled[:, u % 3, n * DV:(n + 1) * DV],
                                         start=(r == 0 and n == 0), stop=(r == R2 - 1), skip_group_check=True)
                    last.then_inc(out_ready, 1)

                for i in range(U + 2):
                    if i < U:
                        scores(i)
                    if i >= 2:
                        products(i - 2)
                pe.wait_ge(o_taken, b * G + G)


def local_transformer_phase(nc, dram, tag, x_dram, s_dram, out_dram, batches):
    L, H, W = 2, 8, 64
    HP = H // 2
    HID = 341
    HK = [128, 128, 85]
    N_ROT = 2 * NC
    N_PAIR = NC * HP
    KEYS = P + W

    with nc.cleanup_on_exit(), ExitStack() as ctx:
        def sb(name, shape, dt=F32):
            return ctx.enter_context(nc.sbuf_tensor(f"{tag}_{name}", shape, dt))

        def sem(name):
            return nc.alloc_semaphore(f"{tag}_{name}")

        def ps(name):
            return ctx.enter_context(nc.psum_tensor(f"{tag}_{name}_ps", [P, 512], F32))

        rows = Rows(nc, ctx, tag, x_dram)
        gate = Gate(nc, ctx, tag, x_dram, s_dram, out_dram)
        x = gate.y
        ident, ident16 = sb("ident", [P, P]), sb("ident16", [P, P], BF16)
        band16, band = sb("band16", [P, KEYS], BF16), sb("band", [P, KEYS])
        rotary = sb("rotary", [P, 4, NC, W])
        scale = sb("scale", [P, 2, L, W])
        turnings = sb("turnings", [P, L, 2, 2, NC, W])
        w_qkv = sb("w_qkv", [D, L, 3 * H * W])
        w_o = sb("w_o", [P, L, 4, D])
        ln_g, ln_b = sb("ln_g", [D, L]), sb("ln_b", [D, L])
        w1, w2 = sb("w1", [D, L, 2 * HID]), sb("w2", [P, L, 3, D])
        b1, b2 = sb("b1", [P, L, 2, 3]), sb("b2", [P, L, D])
        hT = sb("hT", [D, T])
        hnT = sb("hnT", [D, T])
        squares = sb("squares", [P, 2, T])
        sums = sb("sums", [P, 2, H])
        norms = sb("norms", [P, 2, H])
        neg_half = sb("neg_half", [P, H])
        cos_part, sin_part = sb("cos_part", [P, 2, T]), sb("sin_part", [P, 2, T])
        turned_rows = sb("turned_rows", [P, 2, T])
        qT, kT = sb("qT", [P, HP, T]), sb("kT", [P, HP, T])
        v = sb("v", [P, NC, H * W])
        probs = sb("probs", [P, 2, 2, 2 * P])
        probsT = sb("probsT", [P, 2, 4 * P])
        neg_max = sb("neg_max", [P, 2, 2])
        row_sum, inv_sum = sb("row_sum", [P, NC * H]), sb("inv_sum", [P, NC * H])
        o = sb("o", [P, NC, H * W])
        oT = sb("oT", [P, 2, 4, P])
        stats, moments = sb("lstats", [P, NC, 6]), sb("lmoments", [P, NC, 2])
        var_eps, rstd = sb("lvar_eps", [P, NC]), sb("lrstd", [P, NC])
        hn = sb("hn", [P, NC, D])
        gelu = sb("gelu", [P, 2, T])
        mixed = sb("mixed", [P, 3, T])
        a_ps, b_ps = ps("a"), ps("b")
        s_ps, t_ps, o_ps = [ps("s0"), ps("s1")], [ps("t0"), ps("t1")], [ps("o0"), ps("o1")]
        pair_banks = [(s_ps[0], a_ps), (s_ps[1], b_ps)]
        qkv_banks = [s_ps[0], s_ps[1], o_ps[0], o_ps[1]]

        weights = sem("weights")
        tables = sem("tables")
        x_ready = sem("x_ready")
        x_turned, hT_ready = sem("x_turned"), sem("hT_ready")
        qkv_done = sem("qkv_done")
        squares_ready, sums_ready, rotated = sem("squares_ready"), sem("sums_ready"), sem("rotated")
        rows_turned, rowsT_kept = sem("rows_turned"), sem("rowsT_kept")
        v_kept = sem("v_kept")
        scores_ready, max_ready, probs_ready = sem("scores_ready"), sem("max_ready"), sem("probs_ready")
        probs_turned, probsT_ready, out_ready = sem("probs_turned"), sem("probsT_ready"), sem("out_ready")
        o_taken, o_turned, oT_ready = sem("o_taken"), sem("o_turned"), sem("oT_ready")
        wo_done = sem("wo_done")
        h_back, lvar_ready, lrstd_ready = sem("h_back"), sem("lvar_ready"), sem("lrstd_ready")
        hn_ready, hn_turned, hnT_ready = sem("hn_ready"), sem("hn_turned"), sem("hnT_ready")
        up_done, gelu_ready, mixed_ready = sem("up_done"), sem("gelu_ready"), sem("mixed_ready")
        down_done = sem("down_done")
        pads = sem("pads")
        dve_chain, pool_chain = sem("dve_chain"), sem("pool_chain")

        loads = [(ident[:], dram["ident"]), (band[:], dram["band"]),
                 (rotary[:], dram["L1_rotary"]), (scale[:, 0], dram["L1_q_scale"].partition_broadcast(P)),
                 (scale[:, 1], dram["L1_k_scale"].partition_broadcast(P)),
                 (b2[:], dram["L1_b2"].partition_broadcast(P))]
        for l in range(L):
            loads += [(w_qkv[:, l, :], dram["L1_wqkv"][l]), (w_o[:, l], dram["L1_wo"][l]),
                      (ln_g[:, l:l + 1], dram["L1_ln_g"][l]), (ln_b[:, l:l + 1], dram["L1_ln_b"][l]),
                      (w1[:, l, :], dram["L1_w1"][l])]
            for k, n in enumerate(HK):
                loads += [(w2[0:n, l, k, :], dram["L1_w2"][l, k * P:k * P + n, :])]
                for half in range(2):
                    loads += [(b1[0:n, l, half, k:k + 1],
                               dram["L1_b1"][l, half * HID + k * P:half * HID + k * P + n, :])]

        def heads(ap):
            return ap.rearrange("p (h w) -> p h w", h=H)

        block = ctx.enter_context(nc.Block())

        @block.sync
        def _(sp):
            for dst, src in loads:
                sp.dma_start(dst, src).then_inc(weights, 16)
            with sp.Fori(0, batches) as b:
                rows.load(sp, b)
                gate.load(sp, b)

        @block.gpsimd
        def _(pool):
            gate.before_loop(pool)
            chain = Chain(pool, pool_chain)
            pool.wait_ge(pads, 1)
            with pool.Fori(0, batches) as b:
                chain.restart()
                rows.root(pool, b)
                for l in range(L):
                    for n in range(N_ROT):
                        pool.wait_ge(sums_ready, b * L * N_ROT + (l * N_ROT + n + 1))
                        pool.tensor_tensor(norms[:, n % 2, :], sums[:, n % 2, :], neg_half[:], ALU.pow)
                        chain(pool.tensor_tensor(cos_part[:, n % 2, :], cos_part[:, n % 2, :],
                                                 sin_part[:, n % 2, :], ALU.add))
                        if n >= 2:
                            pool.wait_ge(rows_turned, b * L * N_ROT + (l * N_ROT + n - 1))
                        pool.tensor_tensor(heads(turned_rows[:, n % 2, :]), heads(cos_part[:, n % 2, :]),
                                           norms[:, n % 2, :].unsqueeze(2).to_broadcast([P, H, W]),
                                           ALU.mult).then_inc(rotated, 1)
                    pool.wait_ge(lvar_ready, b * L + (l + 1))
                    pool.tensor_tensor(rstd[:], var_eps[:], neg_half[:, 0:NC], ALU.pow).then_inc(lrstd_ready, 1)
                gate.store(pool, b)

        @block.scalar
        def _(act):
            act.wait_ge(weights, 16 * len(loads))
            act.wait_ge(pads, 1)

            def shift(src):
                act.activation(hT[0:W, :], src[0:W, :], ACT.Copy)
                return act.activation(hT[W:D, 1:T], src[W:D, 0:T - 1], ACT.Copy)

            with act.Fori(0, batches) as b:
                for l in range(L):
                    act.wait_ge(x_turned, b * 2 * L + (2 * l + 1))
                    shift(a_ps).then_inc(hT_ready, 1)

                    def first(j):
                        c, kind = divmod(j, 3)
                        bank = qkv_banks[j % 4]
                        act.wait_ge(qkv_done, b * L * 3 * NC + (l * 3 * NC + j + 1))
                        if kind < 2:
                            n = 2 * c + kind
                            if n >= 2:
                                act.wait_ge(sums_ready, b * L * N_ROT + (l * N_ROT + n - 1))
                            act.activation(squares[:, n % 2, :], bank[:], ACT.Square).then_inc(squares_ready, 1)
                        else:
                            act.activation(v[:, c, :], bank[:], ACT.Copy).then_inc(v_kept, 1)

                    def keep(j):
                        c, kind = divmod(j, 3)
                        if kind < 2:
                            n = 2 * c + kind
                            act.wait_ge(rows_turned, b * L * N_ROT + (l * N_ROT + n + 1))
                            act.activation((qT, kT)[kind][:, :, c * P:(c + 1) * P],
                                           t_ps[n % 2][:].rearrange("p (h t) -> p h t", h=HP),
                                           ACT.Copy).then_inc(rowsT_kept, 1)

                    for i in range(3 * NC + 4):
                        if i < 3 * NC:
                            first(i)
                        if i >= 4:
                            keep(i - 4)

                    for i in range(N_PAIR):
                        c = i // HP
                        lo = 0 if c else W
                        act.wait_ge(max_ready, b * L * N_PAIR + (l * N_PAIR + i + 1))
                        if i >= 2:
                            act.wait_ge(probs_turned, b * L * N_PAIR + (l * N_PAIR + i - 1))
                        for hh in range(2):
                            h = (i % HP) * 2 + hh
                            last = act.activation(probs[:, i % 2, hh, W + lo:2 * P],
                                                  pair_banks[i % 2][hh][:, lo:KEYS], ACT.Exp,
                                                  bias=neg_max[:, i % 2, hh:hh + 1],
                                                  accum_out=row_sum[:, c * H + h:c * H + h + 1])
                        last.then_inc(probs_ready, 1)
                    for c in range(NC):
                        act.wait_ge(o_turned, b * L * NC + (l * NC + c + 1))
                        if c >= 2:
                            act.wait_ge(wo_done, b * L * NC + (l * NC + c - 1))
                        act.activation(oT[:, c % 2].rearrange("p k t -> p (k t)"), t_ps[c % 2][:],
                                       ACT.Copy).then_inc(oT_ready, 1)
                    act.wait_ge(x_turned, b * 2 * L + (2 * l + 2))
                    shift(a_ps).then_inc(hT_ready, 1)
                    for k, m in enumerate(HK):
                        act.wait_ge(up_done, b * L * 3 + (l * 3 + k + 1))
                        if k >= 2:
                            act.wait_ge(mixed_ready, b * L * 3 + (l * 3 + k - 1))
                        act.activation(gelu[0:m, k % 2, :], s_ps[k % 2][0:m, :], ACT.Gelu,
                                       bias=b1[0:m, l, 1, k:k + 1]).then_inc(gelu_ready, 1)
                gate.exp(act, b)

        @block.vector
        def _(dve):
            chain = Chain(dve, dve_chain)
            rows.before_loop(dve)
            dve.memset(neg_half[:], -0.5)
            dve.memset(hT[W:D, 0:1], 0.0)
            chain(dve.memset(probs[:], 0.0))
            dve.sem_inc(pads, 1)
            dve.wait_ge(weights, 16 * len(loads))
            for l in range(L):
                for kind in range(2):
                    s = scale[:, kind, l, :].unsqueeze(1)
                    HW = W // 2
                    t = turnings[:, l, kind]
                    dve.tensor_tensor(t[:, 0], rotary[:, 2 * kind], s.to_broadcast([P, NC, W]), ALU.mult)
                    for dst, src in ((0, HW), (HW, 0)):
                        last = dve.tensor_tensor(t[:, 1, :, dst:dst + HW], rotary[:, 2 * kind + 1, :, dst:dst + HW],
                                                 s[:, :, src:src + HW].to_broadcast([P, NC, HW]), ALU.mult)
            chain(last)
            dve.tensor_copy(ident16[:], ident[:]).then_inc(tables, 1)
            dve.tensor_copy(band16[:], band[:]).then_inc(tables, 1)

            with dve.Fori(0, batches) as b:
                chain.restart()
                dve.wait_ge(rows.x_loaded, b * 16 + 16)
                for c in range(NC):
                    last = dve.bn_stats(rows.stats[:, c, :], rows.x[:, c, :])
                chain(last)
                for c in range(NC):
                    last = dve.bn_aggr(rows.moments[:, c, :], rows.stats[:, c, :])
                chain(last)
                dve.tensor_scalar(rows.var_eps[:], rows.moments[:, :, 1], EPS, None,
                                  ALU.add).then_inc(rows.var_ready, 1)
                dve.wait_ge(rows.rstd_ready, b + 1)
                for c in range(NC):
                    last = dve.tensor_scalar(x[:, c, :], rows.x[:, c, :], rows.moments[:, c, 0:1],
                                             rows.rstd[:, c:c + 1], ALU.subtract, ALU.mult)
                chain(last)
                dve.sem_inc(x_ready, 1)
                dve.sem_inc(rows.x_free, 1)

                for l in range(L):
                    for n in range(N_ROT):
                        c, kind = divmod(n, 2)
                        j = 3 * c + kind
                        bank = heads(qkv_banks[j % 4][:])
                        t = turnings[:, l, kind]
                        HW = W // 2
                        dve.wait_ge(squares_ready, b * L * N_ROT + (l * N_ROT + n + 1))
                        if n >= 2:
                            dve.wait_ge(rotated, b * L * N_ROT + (l * N_ROT + n - 1))
                        dve.tensor_tensor(heads(cos_part[:, n % 2, :]), bank,
                                          t[:, 0, c, :].unsqueeze(1).to_broadcast([P, H, W]), ALU.mult)
                        for dst, src in ((0, HW), (HW, 0)):
                            dve.tensor_tensor(heads(sin_part[:, n % 2, :])[:, :, dst:dst + HW],
                                              bank[:, :, src:src + HW],
                                              t[:, 1, c, dst:dst + HW].unsqueeze(1).to_broadcast([P, H, HW]),
                                              ALU.mult)
                        chain(dve.tensor_reduce(sums[:, n % 2, :], heads(squares[:, n % 2, :]), AX.X, ALU.add))
                        dve.tensor_scalar(sums[:, n % 2, :], sums[:, n % 2, :], 1e-24, None,
                                          ALU.max).then_inc(sums_ready, 1)

                    def pair_max(i):
                        lo = 0 if i // HP else W
                        dve.wait_ge(scores_ready, b * L * N_PAIR + (l * N_PAIR + i + 1))
                        if i >= 2:
                            dve.wait_ge(probs_ready, b * L * N_PAIR + (l * N_PAIR + i - 1))
                        for hh in range(2):
                            last = dve.tensor_reduce(neg_max[:, i % 2, hh:hh + 1], pair_banks[i % 2][hh][:, lo:KEYS],
                                                     AX.X, ALU.max, negate=True)
                        last.then_inc(max_ready, 1)

                    def keep_probsT(i):
                        n = 4 * P if i // HP else 2 * P
                        dve.wait_ge(probs_turned, b * L * N_PAIR + (l * N_PAIR + i + 1))
                        if i >= 2:
                            dve.wait_ge(out_ready, b * L * N_PAIR + (l * N_PAIR + i - 1))
                        dve.tensor_copy(probsT[:, i % 2, 0:n], t_ps[i % 2][:, 0:n]).then_inc(probsT_ready, 1)

                    def take(c):
                        dve.wait_ge(out_ready, b * L * N_PAIR + (l * N_PAIR + (c + 1) * HP))
                        chain(dve.reciprocal(inv_sum[:, c * H:(c + 1) * H], row_sum[:, c * H:(c + 1) * H]))
                        dve.tensor_tensor(heads(o[:, c, :]), heads(o_ps[c % 2][:]),
                                          inv_sum[:, c * H:(c + 1) * H].unsqueeze(2).to_broadcast([P, H, W]),
                                          ALU.mult).then_inc(o_taken, 1)

                    for i in range(N_PAIR + 2):
                        if i < N_PAIR:
                            pair_max(i)
                        if 1 <= i <= N_PAIR:
                            keep_probsT(i - 1)
                        if i >= 5 and (i - 1) % HP == 0:
                            take((i - 1) // HP - 1)
                    dve.wait_ge(wo_done, b * L * NC + (l + 1) * NC)
                    chain(dve.tensor_tensor(x[:], x[:], b_ps[:].rearrange("p (c d) -> p c d", c=NC), ALU.add))
                    dve.sem_inc(x_ready, 1)

                    dve.wait_ge(h_back, b * L + (l + 1))
                    for c in range(NC):
                        last = dve.bn_stats(stats[:, c, :], b_ps[:, c * D:(c + 1) * D])
                    chain(last)
                    for c in range(NC):
                        last = dve.bn_aggr(moments[:, c, :], stats[:, c, :])
                    chain(last)
                    dve.tensor_scalar(var_eps[:], moments[:, :, 1], EPS, None, ALU.add).then_inc(lvar_ready, 1)
                    dve.wait_ge(lrstd_ready, b * L + (l + 1))
                    for c in range(NC):
                        last = dve.tensor_scalar(hn[:, c, :], b_ps[:, c * D:(c + 1) * D], moments[:, c, 0:1],
                                                 rstd[:, c:c + 1], ALU.subtract, ALU.mult)
                    last.then_inc(hn_ready, 1)
                    dve.wait_ge(hn_turned, b * L + (l + 1))
                    dve.tensor_scalar(hnT[:], a_ps[:], ln_g[:, l:l + 1], ln_b[:, l:l + 1], ALU.mult,
                                      ALU.add).then_inc(hnT_ready, 1)
                    chain(dve.tensor_tensor(x[:], x[:], b2[:, l:l + 1, :].to_broadcast([P, NC, D]), ALU.add))
                    for k, m in enumerate(HK):
                        dve.wait_ge(gelu_ready, b * L * 3 + (l * 3 + k + 1))
                        dve.scalar_tensor_tensor(mixed[0:m, k, :], t_ps[k % 2][0:m, :], b1[0:m, l, 0, k:k + 1],
                                                 gelu[0:m, k % 2, :], ALU.add, ALU.mult).then_inc(mixed_ready, 1)
                    dve.wait_ge(down_done, b * L + (l + 1))
                    chain(dve.tensor_tensor(x[:], x[:], b_ps[:].rearrange("p (c d) -> p c d", c=NC), ALU.add))
                    if l < L - 1:
                        dve.sem_inc(x_ready, 1)
                gate.finish(dve, chain, b)

        @block.tensor
        def _(pe):
            pe.wait_ge(weights, 16 * len(loads))
            pe.wait_ge(tables, 2)

            def turn(src):
                for c in range(NC):
                    last = pe.transpose(a_ps[:, c * P:(c + 1) * P], src[:, c, :], ident[:])
                return last

            with pe.Fori(0, batches) as b:
                for l in range(L):
                    pe.wait_ge(x_ready, b * 2 * L + (2 * l + 1))
                    turn(x).then_inc(x_turned, 1)
                    pe.wait_ge(hT_ready, b * 2 * L + (2 * l + 1))

                    def project(j):
                        c, kind = divmod(j, 3)
                        if j >= 4:
                            cc, kk = divmod(j - 4, 3)
                            if kk < 2:
                                pe.wait_ge(sums_ready, b * L * N_ROT + (l * N_ROT + 2 * cc + kk + 1))
                            else:
                                pe.wait_ge(v_kept, b * L * NC + (l * NC + cc + 1))
                        pe.matmul(qkv_banks[j % 4][:], hT[:, c * P:(c + 1) * P],
                                  w_qkv[:, l, kind * H * W:(kind + 1) * H * W], start=True,
                                  stop=True).then_inc(qkv_done, 1)

                    def turn_rows(j):
                        c, kind = divmod(j, 3)
                        if kind < 2:
                            n = 2 * c + kind
                            pe.wait_ge(rotated, b * L * N_ROT + (l * N_ROT + n + 1))
                            if n >= 2:
                                pe.wait_ge(rowsT_kept, b * L * N_ROT + (l * N_ROT + n - 1))
                            for k in range(HP):
                                last = pe.transpose(t_ps[n % 2][:, k * P:(k + 1) * P],
                                                    turned_rows[:, n % 2, k * P:(k + 1) * P], ident[:])
                            last.then_inc(rows_turned, 1)

                    for i in range(3 * NC + 4):
                        if i < 3 * NC:
                            project(i)
                        if i >= 4:
                            turn_rows(i - 4)
                    pe.wait_ge(rowsT_kept, b * L * N_ROT + (l + 1) * N_ROT)
                    pe.wait_ge(v_kept, b * L * NC + (l + 1) * NC)

                    def scores(i):
                        c, hp = divmod(i, HP)
                        lo = 0 if c else W
                        if i >= 2:
                            pe.wait_ge(probs_ready, b * L * N_PAIR + (l * N_PAIR + i - 1))
                        for hh in range(2):
                            pe.matmul(pair_banks[i % 2][hh][:, lo:KEYS], ident16[:], band16[:, lo:KEYS],
                                      start=True, stop=False)
                        for hh in range(2):
                            last = pe.matmul(pair_banks[i % 2][hh][:, lo:KEYS], qT[hh * W:(hh + 1) * W, hp, c * P:(c + 1) * P],
                                             kT[hh * W:(hh + 1) * W, hp, c * P - W + lo:(c + 1) * P],
                                             start=False, stop=True)
                        last.then_inc(scores_ready, 1)

                    def turn_probs(i):
                        c = i // HP
                        pe.wait_ge(probs_ready, b * L * N_PAIR + (l * N_PAIR + i + 1))
                        if i >= 2:
                            pe.wait_ge(probsT_ready, b * L * N_PAIR + (l * N_PAIR + i - 1))
                        n = 0
                        for hh in range(2):
                            for part in ((0, 1) if c else (1,)):
                                last = pe.transpose(t_ps[i % 2][:, n * P:(n + 1) * P],
                                                    probs[:, i % 2, hh, part * P:(part + 1) * P], ident[:])
                                n += 1
                        last.then_inc(probs_turned, 1)

                    def products(i):
                        c, hp = divmod(i, HP)
                        pe.wait_ge(probsT_ready, b * L * N_PAIR + (l * N_PAIR + i + 1))
                        if hp == 0 and c >= 2:
                            pe.wait_ge(o_taken, b * L * NC + (l * NC + c - 1))
                        n = 0
                        for hh in range(2):
                            h = 2 * hp + hh
                            parts = (c - 1, c) if c else (c,)
                            for cc in parts:
                                last = pe.matmul(o_ps[c % 2][:, h * W:(h + 1) * W],
                                                 probsT[:, i % 2, n * P:(n + 1) * P], v[:, cc, h * W:(h + 1) * W],
                                                 start=(cc == parts[0]), stop=(cc == c))
                                n += 1
                        last.then_inc(out_ready, 1)

                    for i in range(N_PAIR + 2):
                        if i < N_PAIR:
                            scores(i)
                        if 1 <= i <= N_PAIR:
                            turn_probs(i - 1)
                        if i >= 2:
                            products(i - 2)

                    def turn_o(c):
                        pe.wait_ge(o_taken, b * L * NC + (l * NC + c + 1))
                        if c >= 2:
                            pe.wait_ge(oT_ready, b * L * NC + (l * NC + c - 1))
                        for k in range(4):
                            last = pe.transpose(t_ps[c % 2][:, k * P:(k + 1) * P], o[:, c, k * P:(k + 1) * P],
                                                ident[:])
                        last.then_inc(o_turned, 1)

                    def project_o(c):
                        pe.wait_ge(oT_ready, b * L * NC + (l * NC + c + 1))
                        for k in range(4):
                            last = pe.matmul(b_ps[:, c * D:(c + 1) * D], oT[:, c % 2, k, :], w_o[:, l, k, :],
                                             start=(k == 0), stop=(k == 3))
                        last.then_inc(wo_done, 1)

                    turn_o(0)
                    for c in range(1, NC):
                        turn_o(c)
                        project_o(c - 1)
                    project_o(NC - 1)

                    pe.wait_ge(x_ready, b * 2 * L + (2 * l + 2))
                    turn(x).then_inc(x_turned, 1)
                    pe.wait_ge(hT_ready, b * 2 * L + (2 * l + 2))
                    for c in range(NC):
                        last = pe.transpose(b_ps[:, c * D:(c + 1) * D], hT[:, c * P:(c + 1) * P], ident[:])
                    last.then_inc(h_back, 1)
                    pe.wait_ge(hn_ready, b * L + (l + 1))
                    turn(hn).then_inc(hn_turned, 1)
                    pe.wait_ge(hnT_ready, b * L + (l + 1))
                    for k, m in enumerate(HK):
                        if k >= 2:
                            pe.wait_ge(mixed_ready, b * L * 3 + (l * 3 + k - 1))
                        pe.matmul(t_ps[k % 2][0:m, :], w1[:, l, k * P:k * P + m], hnT[:], start=True, stop=True)
                        pe.matmul(s_ps[k % 2][0:m, :], w1[:, l, HID + k * P:HID + k * P + m], hnT[:], start=True,
                                  stop=True).then_inc(up_done, 1)
                    pe.wait_ge(mixed_ready, b * L * 3 + (l + 1) * 3)
                    for c in range(NC):
                        for k, m in enumerate(HK):
                            last = pe.matmul(b_ps[:, c * D:(c + 1) * D], mixed[0:m, k, c * P:(c + 1) * P],
                                             w2[0:m, l, k, :], start=(k == 0), stop=(k == 2))
                    last.then_inc(down_done, 1)


def constants():
    out = {}
    out["ident"] = np.eye(P, dtype=np.float32)
    i, j = np.arange(P)[:, None], np.arange(P)[None, :]
    out["causal"] = np.where(j > i, NEG_BIG, 0.0).astype(np.float32)
    tok = np.arange(T).reshape(NC, P).T
    out["keep_triu"] = (np.arange(T)[None, None, :] >= tok[:, :, None]).astype(np.float32)
    out["rank"] = np.broadcast_to(8.0 - np.arange(8), (P, NC, 8)).astype(np.float32).copy()
    f = np.arange(D)
    out["L0_head_scale"] = ((f[:, None] // 8 == np.arange(16)[None, :]) / math.sqrt(8)).astype(np.float32)
    inv = 1.0 / 10000.0 ** (np.arange(0, 8, 2) / 8)
    ang = (np.arange(T)[None, :].astype(np.float32) * inv.astype(np.float32)[f % 4][:, None]).astype(np.float64)
    root = 8.0 ** -0.25
    out["L2_cos"] = (np.cos(ang) * root).astype(np.float32)
    out["L2_sin"] = (np.sin(ang) * np.where(f % 8 < 4, -1.0, 1.0)[:, None] * root).astype(np.float32)
    k = np.arange(192)[None, :] - 64
    out["band"] = np.where((k > i) | (k < i - 64), NEG_BIG, 0.0).astype(np.float32)
    half = np.arange(0, 64, 2).astype(np.float32)
    inv = (1.0 / 10000.0 ** (half / 64)).astype(np.float32)
    t = np.arange(T).astype(np.float32)
    fr = np.concatenate([t[:, None] * inv[None, :]] * 2, axis=1).astype(np.float32).astype(np.float64)
    base = ((half + 0.4 * 64) / (1.4 * 64)).astype(np.float64)
    power = (t - T // 2) / 32.0
    sc = np.concatenate([base[None, :] ** power[:, None]] * 2, axis=1)
    sign = np.where(np.arange(64) < 32, -1.0, 1.0)[None, :]
    tabs = [np.cos(fr) * sc * 8.0, np.sin(fr) * sc * sign * 8.0, np.cos(fr) / sc, np.sin(fr) / sc * sign]
    out["L1_rotary"] = np.stack(tabs).reshape(4, NC, P, 64).transpose(2, 0, 1, 3).astype(np.float32).copy()
    return out


def layouts(a):
    out = {}
    out["L0_w_in"] = np.stack([a["L0_attn_Wq"].T, a["L0_attn_Wk"].T, a["L0_attn_Wv"].T], axis=1)
    out["L0_WoT"] = a["L0_attn_Wo"].T
    out["L0_w_gate"] = a["L0_ffn_expert_embeddings"].T
    out["L0_w1"] = a["L0_ffn_first_linear"].reshape(16, 128, 128).transpose(2, 0, 1)
    out["L0_w2"] = a["L0_ffn_second_linear"].transpose(0, 2, 1).reshape(16, 128, 128).transpose(1, 0, 2)
    out["L1_Mq"], out["L1_Mk"], out["L1_Mv"] = a["L1_attn_Mq"], a["L1_attn_Mk"], a["L1_attn_Mv"]
    out["L1_wqkv"] = a["L1_ffn_wqkv"]
    out["L1_q_scale"], out["L1_k_scale"] = a["L1_ffn_q_scale"], a["L1_ffn_k_scale"]
    out["L1_wo"] = a["L1_ffn_wo"].reshape(2, 4, 128, 128).transpose(0, 2, 1, 3)
    out["L1_ln_g"], out["L1_ln_b"] = a["L1_ffn_ln_g"].reshape(2, 128, 1), a["L1_ffn_ln_b"].reshape(2, 128, 1)
    out["L1_w1"] = a["L1_ffn_w1"]
    out["L1_b1"] = a["L1_ffn_b1"].reshape(2, 682, 1)
    out["L1_w2"] = a["L1_ffn_w2"]
    out["L1_b2"] = a["L1_ffn_b2"]
    swap = (np.arange(128) // 8) * 8 + (np.arange(128) + 4) % 8
    w, bias = a["L2_attn_Wqkv"], a["L2_attn_bqkv"]
    out["L2_w_in"] = np.stack([w[0:128].T, w[128:256].T, w[256:384].T, w[0:128][swap].T, w[128:256][swap].T], axis=1)
    out["L2_b_in"] = np.stack([bias[0:128], bias[0:128][swap], bias[128:256], bias[128:256][swap]], axis=1)
    out["L2_b_v"] = bias[256:384]
    out["L2_pre"] = np.repeat(a["L2_attn_Wpre"].T, 8, axis=0)
    out["L2_post"] = np.repeat(a["L2_attn_Wpost"].T, 8, axis=1)
    out["L2_WoutT"] = a["L2_attn_Wout"].T
    out["L2_attn_bout"] = a["L2_attn_bout"]
    out["L2f_w_gate"] = a["L2_ffn_Wg"].T
    out["L2_ffn_bg"] = a["L2_ffn_bg"]
    out["L2f_w1"] = a["L2_ffn_W1"].reshape(4, 128, 128).transpose(2, 0, 1)
    out["L2f_w2"] = a["L2_ffn_W2"].transpose(0, 2, 1).reshape(4, 128, 128).transpose(1, 0, 2)
    out["L3_w_in"] = a["L3_attn_W"].reshape(128, 3, 128)
    out["L3f_w_gate"] = a["L3_ffn_wg_red"].T
    out["L3_ffn_wg"] = a["L3_ffn_wg"]
    out["L3f_w1"] = a["L3_ffn_w1"].transpose(1, 0, 2).reshape(128, 32, 128)
    out["L3f_w2"] = a["L3_ffn_w2"].reshape(32, 128, 128).transpose(1, 0, 2)
    out["L3f_b1"] = a["L3_ffn_b1"].reshape(32, 128).T
    out["L3_ffn_b2"] = a["L3_ffn_b2"]
    return out


def program(nc, dram, x_in, x_out, layers, batches):
    scratch = [nc.dram_tensor(f"x_after_{n}", (batches, T, D), F32, kind="Internal").ap() for n in layers[:-1]]
    xs = [x_in] + scratch + [x_out]
    s = nc.dram_tensor("attention_out", (batches, T, D), F32, kind="Internal").ap()
    for n, layer in enumerate(layers):
        src, dst = xs[n], xs[n + 1]
        if layer == 0:
            attention_phase(nc, dram, "a0", "causal", src, s, batches)
            experts_phase(nc, dram, "f0", "capacity", src, s, dst, batches)
        elif layer == 1:
            grouped_attention_phase(nc, dram, "a1", src, s, batches)
            local_transformer_phase(nc, dram, "f1", src, s, dst, batches)
        elif layer == 2:
            attention_phase(nc, dram, "a2", "mixed", src, s, batches)
            experts_phase(nc, dram, "f2", "lora", src, s, dst, batches)
        else:
            attention_phase(nc, dram, "a3", "triu", src, s, batches)
            experts_phase(nc, dram, "f3", "top1", src, s, dst, batches)


def build(nc, inputs, layers, batches):
    arrays, dram = {}, {}
    host = {**constants(), **layouts(inputs), "x": inputs["L0_attn_x"]}
    for name, a in host.items():
        arrays[f"in_{name}"] = np.ascontiguousarray(a)
        dram[name] = nc.dram_tensor(f"in_{name}", a.shape, mybir.dt.from_np(a.dtype), kind="ExternalInput").ap()
    out = nc.dram_tensor("out", (batches, T, D), F32, kind="ExternalOutput").ap()
    program(nc, dram, dram["x"], out, layers, batches)
    return arrays


def kernel(**inputs):
    import concourse.bacc as bacc
    from concourse.bass_utils import run_bass_kernel_spmd

    nc = bacc.Bacc("TRN2", target_bir_lowering=False, num_devices=1)
    a = {name: np.asarray(value) for name, value in inputs.items()}
    arrays = build(nc, a, [0, 1, 2, 3], NB)
    r = run_bass_kernel_spmd(nc, [arrays], core_ids=[0])
    return r.results[0]["out"]
```

```python
import math
from contextlib import ExitStack

import numpy as np

import concourse.bass as bass
from concourse import mybir

F32 = mybir.dt.float32
BF16 = mybir.dt.bfloat16
ALU = mybir.AluOpType
ACT = mybir.ActivationFunctionType
AX = mybir.AxisListType

P = 128
D = 128
T = 512
NC = T // P
NB = 16
EPS = 1e-5
NEG_BIG = -1.0e30
NEG_BAND = -1.0e20
MASK_NEG = -9000000000000000.0


class Chain:

    def __init__(self, eng, sem):
        self.eng, self.sem, self.n = eng, sem, 0

    def restart(self):
        self.eng.sem_clear(self.sem)
        self.n = 0

    def __call__(self, ins):
        self.n += 1
        ins.then_inc(self.sem, 1)
        self.eng.wait_ge(self.sem, self.n)


class Rows:

    def __init__(self, nc, ctx, tag, x_dram):
        def sb(name, shape, dt=F32):
            return ctx.enter_context(nc.sbuf_tensor(f"{tag}_{name}", shape, dt))

        def sem(name):
            return nc.alloc_semaphore(f"{tag}_{name}")

        self.nc = nc
        self.x_dram = x_dram.rearrange("b (c p) d -> b p c d", p=P)
        self.x = sb("x", [P, NC, D])
        self.stats = sb("stats", [P, NC, 6])
        self.moments = sb("moments", [P, NC, 2])
        self.var_eps = sb("var_eps", [P, NC])
        self.rstd = sb("rstd", [P, NC])
        self.half = sb("half", [P, NC])
        self.xn = sb("xn", [P, NC, D])
        self.xT = sb("xT", [D, T])
        self.x_loaded = sem("x_loaded")
        self.x_free = sem("x_free")
        self.half_ready = sem("half_ready")
        self.var_ready = sem("var_ready")
        self.rstd_ready = sem("rstd_ready")
        self.xn_ready = sem("xn_ready")
        self.xn_turned = sem("xn_turned")
        self.xT_ready = sem("xT_ready")

    def load(self, sp, b, at):
        sp.wait_ge(self.x_free, b + 1)
        sp.dma_start(self.x[:], self.x_dram[at]).then_inc(self.x_loaded, 16)

    def before_loop(self, dve):
        dve.memset(self.half[:], -0.5).then_inc(self.half_ready, 1)
        dve.memset(self.stats[:], 0.0).then_inc(self.x_free, 1)

    def root(self, pool, b):
        pool.wait_ge(self.half_ready, 1)
        pool.wait_ge(self.var_ready, b + 1)
        pool.tensor_tensor(self.rstd[:], self.var_eps[:], self.half[:], ALU.pow).then_inc(self.rstd_ready, 1)

    def moments_of(self, dve, chain, b):
        dve.wait_ge(self.x_loaded, b * 16 + 16)
        for c in range(NC):
            last = dve.bn_stats(self.stats[:, c, :], self.x[:, c, :])
        chain(last)
        for c in range(NC):
            last = dve.bn_aggr(self.moments[:, c, :], self.stats[:, c, :])
        chain(last)
        dve.tensor_scalar(self.var_eps[:], self.moments[:, :, 1], EPS, None, ALU.add).then_inc(self.var_ready, 1)

    def normalise(self, dve, b):
        dve.wait_ge(self.rstd_ready, b + 1)
        for c in range(NC):
            last = dve.tensor_scalar(self.xn[:, c, :], self.x[:, c, :], self.moments[:, c, 0:1],
                                     self.rstd[:, c:c + 1], ALU.subtract, ALU.mult)
            last.then_inc(self.xn_ready, 1)
        dve.wait_ge(self.xn_ready, b * NC + NC)
        dve.sem_inc(self.x_free, 1)

    def turn(self, pe, bank, ident, b):
        pe.wait_ge(self.xn_ready, b * NC + NC)
        for c in range(NC):
            last = pe.transpose(bank[:, c * P:(c + 1) * P], self.xn[:, c, :], ident[:])
        last.then_inc(self.xn_turned, 1)

    def keep_turned(self, act, bank, b):
        act.wait_ge(self.xn_turned, b + 1)
        act.activation(self.xT[:], bank[:], ACT.Copy).then_inc(self.xT_ready, 1)


def attention_phase(nc, dram, tag, kind, x_dram, s_dram, batches):
    H = 1 if kind == "triu" else 16
    DH = D // H
    U = NC * H
    causal, mixed, triu = kind == "causal", kind == "mixed", kind == "triu"

    with nc.cleanup_on_exit(), ExitStack() as ctx:
        def sb(name, shape, dt=F32):
            return ctx.enter_context(nc.sbuf_tensor(f"{tag}_{name}", shape, dt))

        def sem(name):
            return nc.alloc_semaphore(f"{tag}_{name}")

        def ps(name):
            return ctx.enter_context(nc.psum_tensor(f"{tag}_{name}_ps", [P, 512], F32))

        rows = Rows(nc, ctx, tag, x_dram)
        ident = sb("ident", [P, P])
        n_w = {"causal": 3, "mixed": 5, "triu": 3}[kind]
        w_in = sb("w_in", [D, n_w, D])
        qT, kT = sb("qT", [D, T]), sb("kT", [D, T])
        v = sb("v", [P, NC, D])
        probs = sb("probs", [P, 2, T])
        probsT = sb("probsT", [P, 2, T])
        neg_max = sb("neg_max", [P, 2])
        row_sum = sb("row_sum", [P, U])
        inv_sum = sb("inv_sum", [P, U])
        o = sb("o", [P, NC, D])
        s_out = sb("s_out", [P, NC, D])
        if not triu:
            w_out = sb("w_out", [D, D])
            oT = sb("oT", [D, T])
            head_scale = sb("head_scale", [D, H])
            q_head = sb("q_head", [D, 4, P])
        if causal:
            ident16 = sb("ident16", [P, P], BF16)
            mask16, mask = sb("mask16", [P, P], BF16), sb("mask", [P, P])
        if mixed:
            b_in = sb("b_in", [D, 4])
            b_v = sb("b_v", [P, D])
            b_out = sb("b_out", [P, D])
            cos, sin = sb("cos", [D, T]), sb("sin", [D, T])
            cos_part, sin_part = sb("cos_part", [D, T]), sb("sin_part", [D, T])
            post = sb("post", [P, H, D])
            v_post = sb("v_post", [P, H, NC, D])
        if triu:
            keep = sb("keep", [P, NC, T])
            masked = sb("masked", [P, 2, T])
            is_zero = sb("is_zero", [P, T])
        scores_ps = [ps("scores0"), ps("scores1")]
        turned_ps = [ps("turned0"), ps("turned1")]
        out_ps = [ps("out0"), ps("out1")]
        a_ps, b_ps = ps("a"), ps("b")

        weights = sem("weights")
        mask_ready = sem("mask_ready")
        projected = sem("projected")
        q_ready, k_ready, v_ready = sem("q_ready"), sem("k_ready"), sem("v_ready")
        v_post_ready = sem("v_post_ready")
        q_head_ready = sem("q_head_ready")
        scores_ready = sem("scores_ready")
        max_ready = sem("max_ready")
        probs_ready = sem("probs_ready")
        probs_turned = sem("probs_turned")
        probsT_ready = sem("probsT_ready")
        out_ready = sem("out_ready")
        o_taken = sem("o_taken")
        o_turned = sem("o_turned")
        oT_ready = sem("oT_ready")
        y_ready = sem("y_ready")
        s_ready = sem("s_ready")
        s_stored = sem("s_stored")
        s_free = sem("s_free")
        dve_chain = sem("dve_chain")

        loads = [(ident[:], dram["ident"])]
        if causal:
            loads += [(w_in[:], dram["L0_w_in"].rearrange("i n o -> i n o")), (w_out[:], dram["L0_WoT"]),
                      (head_scale[:], dram["L0_head_scale"]), (mask[:], dram["causal"])]
        if mixed:
            loads += [(w_in[:], dram["L2_w_in"]), (w_out[:], dram["L2_WoutT"]),
                      (head_scale[:], dram["L2_pre"]), (b_in[:], dram["L2_b_in"]),
                      (b_v[:], dram["L2_b_v"].partition_broadcast(P)),
                      (b_out[:], dram["L2_attn_bout"].partition_broadcast(P)),
                      (cos[:], dram["L2_cos"]), (sin[:], dram["L2_sin"]),
                      (post[:], dram["L2_post"].partition_broadcast(P))]
        if triu:
            loads += [(w_in[:], dram["L3_w_in"]), (keep[:], dram["keep_triu"])]
        SCORE_SCALE = 1.0 / math.sqrt(DH)
        MOMENTS, NORMALISE, TURN = (1, 2, 2) if triu else (U - 24, U - 20, U - 16)

        def own_columns(bank, first):
            ap = bank[:, first:first + DH].copy()
            return bass.AP(ap.tensor, ap.offset, [list(ap.ap[0]), [D + DH, 4], [1, DH]])

        s_rows = s_dram.rearrange("b (c p) d -> b p c d", p=P)
        used = (lambda c: (c + 1) * P) if causal else (lambda c: T)

        block = ctx.enter_context(nc.Block())

        @block.sync
        def _(sp):
            for dst, src in loads:
                sp.dma_start(dst, src).then_inc(weights, 16)
            rows.load(sp, 0, 0)
            with sp.Fori(0, batches) as b:
                rows.load(sp, b + 1, (b + 1) % batches)

        @block.gpsimd
        def _(pool):
            pool.sem_inc(s_free, 1)
            pool.wait_ge(weights, 16 * len(loads))
            rows.root(pool, 0)
            with pool.Fori(0, batches) as b:
                if not triu:
                    pool.wait_ge(q_ready, b + 1)
                    if mixed:
                        pool.wait_ge(v_ready, b + 1)
                    for u in range(U):
                        c, h = divmod(u, H)
                        if u == MOMENTS + 2:
                            rows.root(pool, b + 1)
                        if u >= 4:
                            pool.wait_ge(scores_ready, b * U + (u - 3))
                        pool.tensor_tensor(q_head[:, u % 4, :], qT[:, c * P:(c + 1) * P],
                                           head_scale[:, h:h + 1].to_broadcast([D, P]),
                                           ALU.mult).then_inc(q_head_ready, 1)
                        if mixed and c == 0:
                            pool.tensor_tensor(v_post[:, h, :, :], v[:],
                                               post[:, h:h + 1, :].to_broadcast([P, NC, D]),
                                               ALU.mult).then_inc(v_post_ready, 1)
                if triu:
                    rows.root(pool, b + 1)
                pool.wait_ge(s_ready, b + 1)
                pool.dma_start(s_rows[b], s_out[:]).then_inc(s_stored, 16)
                pool.wait_ge(s_stored, b * 16 + 16)
                pool.sem_inc(s_free, 1)

        @block.scalar
        def _(act):
            def keep_projections(b):
                act.wait_ge(projected, b * 3 + 1)
                act.activation(qT[:], b_ps[:], ACT.Copy,
                               scale=(SCORE_SCALE if triu else 1.0)).then_inc(q_ready, 1)
                act.wait_ge(projected, b * 3 + 2)
                act.activation(kT[:], a_ps[:], ACT.Copy).then_inc(k_ready, 1)
                act.wait_ge(projected, b * 3 + 3)
                act.activation(v[:].rearrange("p c d -> p (c d)"), out_ps[0][:], ACT.Copy).then_inc(v_ready, 1)

            rows.keep_turned(act, a_ps, 0)
            if not mixed:
                keep_projections(0)
            with act.Fori(0, batches) as b:
                def exps(u):
                    c, h = divmod(u, H)
                    act.wait_ge(max_ready, b * U + (u + 1))
                    if u >= 2:
                        act.wait_ge(probs_turned, b * U + (u - 1))
                    src = masked[:, u % 2, :] if triu else scores_ps[u % 2][:, 0:used(c)]
                    act.activation(probs[:, u % 2, 0:used(c)], src, ACT.Exp, bias=neg_max[:, u % 2:u % 2 + 1],
                                   scale=1.0, accum_out=row_sum[:, u:u + 1]).then_inc(probs_ready, 1)

                def keep_probsT(u):
                    act.wait_ge(probs_turned, b * U + (u + 1))
                    if u >= 2:
                        act.wait_ge(out_ready, b * U + (u - 1))
                    act.activation(probsT[:, u % 2, :], turned_ps[u % 2][:], ACT.Copy).then_inc(probsT_ready, 1)

                for i in range(U + 1):
                    if i < U:
                        exps(i)
                    if i >= 1 and not causal:
                        keep_probsT(i - 1)
                    if i == TURN:
                        rows.keep_turned(act, a_ps, b + 1)
                if not mixed:
                    keep_projections(b + 1)
                if not triu:
                    act.wait_ge(o_turned, b + 1)
                    act.activation(oT[:], turned_ps[0][:], ACT.Copy).then_inc(oT_ready, 1)
                if causal:
                    act.wait_ge(y_ready, b + 1)
                    act.wait_ge(s_free, b + 1)
                    act.activation(s_out[:].rearrange("p c d -> p (c d)"), turned_ps[1][:],
                                   ACT.Copy).then_inc(s_ready, 1)

        @block.vector
        def _(dve):
            chain = Chain(dve, dve_chain)
            rows.before_loop(dve)
            dve.wait_ge(weights, 16 * len(loads))
            if causal:
                dve.tensor_copy(ident16[:], ident[:]).then_inc(mask_ready, 1)
                dve.tensor_copy(mask16[:], mask[:]).then_inc(mask_ready, 1)
            def rotate_projections(b):
                for n, (plain, swapped, dst, ready) in enumerate(
                        [(b_ps, scores_ps[0], qT, q_ready), (a_ps, scores_ps[1], kT, k_ready)]):
                    dve.wait_ge(projected, b * 5 + 2 * n + 1)
                    dve.scalar_tensor_tensor(cos_part[:], plain[:], b_in[:, 2 * n:2 * n + 1], cos[:],
                                             ALU.add, ALU.mult)
                    dve.wait_ge(projected, b * 5 + 2 * n + 2)
                    chain(dve.scalar_tensor_tensor(sin_part[:], swapped[:], b_in[:, 2 * n + 1:2 * n + 2],
                                                   sin[:], ALU.add, ALU.mult))
                    dve.tensor_tensor(dst[:], cos_part[:], sin_part[:], ALU.add).then_inc(ready, 1)
                    dve.wait_ge(ready, b + 1)
                dve.wait_ge(projected, b * 5 + 5)
                dve.tensor_tensor(v[:], out_ps[0][:].rearrange("p (c d) -> p c d", c=NC),
                                  b_v[:].unsqueeze(1).to_broadcast([P, NC, D]),
                                  ALU.add).then_inc(v_ready, 1)

            rows.moments_of(dve, chain, 0)
            rows.normalise(dve, 0)
            if mixed:
                rotate_projections(0)
            with dve.Fori(0, batches) as b:
                chain.restart()
                def row_max(u):
                    c, h = divmod(u, H)
                    dve.wait_ge(scores_ready, b * U + (u + 1))
                    if u >= 2:
                        dve.wait_ge(probs_ready, b * U + (u - 1))
                    src = scores_ps[u % 2][:, 0:used(c)]
                    if triu:
                        m = masked[:, u % 2, :]
                        chain(dve.tensor_tensor(m, src, keep[:, c, :], ALU.mult))
                        chain(dve.tensor_scalar(is_zero[:], m, 0.0, MASK_NEG, ALU.is_equal, ALU.mult))
                        chain(dve.tensor_tensor(m, m, is_zero[:], ALU.add))
                        src = m
                    dve.tensor_reduce(neg_max[:, u % 2:u % 2 + 1], src, AX.X, ALU.max,
                                      negate=True).then_inc(max_ready, 1)

                def keep_probsT(u):
                    c = u // H
                    dve.wait_ge(probs_turned, b * U + (u + 1))
                    if u >= 2:
                        dve.wait_ge(out_ready, b * U + (u - 1))
                    dve.tensor_copy(probsT[:, u % 2, 0:used(c)],
                                    turned_ps[u % 2][:, 0:used(c)]).then_inc(probsT_ready, 1)

                def take_heads(n):
                    c, q = divmod(n, H // 4)
                    lo = c * H + 4 * q
                    dve.wait_ge(out_ready, b * U + (n + 1) * 4)
                    chain(dve.reciprocal(inv_sum[:, lo:lo + 4], row_sum[:, lo:lo + 4]))
                    first = 4 * q * DH
                    dve.tensor_tensor(o[:, c, first:first + 4 * DH].rearrange("p (h d) -> p h d", h=4),
                                      own_columns(out_ps[n % 2], first),
                                      inv_sum[:, lo:lo + 4].unsqueeze(2).to_broadcast([P, 4, DH]),
                                      ALU.mult).then_inc(o_taken, 1)

                def take_unit(u):
                    c, h = divmod(u, H)
                    dve.wait_ge(out_ready, b * U + (u + 1))
                    chain(dve.reciprocal(inv_sum[:, u:u + 1], row_sum[:, u:u + 1]))
                    dst = s_out if triu else o
                    if h == 0:
                        if triu and c == 0:
                            dve.wait_ge(s_free, b + 1)
                        dve.tensor_scalar(dst[:, c, :], out_ps[u % 2][:, 0:D], inv_sum[:, u:u + 1], None,
                                          ALU.mult).then_inc(o_taken, 1)
                    else:
                        dve.wait_ge(o_taken, b * U + u)
                        dve.scalar_tensor_tensor(o[:, c, :], out_ps[u % 2][:, 0:D], inv_sum[:, u:u + 1],
                                                 o[:, c, :], ALU.mult, ALU.add).then_inc(o_taken, 1)

                for i in range(U + 2):
                    if i < U:
                        row_max(i)
                    if causal and 1 <= i <= U:
                        keep_probsT(i - 1)
                    if causal and i >= 5 and (i - 1) % 4 == 0:
                        take_heads((i - 1) // 4 - 1)
                    if not causal and i >= 2:
                        take_unit(i - 2)
                    if i == MOMENTS:
                        rows.moments_of(dve, chain, b + 1)
                    if i == NORMALISE:
                        rows.normalise(dve, b + 1)
                if mixed:
                    rotate_projections(b + 1)
                    dve.wait_ge(y_ready, b + 1)
                    dve.wait_ge(s_free, b + 1)
                    dve.tensor_tensor(s_out[:], turned_ps[1][:].rearrange("p (c d) -> p c d", c=NC),
                                      b_out[:].unsqueeze(1).to_broadcast([P, NC, D]),
                                      ALU.add).then_inc(s_ready, 1)
                if triu:
                    dve.wait_ge(o_taken, b * U + U)
                    dve.sem_inc(s_ready, 1)

        @block.tensor
        def _(pe):
            pe.wait_ge(weights, 16 * len(loads))
            if causal:
                pe.wait_ge(mask_ready, 2)
            n_taken = U // 4 if causal else U

            def project(b):
                pe.wait_ge(rows.xT_ready, b + 1)
                banks = [(0, b_ps), (3, scores_ps[0]), (1, a_ps), (4, scores_ps[1])] if mixed else \
                    [(0, b_ps), (1, a_ps)]
                for n, bank in banks:
                    pe.matmul(bank[:], w_in[:, n, :], rows.xT[:], start=True, stop=True).then_inc(projected, 1)
                for c in range(NC):
                    last = pe.matmul(out_ps[0][:, c * D:(c + 1) * D], rows.xT[:, c * P:(c + 1) * P], w_in[:, 2, :],
                                     start=True, stop=True)
                last.then_inc(projected, 1)

            rows.turn(pe, a_ps, ident, 0)
            project(0)
            with pe.Fori(0, batches) as b:
                pe.wait_ge(k_ready, b + 1)
                if triu:
                    pe.wait_ge(q_ready, b + 1)
                    pe.wait_ge(v_ready, b + 1)

                def scores(u):
                    c, h = divmod(u, H)
                    if not triu:
                        pe.wait_ge(q_head_ready, b * U + (u + 1))
                    if u >= 2:
                        pe.wait_ge(probs_ready, b * U + (u - 1))
                    q = qT[:, c * P:(c + 1) * P] if triu else q_head[:, u % 4, :]
                    if causal:
                        pe.matmul(scores_ps[u % 2][:, c * P:(c + 1) * P], ident16[:], mask16[:],
                                  start=True, stop=False, skip_group_check=True)
                    pe.matmul(scores_ps[u % 2][:, 0:used(c)], q, kT[:, 0:used(c)], start=not causal, stop=True,
                              skip_group_check=causal).then_inc(scores_ready, 1)

                def turn_probs(u):
                    c = u // H
                    pe.wait_ge(probs_ready, b * U + (u + 1))
                    if u >= 2:
                        pe.wait_ge(probsT_ready, b * U + (u - 1))
                    for j in range(used(c) // P):
                        last = pe.transpose(turned_ps[u % 2][:, j * P:(j + 1) * P],
                                            probs[:, u % 2, j * P:(j + 1) * P], ident[:])
                    last.then_inc(probs_turned, 1)

                def products(u):
                    c, h = divmod(u, H)
                    pe.wait_ge(probsT_ready, b * U + (u + 1))
                    if causal:
                        if u == 0:
                            pe.wait_ge(v_ready, b + 1)
                        if u % 4 == 0 and u >= 8:
                            pe.wait_ge(o_taken, b * n_taken + (u // 4 - 1))
                        dst = out_ps[u // 4 % 2][:, u % 4 * D:(u % 4 + 1) * D]
                    else:
                        if u == 0 and mixed:
                            pe.wait_ge(v_ready, b + 1)
                        if u >= 2:
                            pe.wait_ge(o_taken, b * U + (u - 1))
                        if mixed and c == 0:
                            pe.wait_ge(v_post_ready, b * H + (h + 1))
                        dst = out_ps[u % 2][:, 0:D]
                    n = used(c) // P
                    for j in range(n):
                        rhs = v_post[:, h, j, :] if mixed else v[:, j, :]
                        last = pe.matmul(dst, probsT[:, u % 2, j * P:(j + 1) * P], rhs,
                                         start=(j == 0), stop=(j == n - 1))
                    last.then_inc(out_ready, 1)

                for i in range(U + 2):
                    if i < U:
                        scores(i)
                    if 1 <= i <= U:
                        turn_probs(i - 1)
                    if i >= 2:
                        products(i - 2)
                    if i == TURN:
                        rows.turn(pe, a_ps, ident, b + 1)
                pe.wait_ge(o_taken, b * n_taken + (n_taken - 1))
                project(b + 1)
                pe.wait_ge(o_taken, b * n_taken + n_taken)
                if not triu:
                    for c in range(NC):
                        last = pe.transpose(turned_ps[0][:, c * P:(c + 1) * P], o[:, c, :], ident[:])
                    last.then_inc(o_turned, 1)
                    pe.wait_ge(oT_ready, b + 1)
                    for c in range(NC):
                        last = pe.matmul(turned_ps[1][:, c * D:(c + 1) * D], oT[:, c * P:(c + 1) * P], w_out[:],
                                         start=True, stop=True)
                    last.then_inc(y_ready, 1)
                    pe.wait_ge(s_ready, b + 1)


class Gate:

    def __init__(self, nc, ctx, tag, x_dram, s_dram, out_dram):
        def sb(name):
            return ctx.enter_context(nc.sbuf_tensor(f"{tag}_{name}", [P, NC, D], F32))

        def sem(name):
            return nc.alloc_semaphore(f"{tag}_{name}")

        self.x_rows, self.s_rows, self.out_rows = (
            a.rearrange("b (c p) d -> b p c d", p=P) for a in (x_dram, s_dram, out_dram))
        self.x, self.s, self.y, self.e, self.out = sb("gx"), sb("gs"), sb("y"), sb("ge"), sb("gout")
        self.loaded = sem("gate_loaded")
        self.free = sem("gate_free")
        self.neg_abs_ready = sem("neg_abs_ready")
        self.exp_ready = sem("exp_ready")
        self.out_full = sem("out_full")
        self.stored = sem("stored")
        self.out_free = sem("out_free")

    def load(self, sp, b):
        sp.wait_ge(self.free, b + 1)
        sp.dma_start(self.x[:], self.x_rows[b]).then_inc(self.loaded, 16)
        sp.dma_start(self.s[:], self.s_rows[b]).then_inc(self.loaded, 16)

    def exp(self, act, b):
        act.wait_ge(self.neg_abs_ready, b + 1)
        act.activation(self.e[:], self.e[:], ACT.Exp).then_inc(self.exp_ready, 1)

    def finish(self, dve, chain, b):
        dve.scalar_tensor_tensor(self.e[:], self.y[:], -1.0, self.y[:], ALU.mult,
                                 ALU.min).then_inc(self.neg_abs_ready, 1)
        dve.wait_ge(self.loaded, b * 32 + 32)
        chain(dve.tensor_tensor(self.s[:], self.s[:], self.y[:], ALU.mult))
        dve.wait_ge(self.exp_ready, b + 1)
        chain(dve.scalar_tensor_tensor(self.y[:], self.y[:], 0.0, self.e[:], ALU.is_ge, ALU.max))
        dve.tensor_scalar(self.e[:], self.e[:], 1.0, None, ALU.add)
        chain(dve.tensor_tensor(self.s[:], self.s[:], self.y[:], ALU.mult))
        chain(dve.reciprocal(self.e[:], self.e[:]))
        chain(dve.tensor_tensor(self.s[:], self.s[:], self.e[:], ALU.mult))
        dve.wait_ge(self.out_free, b + 1)
        dve.tensor_tensor(self.out[:], self.s[:], self.x[:], ALU.add).then_inc(self.out_full, 1)
        dve.wait_ge(self.out_full, b + 1)
        dve.sem_inc(self.free, 1)

    def before_loop(self, pool):
        pool.sem_inc(self.free, 1)
        pool.sem_inc(self.out_free, 1)

    def store(self, pool, b):
        pool.wait_ge(self.out_full, b + 1)
        pool.dma_start(self.out_rows[b], self.out[:]).then_inc(self.stored, 16)
        pool.wait_ge(self.stored, b * 16 + 16)
        pool.sem_inc(self.out_free, 1)


def experts_phase(nc, dram, tag, kind, x_dram, s_dram, out_dram, batches):
    E = 8
    capacity, lora, top1 = kind == "capacity", kind == "lora", kind == "top1"
    I = {"capacity": 256, "lora": 64, "top1": 512}[kind]
    PAIR = max(1, P // I)
    K = max(1, I // P)
    G = E // PAIR
    CAPACITY = NB * T // E
    GR = 16

    with nc.cleanup_on_exit(), ExitStack() as ctx:
        def sb(name, shape, dt=F32):
            return ctx.enter_context(nc.sbuf_tensor(f"{tag}_{name}", shape, dt))

        def sem(name):
            return nc.alloc_semaphore(f"{tag}_{name}")

        def ps(name):
            return ctx.enter_context(nc.psum_tensor(f"{tag}_{name}_ps", [P, 512], F32))

        rows = Rows(nc, ctx, tag, x_dram)
        gate = Gate(nc, ctx, tag, x_dram, s_dram, out_dram)
        ident = sb("ident", [P, P])
        rank = sb("rank", [P, NC, E])
        w_gate = sb("w_gate", [D, GR if top1 else E])
        w1 = sb("w1", [D, G * K, P])
        w2 = sb("w2", [P, E * K, D])
        hidden = sb("hidden", [P, 2, K, T])
        logits = sb("logits", [P, NC, E])
        eq = sb("eq", [P, NC, E])
        first = sb("first", [P, NC, E])
        second = sb("second", [P, NC, E])
        top = sb("top", [P, NC])
        top_rank = sb("top_rank", [P, NC])
        top2 = sb("top2", [P, NC])
        diff = sb("diff", [P, NC, E] if top1 else [P, NC])
        weight = sb("weight", [P, NC])
        weight2 = sb("weight2", [P, NC])
        gates = sb("gates", [P, NC, E])
        gatesT = sb("gatesT", [E, T])
        if capacity:
            picked, zeros, count = sb("picked", [E, T]), sb("zeros", [E, T]), sb("count", [E, T])
            carry = sb("carry", [E, 1])
            capped = sb("capped", [P, NC, E])
        if lora:
            b_gate = sb("b_gate", [P, E])
        if top1:
            b1 = sb("b1", [P, E * K])
            b2 = sb("b2", [E, D])
            wg, wg_sq, wg_norm = sb("wg", [E, GR]), sb("wg_sq", [E, GR]), sb("wg_norm", [E, 1])
            wg_half = sb("wg_half", [E, 1])
            wg_unit = sb("wg_unit", [E, GR])
            wg_unitT = sb("wg_unitT", [GR, E])
            reducedT = sb("reducedT", [GR, T])
        hidden_ps = [ps("hidden0"), ps("hidden1")]
        y_ps = [ps("y0"), ps("y1")]
        a_ps, router_ps, gatesT_ps, extra_ps = ps("a"), ps("router"), ps("gatesT"), ps("extra")

        weights = sem("weights")
        gate_weights = sem("gate_weights")
        reduced_done, reduced_ready = sem("reduced_done"), sem("reduced_ready")
        logits_done = sem("logits_done")
        diff_ready, weight_ready = sem("diff_ready"), sem("weight_ready")
        gates_ready = sem("gates_ready")
        gates_turned, gatesT_ready = sem("gates_turned"), sem("gatesT_ready")
        back_turned = sem("back_turned")
        bias_done = sem("bias_done")
        hidden_done, hidden_ready = sem("hidden_done"), sem("hidden_ready")
        y_done, y_taken = sem("y_done"), sem("y_taken")
        dve_chain = sem("dve_chain")

        pre = {"capacity": "L0", "lora": "L2f", "top1": "L3f"}[kind]
        loads = [(ident[:], dram["ident"]), (rank[:], dram["rank"]), (w_gate[:], dram[f"{pre}_w_gate"]),
                 (w1[:], dram[f"{pre}_w1"]), (w2[:], dram[f"{pre}_w2"])]
        if lora:
            loads += [(b_gate[:], dram["L2_ffn_bg"].partition_broadcast(P))]
        if top1:
            loads += [(b1[:], dram["L3f_b1"]), (b2[:], dram["L3_ffn_b2"]), (wg[:], dram["L3_ffn_wg"])]
        act_fn = ACT.Relu if capacity else ACT.Gelu

        block = ctx.enter_context(nc.Block())

        @block.sync
        def _(sp):
            for dst, src in loads:
                sp.dma_start(dst, src).then_inc(weights, 16)
            rows.load(sp, 0, 0)
            with sp.Fori(0, batches) as b:
                gate.load(sp, b)
                rows.load(sp, b + 1, (b + 1) % batches)

        @block.gpsimd
        def _(pool):
            gate.before_loop(pool)
            if top1:
                pool.wait_ge(gate_weights, 2)
                pool.tensor_tensor(wg_norm[:], wg_norm[:], wg_half[:], ALU.pow).then_inc(gate_weights, 1)
            rows.root(pool, 0)
            with pool.Fori(0, batches) as b:
                rows.root(pool, b + 1)
                gate.store(pool, b)

        @block.scalar
        def _(act):
            act.wait_ge(weights, 16 * len(loads))
            if top1:
                act.wait_ge(gate_weights, 5)
                act.activation(wg_unitT[:], a_ps[0:GR, 0:E], ACT.Copy).then_inc(gate_weights, 1)
            rows.keep_turned(act, a_ps, 0)
            with act.Fori(0, batches) as b:
                if top1:
                    act.wait_ge(reduced_done, b + 1)
                    act.activation(reducedT[:], gatesT_ps[0:GR, :], ACT.Copy).then_inc(reduced_ready, 1)
                act.wait_ge(diff_ready, b + 1)
                act.activation(diff[:], diff[:], ACT.Exp).then_inc(weight_ready, 1)
                for g in range(G):
                    if g >= 2:
                        act.wait_ge(y_done, b * E + (g - 1) * PAIR)
                    for k in range(K):
                        n = g * K + k
                        act.wait_ge(hidden_done, b * G * K + (n + 1))
                        bias = b1[:, n:n + 1] if top1 else 0.0
                        act.activation(hidden[:, g % 2, k, :], hidden_ps[n % 2][:], act_fn,
                                       bias=bias).then_inc(hidden_ready, 1)
                rows.keep_turned(act, a_ps, b + 1)
                gate.exp(act, b)

        @block.vector
        def _(dve):
            chain = Chain(dve, dve_chain)
            rows.before_loop(dve)
            dve.wait_ge(weights, 16 * len(loads))
            if capacity:
                dve.memset(zeros[:], 0.0)
                chain(dve.memset(carry[:], 0.0))
            if top1:
                chain(dve.tensor_tensor(wg_sq[:], wg[:], wg[:], ALU.mult))
                dve.memset(wg_half[:], 0.5).then_inc(gate_weights, 1)
                dve.tensor_reduce(wg_norm[:], wg_sq[:], AX.X, ALU.add).then_inc(gate_weights, 1)
                dve.wait_ge(gate_weights, 3)
                chain(dve.tensor_scalar(wg_norm[:], wg_norm[:], 1e-4, None, ALU.max))
                chain(dve.reciprocal(wg_norm[:], wg_norm[:]))
                dve.tensor_scalar(wg_unit[:], wg[:], wg_norm[:], None, ALU.mult).then_inc(gate_weights, 1)

            def wide(a):
                return a[:].unsqueeze(2).to_broadcast([P, NC, E])

            def one_hot(dst, top_value):
                chain(dve.tensor_reduce(top_value[:], logits[:], AX.X, ALU.max))
                chain(dve.tensor_tensor(eq[:], logits[:], wide(top_value), ALU.is_equal))
                chain(dve.tensor_tensor(eq[:], eq[:], rank[:], ALU.mult))
                chain(dve.tensor_reduce(top_rank[:], eq[:], AX.X, ALU.max))
                chain(dve.tensor_tensor(dst[:], eq[:], wide(top_rank), ALU.is_equal))

            rows.moments_of(dve, chain, 0)
            rows.normalise(dve, 0)
            dve.sem_inc(y_taken, 2)
            with dve.Fori(0, batches) as b:
                chain.restart()
                dve.wait_ge(logits_done, b + 1)
                src = router_ps[:, 0:NC * E].rearrange("p (c e) -> p c e", c=NC)
                if lora:
                    chain(dve.tensor_tensor(logits[:], src, b_gate[:].unsqueeze(1).to_broadcast([P, NC, E]), ALU.add))
                else:
                    chain(dve.tensor_copy(logits[:], src))
                one_hot(first, top)
                if top1:
                    dve.tensor_tensor(diff[:], logits[:], wide(top), ALU.subtract).then_inc(diff_ready, 1)
                    dve.wait_ge(weight_ready, b + 1)
                    chain(dve.tensor_reduce(weight[:], diff[:], AX.X, ALU.add))
                    chain(dve.reciprocal(weight[:], weight[:]))
                    dve.tensor_tensor(gates[:], first[:], wide(weight), ALU.mult).then_inc(gates_ready, 1)
                    dve.wait_ge(gates_ready, b + 1)
                else:
                    chain(dve.scalar_tensor_tensor(logits[:], first[:], -3.0e38, logits[:], ALU.mult, ALU.add))
                    one_hot(second, top2)
                    dve.tensor_tensor(diff[:], top2[:], top[:], ALU.subtract).then_inc(diff_ready, 1)
                    dve.wait_ge(weight_ready, b + 1)
                    chain(dve.tensor_scalar(weight[:], diff[:], 1.0, None, ALU.add))
                    chain(dve.reciprocal(weight[:], weight[:]))
                    if lora:
                        chain(dve.tensor_scalar(weight[:], weight[:], 2.0, None, ALU.mult))
                    chain(dve.tensor_tensor(weight2[:], diff[:], weight[:], ALU.mult))
                    dve.tensor_tensor(first[:], first[:], wide(weight), ALU.mult)
                    chain(dve.tensor_tensor(second[:], second[:], wide(weight2), ALU.mult))
                    dve.tensor_tensor(gates[:], first[:], second[:], ALU.add).then_inc(gates_ready, 1)
                    dve.wait_ge(gates_ready, b + 1)
                if capacity:
                    dve.wait_ge(gates_turned, b + 1)
                    chain(dve.tensor_copy(gatesT[:], gatesT_ps[0:E, :]))
                    chain(dve.tensor_scalar(picked[:], gatesT[:], 0.0, None, ALU.is_gt))
                    chain(dve.tensor_tensor_scan(count[:], picked[:], zeros[:], carry[:], ALU.add, ALU.add))
                    dve.tensor_copy(carry[:], count[:, T - 1:T])
                    chain(dve.scalar_tensor_tensor(gatesT[:], count[:], float(CAPACITY), gatesT[:],
                                                   ALU.is_le, ALU.mult))
                    dve.sem_inc(gatesT_ready, 1)
                    dve.wait_ge(back_turned, b + 1)
                    chain(dve.tensor_copy(capped[:], router_ps[:, 64:64 + NC * E].rearrange("p (c e) -> p c e", c=NC)))
                if top1:
                    dve.wait_ge(gates_turned, b + 1)
                    dve.tensor_copy(gatesT[:], gatesT_ps[0:E, :]).then_inc(gatesT_ready, 1)
                    dve.wait_ge(bias_done, b + 1)
                    chain(dve.tensor_copy(gate.y[:], extra_ps[:].rearrange("p (c d) -> p c d", c=NC)))
                g_src = capped if capacity else gates
                for e in range(E):
                    dve.wait_ge(y_done, b * E + (e + 1))
                    for c in range(NC):
                        src = y_ps[e % 2][:, c * D:(c + 1) * D]
                        if e == 0 and not top1:
                            last = dve.tensor_scalar(gate.y[:, c, :], src, g_src[:, c, e:e + 1], None, ALU.mult)
                        else:
                            last = dve.scalar_tensor_tensor(gate.y[:, c, :], src, g_src[:, c, e:e + 1],
                                                            gate.y[:, c, :], ALU.mult, ALU.add)
                    last.then_inc(y_taken, 1)
                    dve.wait_ge(y_taken, b * E + (e + 3))
                    if e == E - 4:
                        rows.moments_of(dve, chain, b + 1)
                    if e == E - 3:
                        rows.normalise(dve, b + 1)
                gate.finish(dve, chain, b)

        @block.tensor
        def _(pe):
            pe.wait_ge(weights, 16 * len(loads))
            if top1:
                pe.wait_ge(gate_weights, 4)
                pe.transpose(a_ps[0:GR, 0:E], wg_unit[:], ident[0:E, 0:E]).then_inc(gate_weights, 1)
                pe.wait_ge(gate_weights, 6)
            rows.turn(pe, a_ps, ident, 0)
            with pe.Fori(0, batches) as b:
                pe.wait_ge(rows.xT_ready, b + 1)
                if top1:
                    pe.matmul(gatesT_ps[0:GR, :], w_gate[:], rows.xT[:], start=True, stop=True).then_inc(reduced_done, 1)
                    pe.wait_ge(reduced_ready, b + 1)
                for c in range(NC):
                    lhsT = (reducedT if top1 else rows.xT)[:, c * P:(c + 1) * P]
                    last = pe.matmul(router_ps[:, c * E:(c + 1) * E], lhsT, (wg_unitT if top1 else w_gate)[:],
                                     start=True, stop=True)
                last.then_inc(logits_done, 1)

                def hidden_tiles(g):
                    for k in range(K):
                        n = g * K + k
                        if n >= 2:
                            pe.wait_ge(hidden_ready, b * G * K + (n - 1))
                        pe.matmul(hidden_ps[n % 2][:], w1[:, n, :], rows.xT[:], start=True,
                                  stop=True).then_inc(hidden_done, 1)

                def outputs(g):
                    pe.wait_ge(hidden_ready, b * G * K + (g + 1) * K)
                    for e in range(g * PAIR, (g + 1) * PAIR):
                        pe.wait_ge(y_taken, b * E + (e + 1))
                        for c in range(NC):
                            for k in range(K):
                                last = pe.matmul(y_ps[e % 2][:, c * D:(c + 1) * D],
                                                 hidden[:, g % 2, k, c * P:(c + 1) * P],
                                                 w2[:, e * K + k, :], start=(k == 0), stop=(k == K - 1))
                        last.then_inc(y_done, 1)

                hidden_tiles(0)
                hidden_tiles(1)
                outputs(0)
                if not lora:
                    pe.wait_ge(gates_ready, b + 1)
                    for c in range(NC):
                        last = pe.transpose(gatesT_ps[0:E, c * P:(c + 1) * P], gates[:, c, :], ident[:])
                    last.then_inc(gates_turned, 1)
                hidden_tiles(2)
                if not lora:
                    pe.wait_ge(gatesT_ready, b + 1)
                    outputs(1)
                    for c in range(NC):
                        if capacity:
                            last = pe.transpose(router_ps[:, 64 + c * E:64 + (c + 1) * E],
                                                gatesT[:, c * P:(c + 1) * P], ident[0:E, 0:E])
                        else:
                            last = pe.matmul(extra_ps[:, c * D:(c + 1) * D], gatesT[:, c * P:(c + 1) * P], b2[:],
                                             start=True, stop=True)
                    last.then_inc(back_turned if capacity else bias_done, 1)
                else:
                    outputs(1)
                for g in range(3, G):
                    hidden_tiles(g)
                    outputs(g - 1)
                rows.turn(pe, a_ps, ident, b + 1)
                outputs(G - 1)


def grouped_attention_phase(nc, dram, tag, x_dram, s_dram, batches):
    G, S, W = 8, 8, 64
    R2 = S // 2
    U = G * R2
    DV = D // S

    with nc.cleanup_on_exit(), ExitStack() as ctx:
        def sb(name, shape, dt=F32):
            return ctx.enter_context(nc.sbuf_tensor(f"{tag}_{name}", shape, dt))

        def sem(name):
            return nc.alloc_semaphore(f"{tag}_{name}")

        def ps(name):
            return ctx.enter_context(nc.psum_tensor(f"{tag}_{name}_ps", [P, 512], F32))

        rows = Rows(nc, ctx, tag, x_dram)
        ident = sb("ident", [P, P])
        wq, wk, wv = sb("wq", [D, S, W]), sb("wk", [D, S, W]), sb("wv", [D, D])
        qT = sb("qT", [P, G, S, T // G])
        kT = sb("kT", [P, G, S, T // G])
        own = sb("own", [D, G, T // G])
        own_out = sb("own_out", [D, G, T // G])
        outT = sb("outT", [D, 2, 2, T // G])
        xT_twice = sb("xT_twice", [D, G, 2, T // G])
        v = sb("v", [P, R2, G, DV])
        v_scaled = sb("v_scaled", [P, 3, G * DV])
        probs = sb("probs", [P, 3, T])
        neg_max = sb("neg_max", [P, 3])
        col_sum = sb("col_sum", [P, U])
        inv_sum = sb("inv_sum", [P, U])
        s_out = sb("s_out", [P, NC, D])
        scores_ps = [ps("scores0"), ps("scores1"), ps("scores2")]
        out_ps = [ps("out0"), ps("out1")]
        a_ps = ps("a")
        v_ps = [ps("v0"), ps("v1")]

        weights = sem("weights")
        pads = sem("pads")
        outT_ready, out_turned = sem("outT_ready"), sem("out_turned")
        projected = sem("projected")
        q_kept, k_kept = sem("q_kept"), sem("k_kept")
        twice_ready = sem("twice_ready")
        v_projected, v_ready = sem("v_projected"), sem("v_ready")
        scores_ready, max_ready, probs_ready = sem("scores_ready"), sem("max_ready"), sem("probs_ready")
        v_scaled_ready = sem("v_scaled_ready")
        out_ready = sem("out_ready")
        o_taken = sem("o_taken")
        s_free, s_stored = sem("s_free"), sem("s_stored")
        dve_chain = sem("dve_chain")

        loads = [(ident[:], dram["ident"]), (wq[:].rearrange("p s w -> p (s w)"), dram["L1_Mq"]),
                 (wk[:].rearrange("p s w -> p (s w)"), dram["L1_Mk"]), (wv[:], dram["L1_Mv"]),
                 (own[:], dram["L1_own"])]
        MOMENTS, NORMALISE, TURN = 8, 12, 14
        s_rows = s_dram.rearrange("b (c p) d -> b p c d", p=P)
        banks = [scores_ps[0], out_ps[0], scores_ps[1], out_ps[1]]

        block = ctx.enter_context(nc.Block())

        @block.sync
        def _(sp):
            for dst, src in loads:
                sp.dma_start(dst, src).then_inc(weights, 16)
            rows.load(sp, 0, 0)
            with sp.Fori(0, batches) as b:
                rows.load(sp, b + 1, (b + 1) % batches)

        @block.gpsimd
        def _(pool):
            pool.sem_inc(s_free, 1)
            rows.root(pool, 0)
            with pool.Fori(0, batches) as b:
                rows.root(pool, b + 1)
                pool.wait_ge(o_taken, b + 1)
                pool.dma_start(s_rows[b], s_out[:]).then_inc(s_stored, 16)
                pool.wait_ge(s_stored, b * 16 + 16)
                pool.sem_inc(s_free, 1)

        @block.scalar
        def _(act):
            def keep_twice(b):
                rows.keep_turned(act, a_ps, b)
                act.activation(xT_twice[:], a_ps[:].rearrange("p (g t) -> p g t", g=G).unsqueeze(2)
                               .to_broadcast([D, G, 2, T // G]), ACT.Copy).then_inc(twice_ready, 1)

            keep_twice(0)
            act.wait_ge(pads, 1)
            with act.Fori(0, batches) as b:
                for n in range(S):
                    act.wait_ge(projected, b * 2 * S + (2 * n + 1))
                    act.activation(qT[0:W, :, n, :], banks[2 * n % 4][0:W, :].rearrange("p (g t) -> p g t", g=G),
                                   ACT.Copy, scale=1.0 / math.sqrt(W)).then_inc(q_kept, 1)
                for u in range(U):
                    act.wait_ge(max_ready, b * U + (u + 1))
                    if u >= 3:
                        act.wait_ge(out_ready, b * U + (u - 2))
                    act.activation(probs[:, u % 3, :], scores_ps[u % 3][:], ACT.Exp, bias=neg_max[:, u % 3:u % 3 + 1],
                                   accum_out=col_sum[:, u:u + 1]).then_inc(probs_ready, 1)
                    if u == TURN:
                        keep_twice(b + 1)

        @block.vector
        def _(dve):
            chain = Chain(dve, dve_chain)
            rows.before_loop(dve)
            dve.memset(qT[W:P], 0.0)
            chain(dve.memset(kT[W:P], 0.0))
            dve.sem_inc(pads, 1)
            rows.moments_of(dve, chain, 0)
            rows.normalise(dve, 0)
            with dve.Fori(0, batches) as b:
                chain.restart()
                for n in range(S):
                    dve.wait_ge(projected, b * 2 * S + (2 * n + 2))
                    dve.tensor_copy(kT[0:W, :, n, :], banks[(2 * n + 1) % 4][0:W, :]
                                    .rearrange("p (g t) -> p g t", g=G)).then_inc(k_kept, 1)
                dve.wait_ge(v_projected, b + 1)
                for half in range(2):
                    for n in range(2):
                        lo = half * 64
                        src = v_ps[n][lo:lo + 64, :].rearrange("p (g r two d) -> p r g two d", g=4, r=R2, two=2)
                        dve.tensor_copy(v[lo:lo + 64, :, n * 4:n * 4 + 4, :], src[:, :, :, half, :]).then_inc(v_ready, 1)
                dve.wait_ge(v_ready, b * 4 + 4)

                def col_max(u):
                    dve.wait_ge(scores_ready, b * U + (u + 1))
                    if u >= 3:
                        dve.wait_ge(probs_ready, b * U + (u - 2))
                    dve.tensor_reduce(neg_max[:, u % 3:u % 3 + 1], scores_ps[u % 3][:], AX.X, ALU.max,
                                      negate=True).then_inc(max_ready, 1)

                def scale_v(u):
                    dve.wait_ge(probs_ready, b * U + (u + 1))
                    chain(dve.reciprocal(inv_sum[:, u:u + 1], col_sum[:, u:u + 1]))
                    if u >= 3:
                        dve.wait_ge(out_ready, b * U + (u - 2))
                    dve.tensor_scalar(v_scaled[:, u % 3, :], v[:, u % R2, :, :].rearrange("p g d -> p (g d)"),
                                      inv_sum[:, u:u + 1], None, ALU.mult).then_inc(v_scaled_ready, 1)

                def pick_own(g):
                    dve.wait_ge(out_ready, b * U + (g + 1) * R2)
                    chain(dve.tensor_tensor(own_out[:], out_ps[g % 2][:].rearrange("p (s t) -> p s t", s=S), own[:],
                                            ALU.mult))
                    if g >= 4 and g % 2 == 0:
                        dve.wait_ge(out_turned, b * NC + (g // 2 - 1))
                    dve.tensor_reduce(outT[:, g // 2 % 2, g % 2, :], own_out[:].rearrange("p s t -> p t s"), AX.X,
                                      ALU.add).then_inc(outT_ready, 1)

                for i in range(U + 4):
                    if i < U:
                        col_max(i)
                    if 2 <= i <= U + 1:
                        scale_v(i - 2)
                    if i >= 7 and (i - 3) % R2 == 0:
                        pick_own((i - 3) // R2 - 1)
                    if i == MOMENTS:
                        rows.moments_of(dve, chain, b + 1)
                    if i == NORMALISE:
                        rows.normalise(dve, b + 1)
                dve.wait_ge(s_free, b + 1)
                dve.wait_ge(out_turned, b * NC + NC)
                dve.tensor_copy(s_out[:], v_ps[0][:].rearrange("p (c d) -> p c d", c=NC)).then_inc(o_taken, 1)

        @block.tensor
        def _(pe):
            pe.wait_ge(weights, 16 * len(loads))
            rows.turn(pe, a_ps, ident, 0)
            with pe.Fori(0, batches) as b:
                pe.wait_ge(rows.xT_ready, b + 1)
                for n in range(2 * S):
                    if n >= 4:
                        pe.wait_ge(q_kept if n % 2 == 0 else k_kept, b * S + ((n - 4) // 2 + 1))
                    pe.matmul(banks[n % 4][0:W, :], (wq if n % 2 == 0 else wk)[:, n // 2, :], rows.xT[:],
                              start=True, stop=True).then_inc(projected, 1)
                pe.wait_ge(twice_ready, b + 1)
                for g in range(G):
                    last = pe.matmul(v_ps[g // 4][:, (g % 4) * D:(g % 4 + 1) * D],
                                     xT_twice[:, g, :, :].rearrange("p a t -> p (a t)"), wv[:],
                                     start=True, stop=True)
                last.then_inc(v_projected, 1)
                pe.wait_ge(q_kept, b * S + S)
                pe.wait_ge(k_kept, b * S + S)

                def scores(u):
                    g, r = divmod(u, R2)
                    if u >= 3:
                        pe.wait_ge(probs_ready, b * U + (u - 2))
                    pe.matmul(scores_ps[u % 3][:], kT[:, g, 2 * r:2 * r + 2, :].rearrange("p a t -> p (a t)"),
                              qT[:, g, :, :].rearrange("p s t -> p (s t)"), start=True,
                              stop=True).then_inc(scores_ready, 1)

                def products(u):
                    g, r = divmod(u, R2)
                    pe.wait_ge(v_scaled_ready, b * U + (u + 1))
                    if r == 0 and g >= 2:
                        pe.wait_ge(outT_ready, b * G + (g - 1))
                    pe.matmul(out_ps[g % 2][:], v_scaled[:, u % 3, :], probs[:, u % 3, :], start=(r == 0),
                              stop=(r == R2 - 1)).then_inc(out_ready, 1)

                def turn_out(c):
                    pe.wait_ge(outT_ready, b * G + (2 * c + 2))
                    if c == 0:
                        pe.wait_ge(v_ready, b * 4 + 4)
                    pe.transpose(v_ps[0][:, c * D:(c + 1) * D], outT[:, c % 2, :, :].rearrange("d g t -> d (g t)"),
                                 ident[:]).then_inc(out_turned, 1)

                for i in range(U + 5):
                    if i < U:
                        scores(i)
                    if 3 <= i < U + 3:
                        products(i - 3)
                    if i >= 12 and i % (2 * R2) == R2:
                        turn_out(i // (2 * R2) - 1)
                    if i == TURN:
                        rows.turn(pe, a_ps, ident, b + 1)
                pe.wait_ge(o_taken, b + 1)


def local_transformer_phase(nc, dram, tag, x_dram, s_dram, out_dram, batches):
    L, H, W = 2, 8, 64
    HP = H // 2
    HID = 341
    HK = [128, 128, 85]
    N_ROT = 2 * NC
    N_PAIR = NC * HP
    KEYS = P + W

    with nc.cleanup_on_exit(), ExitStack() as ctx:
        def sb(name, shape, dt=F32):
            return ctx.enter_context(nc.sbuf_tensor(f"{tag}_{name}", shape, dt))

        def sem(name):
            return nc.alloc_semaphore(f"{tag}_{name}")

        def ps(name):
            return ctx.enter_context(nc.psum_tensor(f"{tag}_{name}_ps", [P, 512], F32))

        rows = Rows(nc, ctx, tag, x_dram)
        gate = Gate(nc, ctx, tag, x_dram, s_dram, out_dram)
        x = gate.y
        ident, ident16 = sb("ident", [P, P]), sb("ident16", [P, P], BF16)
        band16, band = sb("band16", [P, KEYS], BF16), sb("band", [P, KEYS])
        rotary = sb("rotary", [P, 4, NC, W])
        scale = sb("scale", [P, 2, L, W])
        turnings = sb("turnings", [P, L, 2, 2, NC, W])
        w_qkv = sb("w_qkv", [D, L, 3 * H * W])
        w_o = sb("w_o", [P, L, 4, D])
        ln_g, ln_b = sb("ln_g", [D, L]), sb("ln_b", [D, L])
        w1, w2 = sb("w1", [D, L, 2 * HID]), sb("w2", [P, L, 3, D])
        b1, b2 = sb("b1", [P, L, 2, 3]), sb("b2", [P, L, D])
        hT = sb("hT", [D, T])
        hnT = sb("hnT", [D, T])
        squares = sb("squares", [P, 2, T])
        sums = sb("sums", [P, 2, H])
        norms = sb("norms", [P, 2, H])
        q_norms = sb("q_norms", [P, NC, H])
        neg_half = sb("neg_half", [P, H])
        cos_part, sin_part = sb("cos_part", [P, 2, T]), sb("sin_part", [P, 2, T])
        turned_rows = sb("turned_rows", [P, 2, T])
        qT, kT = sb("qT", [P, 2, HP, T]), sb("kT", [P, HP, T])
        v = sb("v", [P, NC, H * W])
        probs = sb("probs", [P, 2, 2, 2 * P])
        probsT = sb("probsT", [P, 2, 4 * P])
        row_max, neg_max = sb("row_max", [P, 2, 2]), sb("neg_max", [P, 2, 2])
        row_sum, inv_sum = sb("row_sum", [P, NC * H]), sb("inv_sum", [P, NC * H])
        o = sb("o", [P, NC, H * W])
        oT = sb("oT", [P, 2, 4, P])
        stats, moments = sb("lstats", [P, NC, 6]), sb("lmoments", [P, NC, 2])
        var_eps, rstd = sb("lvar_eps", [P, NC]), sb("lrstd", [P, NC])
        hn = sb("hn", [P, NC, D])
        gelu = sb("gelu", [P, 2, T])
        mixed = sb("mixed", [P, 3, T])
        a_ps, b_ps = ps("a"), ps("b")
        s_ps, t_ps, o_ps = [ps("s0"), ps("s1")], [ps("t0"), ps("t1")], [ps("o0"), ps("o1")]
        chunk_banks = [(o_ps[0], o_ps[1]), (a_ps, b_ps)]
        qkv_banks = [s_ps[0], s_ps[1], o_ps[0], o_ps[1]]

        weights = sem("weights")
        tables = sem("tables")
        x_ready = sem("x_ready")
        x_turned, hT_ready = sem("x_turned"), sem("hT_ready")
        qkv_done = sem("qkv_done")
        squares_ready, sums_ready, rotated = sem("squares_ready"), sem("sums_ready"), sem("rotated")
        rows_turned, rowsT_kept = sem("rows_turned"), sem("rowsT_kept")
        v_kept = sem("v_kept")
        scores_ready, max_ready, probs_ready = sem("scores_ready"), sem("max_ready"), sem("probs_ready")
        probs_turned, probsT_ready, out_ready = sem("probs_turned"), sem("probsT_ready"), sem("out_ready")
        o_taken, o_turned, oT_ready = sem("o_taken"), sem("o_turned"), sem("oT_ready")
        wo_done = sem("wo_done")
        h_back, lvar_ready, lrstd_ready = sem("h_back"), sem("lvar_ready"), sem("lrstd_ready")
        hn_ready, hn_turned, hnT_ready = sem("hn_ready"), sem("hn_turned"), sem("hnT_ready")
        up_done, gelu_ready, mixed_ready = sem("up_done"), sem("gelu_ready"), sem("mixed_ready")
        down_done = sem("down_done")
        pads = sem("pads")
        dve_chain, pool_chain = sem("dve_chain"), sem("pool_chain")

        loads = [(ident[:], dram["ident"]), (band[:], dram["band"]),
                 (rotary[:], dram["L1_rotary"]), (scale[:, 0], dram["L1_q_scale"].partition_broadcast(P)),
                 (scale[:, 1], dram["L1_k_scale"].partition_broadcast(P)),
                 (b2[:], dram["L1_b2"].partition_broadcast(P))]
        for l in range(L):
            loads += [(w_qkv[:, l, :], dram["L1_wqkv"][l]), (w_o[:, l], dram["L1_wo"][l]),
                      (ln_g[:, l:l + 1], dram["L1_ln_g"][l]), (ln_b[:, l:l + 1], dram["L1_ln_b"][l]),
                      (w1[:, l, :], dram["L1_w1"][l])]
            for k, n in enumerate(HK):
                loads += [(w2[0:n, l, k, :], dram["L1_w2"][l, k * P:k * P + n, :])]
                for half in range(2):
                    loads += [(b1[0:n, l, half, k:k + 1],
                               dram["L1_b1"][l, half * HID + k * P:half * HID + k * P + n, :])]

        def own_halves(bank):
            ap = bank[:]
            return bass.AP(ap.tensor, ap.offset, [list(ap.ap[0]), [2 * P, 2], [P + W, 2], [1, W]])

        def heads(ap):
            return ap.rearrange("p (h w) -> p h w", h=H)

        block = ctx.enter_context(nc.Block())

        @block.sync
        def _(sp):
            for dst, src in loads:
                sp.dma_start(dst, src).then_inc(weights, 16)
            rows.load(sp, 0, 0)
            with sp.Fori(0, batches) as b:
                gate.load(sp, b)
                rows.load(sp, b + 1, (b + 1) % batches)

        @block.gpsimd
        def _(pool):
            gate.before_loop(pool)
            chain = Chain(pool, pool_chain)
            pool.wait_ge(pads, 1)
            rows.root(pool, 0)
            with pool.Fori(0, batches) as b:
                chain.restart()
                for l in range(L):
                    for n in range(N_ROT):
                        pool.wait_ge(sums_ready, b * L * N_ROT + (l * N_ROT + n + 1))
                        if n % 2 == 0:
                            pool.tensor_tensor(q_norms[:, n // 2, :], sums[:, n % 2, :], neg_half[:], ALU.pow)
                            if n >= 2:
                                pool.wait_ge(rows_turned, b * L * N_ROT + (l * N_ROT + n - 1))
                            pool.tensor_tensor(turned_rows[:, n % 2, :], cos_part[:, n % 2, :],
                                               sin_part[:, n % 2, :], ALU.add).then_inc(rotated, 1)
                            continue
                        pool.tensor_tensor(norms[:, n % 2, :], sums[:, n % 2, :], neg_half[:], ALU.pow)
                        chain(pool.tensor_tensor(cos_part[:, n % 2, :], cos_part[:, n % 2, :],
                                                 sin_part[:, n % 2, :], ALU.add))
                        if n >= 2:
                            pool.wait_ge(rows_turned, b * L * N_ROT + (l * N_ROT + n - 1))
                        pool.tensor_tensor(heads(turned_rows[:, n % 2, :]), heads(cos_part[:, n % 2, :]),
                                           norms[:, n % 2, :].unsqueeze(2).to_broadcast([P, H, W]),
                                           ALU.mult).then_inc(rotated, 1)
                    if l == L - 1:
                        rows.root(pool, b + 1)
                    pool.wait_ge(lvar_ready, b * L + (l + 1))
                    pool.tensor_tensor(rstd[:], var_eps[:], neg_half[:, 0:NC], ALU.pow).then_inc(lrstd_ready, 1)
                gate.store(pool, b)

        @block.scalar
        def _(act):
            act.wait_ge(weights, 16 * len(loads))
            act.wait_ge(pads, 1)

            def shift(src):
                act.activation(hT[0:W, :], src[0:W, :], ACT.Copy)
                return act.activation(hT[W:D, 1:T], src[W:D, 0:T - 1], ACT.Copy)

            act.wait_ge(x_turned, 1)
            shift(a_ps).then_inc(hT_ready, 1)
            with act.Fori(0, batches) as b:
                for l in range(L):
                    if l:
                        act.wait_ge(x_turned, b * 2 * L + (2 * l + 1))
                        shift(a_ps).then_inc(hT_ready, 1)

                    def first(j):
                        c, kind = divmod(j, 3)
                        bank = qkv_banks[j % 4]
                        act.wait_ge(qkv_done, b * L * 3 * NC + (l * 3 * NC + j + 1))
                        if kind < 2:
                            n = 2 * c + kind
                            if n >= 2:
                                act.wait_ge(sums_ready, b * L * N_ROT + (l * N_ROT + n - 1))
                            act.activation(squares[:, n % 2, :], bank[:], ACT.Square).then_inc(squares_ready, 1)
                        else:
                            act.activation(v[:, c, :], bank[:], ACT.Copy).then_inc(v_kept, 1)

                    def keep(j):
                        c, kind = divmod(j, 3)
                        if kind < 2:
                            n = 2 * c + kind
                            act.wait_ge(rows_turned, b * L * N_ROT + (l * N_ROT + n + 1))
                            turned = t_ps[n % 2][:].rearrange("p (h t) -> p h t", h=HP)
                            if kind == 0:
                                act.activation(qT[0:W, 0, :, c * P:(c + 1) * P], turned[0:W], ACT.Copy)
                                last = act.activation(qT[W:P, 1, :, c * P:(c + 1) * P], turned[W:P], ACT.Copy)
                            else:
                                last = act.activation(kT[:, :, c * P:(c + 1) * P], turned, ACT.Copy)
                            last.then_inc(rowsT_kept, 1)

                    for i in range(3 * NC + 4):
                        if i < 3 * NC:
                            first(i)
                        if i >= 4:
                            keep(i - 4)

                    for i in range(N_PAIR):
                        c = i // HP
                        lo = 0 if c else W
                        act.wait_ge(max_ready, b * L * N_PAIR + (l * N_PAIR + i + 1))
                        if i >= 2:
                            act.wait_ge(probs_turned, b * L * N_PAIR + (l * N_PAIR + i - 1))
                        for hh in range(2):
                            h = (i % HP) * 2 + hh
                            last = act.activation(probs[:, i % 2, hh, W + lo:2 * P],
                                                  s_ps[i % 2][:, hh * KEYS + lo:(hh + 1) * KEYS], ACT.Exp,
                                                  bias=neg_max[:, i % 2, hh:hh + 1],
                                                  scale=q_norms[:, c, h:h + 1],
                                                  accum_out=row_sum[:, c * H + h:c * H + h + 1])
                        last.then_inc(probs_ready, 1)
                    for c in range(NC):
                        act.wait_ge(o_turned, b * L * NC + (l * NC + c + 1))
                        if c >= 2:
                            act.wait_ge(wo_done, b * L * NC + (l * NC + c - 1))
                        act.activation(oT[:, c % 2].rearrange("p k t -> p (k t)"), t_ps[c % 2][:],
                                       ACT.Copy).then_inc(oT_ready, 1)
                    act.wait_ge(x_turned, b * 2 * L + (2 * l + 2))
                    shift(a_ps).then_inc(hT_ready, 1)
                    for k, m in enumerate(HK):
                        act.wait_ge(up_done, b * L * 3 + (l * 3 + k + 1))
                        if k >= 2:
                            act.wait_ge(mixed_ready, b * L * 3 + (l * 3 + k - 1))
                        act.activation(gelu[0:m, k % 2, :], s_ps[k % 2][0:m, :], ACT.Gelu,
                                       bias=b1[0:m, l, 1, k:k + 1]).then_inc(gelu_ready, 1)
                act.wait_ge(x_turned, b * 2 * L + (2 * L + 1))
                shift(a_ps).then_inc(hT_ready, 1)
                gate.exp(act, b)

        @block.vector
        def _(dve):
            chain = Chain(dve, dve_chain)
            rows.before_loop(dve)
            dve.memset(neg_half[:], -0.5)
            dve.memset(hT[W:D, 0:1], 0.0)
            dve.memset(qT[:], 0.0)
            chain(dve.memset(probs[:], 0.0))
            dve.sem_inc(pads, 1)
            dve.wait_ge(weights, 16 * len(loads))
            for l in range(L):
                for kind in range(2):
                    s = scale[:, kind, l, :].unsqueeze(1)
                    HW = W // 2
                    t = turnings[:, l, kind]
                    dve.tensor_tensor(t[:, 0], rotary[:, 2 * kind], s.to_broadcast([P, NC, W]), ALU.mult)
                    for dst, src in ((0, HW), (HW, 0)):
                        last = dve.tensor_tensor(t[:, 1, :, dst:dst + HW], rotary[:, 2 * kind + 1, :, dst:dst + HW],
                                                 s[:, :, src:src + HW].to_broadcast([P, NC, HW]), ALU.mult)
            chain(last)
            dve.tensor_copy(ident16[:], ident[:]).then_inc(tables, 1)
            dve.tensor_copy(band16[:], band[:]).then_inc(tables, 1)

            rows.moments_of(dve, chain, 0)
            rows.normalise(dve, 0)
            with dve.Fori(0, batches) as b:
                chain.restart()
                for l in range(L):
                    for n in range(N_ROT):
                        c, kind = divmod(n, 2)
                        j = 3 * c + kind
                        bank = heads(qkv_banks[j % 4][:])
                        t = turnings[:, l, kind]
                        HW = W // 2
                        dve.wait_ge(squares_ready, b * L * N_ROT + (l * N_ROT + n + 1))
                        if n >= 2:
                            dve.wait_ge(rotated, b * L * N_ROT + (l * N_ROT + n - 1))
                        dve.tensor_tensor(heads(cos_part[:, n % 2, :]), bank,
                                          t[:, 0, c, :].unsqueeze(1).to_broadcast([P, H, W]), ALU.mult)
                        for dst, src in ((0, HW), (HW, 0)):
                            dve.tensor_tensor(heads(sin_part[:, n % 2, :])[:, :, dst:dst + HW],
                                              bank[:, :, src:src + HW],
                                              t[:, 1, c, dst:dst + HW].unsqueeze(1).to_broadcast([P, H, HW]),
                                              ALU.mult)
                        chain(dve.tensor_reduce(sums[:, n % 2, :], heads(squares[:, n % 2, :]), AX.X, ALU.add))
                        dve.tensor_scalar(sums[:, n % 2, :], sums[:, n % 2, :], 1e-24, None,
                                          ALU.max).then_inc(sums_ready, 1)

                    def pair_max(i):
                        lo = 0 if i // HP else W
                        dve.wait_ge(scores_ready, b * L * N_PAIR + (l * N_PAIR + i + 1))
                        src = s_ps[i % 2][:, 0:2 * KEYS].rearrange("p (a k) -> p a k", a=2)
                        chain(dve.tensor_reduce(row_max[:, i % 2, :], src[:, :, lo:KEYS], AX.X, ALU.max, negate=True))
                        if i >= 2:
                            dve.wait_ge(probs_ready, b * L * N_PAIR + (l * N_PAIR + i - 1))
                        c, hp = divmod(i, HP)
                        dve.tensor_tensor(neg_max[:, i % 2, :], row_max[:, i % 2, :],
                                          q_norms[:, c, 2 * hp:2 * hp + 2], ALU.mult).then_inc(max_ready, 1)

                    def keep_probsT(i):
                        n = 4 * P if i // HP else 2 * P
                        dve.wait_ge(probs_turned, b * L * N_PAIR + (l * N_PAIR + i + 1))
                        if i >= 2:
                            dve.wait_ge(out_ready, b * L * N_PAIR + (l * N_PAIR + i - 1))
                        dve.tensor_copy(probsT[:, i % 2, 0:n], t_ps[i % 2][:, 0:n]).then_inc(probsT_ready, 1)

                    def take(c):
                        dve.wait_ge(out_ready, b * L * N_PAIR + (l * N_PAIR + (c + 1) * HP))
                        chain(dve.reciprocal(inv_sum[:, c * H:(c + 1) * H], row_sum[:, c * H:(c + 1) * H]))
                        for n in range(2):
                            lo = c * H + 4 * n
                            last = dve.tensor_tensor(
                                o[:, c, n * 4 * W:(n + 1) * 4 * W].rearrange("p (a h w) -> p a h w", a=2, h=2),
                                own_halves(chunk_banks[c % 2][n]),
                                inv_sum[:, lo:lo + 4].rearrange("p (a h) -> p a h", a=2).unsqueeze(3)
                                .to_broadcast([P, 2, 2, W]), ALU.mult)
                        last.then_inc(o_taken, 1)

                    for i in range(N_PAIR + 2):
                        if i < N_PAIR:
                            pair_max(i)
                        if 1 <= i <= N_PAIR:
                            keep_probsT(i - 1)
                        if i >= 5 and (i - 1) % HP == 0:
                            take((i - 1) // HP - 1)
                        if l == L - 1 and i == 6:
                            rows.moments_of(dve, chain, b + 1)
                        if l == L - 1 and i == 10:
                            rows.normalise(dve, b + 1)
                    dve.wait_ge(wo_done, b * L * NC + (l + 1) * NC)
                    chain(dve.tensor_tensor(x[:], x[:] if l else rows.xn[:], s_ps[0][:].rearrange("p (c d) -> p c d", c=NC), ALU.add))
                    dve.sem_inc(x_ready, 1)

                    dve.wait_ge(h_back, b * L + (l + 1))
                    for c in range(NC):
                        last = dve.bn_stats(stats[:, c, :], b_ps[:, c * D:(c + 1) * D])
                    chain(last)
                    for c in range(NC):
                        last = dve.bn_aggr(moments[:, c, :], stats[:, c, :])
                    chain(last)
                    dve.tensor_scalar(var_eps[:], moments[:, :, 1], EPS, None, ALU.add).then_inc(lvar_ready, 1)
                    dve.wait_ge(lrstd_ready, b * L + (l + 1))
                    for c in range(NC):
                        last = dve.tensor_scalar(hn[:, c, :], b_ps[:, c * D:(c + 1) * D], moments[:, c, 0:1],
                                                 rstd[:, c:c + 1], ALU.subtract, ALU.mult)
                    last.then_inc(hn_ready, 1)
                    dve.wait_ge(hn_turned, b * L + (l + 1))
                    dve.tensor_scalar(hnT[:], a_ps[:], ln_g[:, l:l + 1], ln_b[:, l:l + 1], ALU.mult,
                                      ALU.add).then_inc(hnT_ready, 1)
                    chain(dve.tensor_tensor(x[:], x[:], b2[:, l:l + 1, :].to_broadcast([P, NC, D]), ALU.add))
                    for k, m in enumerate(HK):
                        dve.wait_ge(gelu_ready, b * L * 3 + (l * 3 + k + 1))
                        dve.scalar_tensor_tensor(mixed[0:m, k, :], t_ps[k % 2][0:m, :], b1[0:m, l, 0, k:k + 1],
                                                 gelu[0:m, k % 2, :], ALU.add, ALU.mult).then_inc(mixed_ready, 1)
                    dve.wait_ge(down_done, b * L + (l + 1))
                    chain(dve.tensor_tensor(x[:], x[:], b_ps[:].rearrange("p (c d) -> p c d", c=NC), ALU.add))
                    if l < L - 1:
                        dve.sem_inc(x_ready, 1)
                gate.finish(dve, chain, b)

        @block.tensor
        def _(pe):
            pe.wait_ge(weights, 16 * len(loads))
            pe.wait_ge(tables, 2)

            def turn(src):
                for c in range(NC):
                    last = pe.transpose(a_ps[:, c * P:(c + 1) * P], src[:, c, :], ident[:])
                return last

            def turn_first(b):
                pe.wait_ge(rows.xn_ready, b * NC + NC)
                turn(rows.xn).then_inc(x_turned, 1)

            turn_first(0)
            with pe.Fori(0, batches) as b:
                for l in range(L):
                    if l:
                        pe.wait_ge(x_ready, b * (2 * L - 1) + 2 * l)
                        turn(x).then_inc(x_turned, 1)
                    pe.wait_ge(hT_ready, b * 2 * L + (2 * l + 1))

                    def project(j):
                        c, kind = divmod(j, 3)
                        if j >= 4:
                            cc, kk = divmod(j - 4, 3)
                            if kk < 2:
                                pe.wait_ge(sums_ready, b * L * N_ROT + (l * N_ROT + 2 * cc + kk + 1))
                            else:
                                pe.wait_ge(v_kept, b * L * NC + (l * NC + cc + 1))
                        pe.matmul(qkv_banks[j % 4][:], hT[:, c * P:(c + 1) * P],
                                  w_qkv[:, l, kind * H * W:(kind + 1) * H * W], start=True,
                                  stop=True).then_inc(qkv_done, 1)

                    def turn_rows(j):
                        c, kind = divmod(j, 3)
                        if kind < 2:
                            n = 2 * c + kind
                            pe.wait_ge(rotated, b * L * N_ROT + (l * N_ROT + n + 1))
                            if n >= 2:
                                pe.wait_ge(rowsT_kept, b * L * N_ROT + (l * N_ROT + n - 1))
                            for k in range(HP):
                                last = pe.transpose(t_ps[n % 2][:, k * P:(k + 1) * P],
                                                    turned_rows[:, n % 2, k * P:(k + 1) * P], ident[:])
                            last.then_inc(rows_turned, 1)

                    for i in range(3 * NC + 4):
                        if i < 3 * NC:
                            project(i)
                        if i >= 4:
                            turn_rows(i - 4)
                    pe.wait_ge(rowsT_kept, b * L * N_ROT + (l + 1) * N_ROT)
                    pe.wait_ge(v_kept, b * L * NC + (l + 1) * NC)

                    def scores(i):
                        c, hp = divmod(i, HP)
                        lo = 0 if c else W
                        if i >= 2:
                            pe.wait_ge(probs_ready, b * L * N_PAIR + (l * N_PAIR + i - 1))
                        for hh in range(2):
                            dst = s_ps[i % 2][:, hh * KEYS + lo:(hh + 1) * KEYS]
                            pe.matmul(dst, ident16[:], band16[:, lo:KEYS], start=True, stop=False)
                            last = pe.matmul(dst, qT[:, hh, hp, c * P:(c + 1) * P],
                                             kT[:, hp, c * P - W + lo:(c + 1) * P], start=False, stop=True)
                        last.then_inc(scores_ready, 1)

                    def turn_probs(i):
                        c = i // HP
                        pe.wait_ge(probs_ready, b * L * N_PAIR + (l * N_PAIR + i + 1))
                        if i >= 2:
                            pe.wait_ge(probsT_ready, b * L * N_PAIR + (l * N_PAIR + i - 1))
                        n = 0
                        for hh in range(2):
                            for part in ((0, 1) if c else (1,)):
                                last = pe.transpose(t_ps[i % 2][:, n * P:(n + 1) * P],
                                                    probs[:, i % 2, hh, part * P:(part + 1) * P], ident[:])
                                n += 1
                        last.then_inc(probs_turned, 1)

                    def products(i):
                        c, hp = divmod(i, HP)
                        pe.wait_ge(probsT_ready, b * L * N_PAIR + (l * N_PAIR + i + 1))
                        if hp == 0 and c >= 2:
                            pe.wait_ge(o_taken, b * L * NC + (l * NC + c - 1))
                        n = 0
                        for hh in range(2):
                            h = 2 * hp + hh
                            parts = (c - 1, c) if c else (c,)
                            for cc in parts:
                                last = pe.matmul(chunk_banks[c % 2][h // 4][:, (h % 4) * P:(h % 4 + 1) * P],
                                                 probsT[:, i % 2, n * P:(n + 1) * P],
                                                 v[:, cc, 2 * hp * W:2 * (hp + 1) * W],
                                                 start=(cc == parts[0]), stop=(cc == c))
                                n += 1
                        last.then_inc(out_ready, 1)

                    for i in range(N_PAIR + 2):
                        if i < N_PAIR:
                            scores(i)
                        if 1 <= i <= N_PAIR:
                            turn_probs(i - 1)
                        if i >= 2:
                            products(i - 2)

                    def turn_o(c):
                        pe.wait_ge(o_taken, b * L * NC + (l * NC + c + 1))
                        if c >= 2:
                            pe.wait_ge(oT_ready, b * L * NC + (l * NC + c - 1))
                        for k in range(4):
                            last = pe.transpose(t_ps[c % 2][:, k * P:(k + 1) * P], o[:, c, k * P:(k + 1) * P],
                                                ident[:])
                        last.then_inc(o_turned, 1)

                    def project_o(c):
                        pe.wait_ge(oT_ready, b * L * NC + (l * NC + c + 1))
                        for k in range(4):
                            last = pe.matmul(s_ps[0][:, c * D:(c + 1) * D], oT[:, c % 2, k, :], w_o[:, l, k, :],
                                             start=(k == 0), stop=(k == 3))
                        last.then_inc(wo_done, 1)

                    turn_o(0)
                    for c in range(1, NC):
                        turn_o(c)
                        project_o(c - 1)
                    project_o(NC - 1)

                    pe.wait_ge(x_ready, b * (2 * L - 1) + (2 * l + 1))
                    turn(x).then_inc(x_turned, 1)
                    pe.wait_ge(hT_ready, b * 2 * L + (2 * l + 2))
                    for c in range(NC):
                        last = pe.transpose(b_ps[:, c * D:(c + 1) * D], hT[:, c * P:(c + 1) * P], ident[:])
                    last.then_inc(h_back, 1)
                    pe.wait_ge(hn_ready, b * L + (l + 1))
                    turn(hn).then_inc(hn_turned, 1)
                    pe.wait_ge(hnT_ready, b * L + (l + 1))
                    for k, m in enumerate(HK):
                        if k >= 2:
                            pe.wait_ge(mixed_ready, b * L * 3 + (l * 3 + k - 1))
                        pe.matmul(t_ps[k % 2][0:m, :], w1[:, l, k * P:k * P + m], hnT[:], start=True, stop=True)
                        pe.matmul(s_ps[k % 2][0:m, :], w1[:, l, HID + k * P:HID + k * P + m], hnT[:], start=True,
                                  stop=True).then_inc(up_done, 1)
                    if l == L - 1:
                        turn_first(b + 1)
                    pe.wait_ge(mixed_ready, b * L * 3 + (l + 1) * 3)
                    for c in range(NC):
                        for k, m in enumerate(HK):
                            last = pe.matmul(b_ps[:, c * D:(c + 1) * D], mixed[0:m, k, c * P:(c + 1) * P],
                                             w2[0:m, l, k, :], start=(k == 0), stop=(k == 2))
                    last.then_inc(down_done, 1)


def constants():
    out = {}
    out["ident"] = np.eye(P, dtype=np.float32)
    i, j = np.arange(P)[:, None], np.arange(P)[None, :]
    out["causal"] = np.where(j > i, NEG_BIG, 0.0).astype(np.float32)
    tok = np.arange(T).reshape(NC, P).T
    out["keep_triu"] = (np.arange(T)[None, None, :] >= tok[:, :, None]).astype(np.float32)
    out["L1_own"] = np.repeat((np.arange(8)[None, :] == np.arange(D)[:, None] // 16), 64, axis=1) \
        .reshape(D, 8, 64).astype(np.float32)
    out["rank"] = np.broadcast_to(8.0 - np.arange(8), (P, NC, 8)).astype(np.float32).copy()
    f = np.arange(D)
    out["L0_head_scale"] = ((f[:, None] // 8 == np.arange(16)[None, :]) / math.sqrt(8)).astype(np.float32)
    inv = 1.0 / 10000.0 ** (np.arange(0, 8, 2) / 8)
    ang = (np.arange(T)[None, :].astype(np.float32) * inv.astype(np.float32)[f % 4][:, None]).astype(np.float64)
    root = 8.0 ** -0.25
    out["L2_cos"] = (np.cos(ang) * root).astype(np.float32)
    out["L2_sin"] = (np.sin(ang) * np.where(f % 8 < 4, -1.0, 1.0)[:, None] * root).astype(np.float32)
    k = np.arange(192)[None, :] - 64
    out["band"] = np.where((k > i) | (k < i - 64), NEG_BAND, 0.0).astype(np.float32)
    half = np.arange(0, 64, 2).astype(np.float32)
    inv = (1.0 / 10000.0 ** (half / 64)).astype(np.float32)
    t = np.arange(T).astype(np.float32)
    fr = np.concatenate([t[:, None] * inv[None, :]] * 2, axis=1).astype(np.float32).astype(np.float64)
    base = ((half + 0.4 * 64) / (1.4 * 64)).astype(np.float64)
    power = (t - T // 2) / 32.0
    sc = np.concatenate([base[None, :] ** power[:, None]] * 2, axis=1)
    sign = np.where(np.arange(64) < 32, -1.0, 1.0)[None, :]
    tabs = [np.cos(fr) * sc * 8.0, np.sin(fr) * sc * sign * 8.0, np.cos(fr) / sc, np.sin(fr) / sc * sign]
    out["L1_rotary"] = np.stack(tabs).reshape(4, NC, P, 64).transpose(2, 0, 1, 3).astype(np.float32).copy()
    return out


def layouts(a):
    out = {}
    out["L0_w_in"] = np.stack([a["L0_attn_Wq"].T, a["L0_attn_Wk"].T, a["L0_attn_Wv"].T], axis=1)
    out["L0_WoT"] = a["L0_attn_Wo"].T
    out["L0_w_gate"] = a["L0_ffn_expert_embeddings"].T
    out["L0_w1"] = a["L0_ffn_first_linear"].reshape(16, 128, 128).transpose(2, 0, 1)
    out["L0_w2"] = a["L0_ffn_second_linear"].transpose(0, 2, 1).reshape(16, 128, 128).transpose(1, 0, 2)
    out["L1_Mq"], out["L1_Mk"], out["L1_Mv"] = a["L1_attn_Mq"], a["L1_attn_Mk"], a["L1_attn_Mv"]
    out["L1_wqkv"] = a["L1_ffn_wqkv"]
    out["L1_q_scale"], out["L1_k_scale"] = a["L1_ffn_q_scale"], a["L1_ffn_k_scale"]
    out["L1_wo"] = a["L1_ffn_wo"].reshape(2, 4, 128, 128).transpose(0, 2, 1, 3)
    out["L1_ln_g"], out["L1_ln_b"] = a["L1_ffn_ln_g"].reshape(2, 128, 1), a["L1_ffn_ln_b"].reshape(2, 128, 1)
    out["L1_w1"] = a["L1_ffn_w1"]
    out["L1_b1"] = a["L1_ffn_b1"].reshape(2, 682, 1)
    out["L1_w2"] = a["L1_ffn_w2"]
    out["L1_b2"] = a["L1_ffn_b2"]
    swap = (np.arange(128) // 8) * 8 + (np.arange(128) + 4) % 8
    w, bias = a["L2_attn_Wqkv"], a["L2_attn_bqkv"]
    out["L2_w_in"] = np.stack([w[0:128].T, w[128:256].T, w[256:384].T, w[0:128][swap].T, w[128:256][swap].T], axis=1)
    out["L2_b_in"] = np.stack([bias[0:128], bias[0:128][swap], bias[128:256], bias[128:256][swap]], axis=1)
    out["L2_b_v"] = bias[256:384]
    out["L2_pre"] = np.repeat(a["L2_attn_Wpre"].T, 8, axis=0)
    out["L2_post"] = np.repeat(a["L2_attn_Wpost"].T, 8, axis=1)
    out["L2_WoutT"] = a["L2_attn_Wout"].T
    out["L2_attn_bout"] = a["L2_attn_bout"]
    out["L2f_w_gate"] = a["L2_ffn_Wg"].T
    out["L2_ffn_bg"] = a["L2_ffn_bg"]
    out["L2f_w1"] = a["L2_ffn_W1"].reshape(4, 128, 128).transpose(2, 0, 1)
    w2 = np.zeros((128, 8, 128), a["L2_ffn_W2"].dtype)
    w2[0:64, 0::2] = a["L2_ffn_W2"][0::2].transpose(2, 0, 1)
    w2[64:128, 1::2] = a["L2_ffn_W2"][1::2].transpose(2, 0, 1)
    out["L2f_w2"] = w2
    out["L3_w_in"] = a["L3_attn_W"].reshape(128, 3, 128)
    out["L3f_w_gate"] = a["L3_ffn_wg_red"].T
    out["L3_ffn_wg"] = a["L3_ffn_wg"]
    out["L3f_w1"] = a["L3_ffn_w1"].transpose(1, 0, 2).reshape(128, 32, 128)
    out["L3f_w2"] = a["L3_ffn_w2"].reshape(32, 128, 128).transpose(1, 0, 2)
    out["L3f_b1"] = a["L3_ffn_b1"].reshape(32, 128).T
    out["L3_ffn_b2"] = a["L3_ffn_b2"]
    return out


def program(nc, dram, x_in, x_out, layers, batches):
    scratch = [nc.dram_tensor(f"x_after_{n}", (batches, T, D), F32, kind="Internal").ap() for n in layers[:-1]]
    xs = [x_in] + scratch + [x_out]
    s = nc.dram_tensor("attention_out", (batches, T, D), F32, kind="Internal").ap()
    for n, layer in enumerate(layers):
        src, dst = xs[n], xs[n + 1]
        if layer == 0:
            attention_phase(nc, dram, "a0", "causal", src, s, batches)
            experts_phase(nc, dram, "f0", "capacity", src, s, dst, batches)
        elif layer == 1:
            grouped_attention_phase(nc, dram, "a1", src, s, batches)
            local_transformer_phase(nc, dram, "f1", src, s, dst, batches)
        elif layer == 2:
            attention_phase(nc, dram, "a2", "mixed", src, s, batches)
            experts_phase(nc, dram, "f2", "lora", src, s, dst, batches)
        else:
            attention_phase(nc, dram, "a3", "triu", src, s, batches)
            experts_phase(nc, dram, "f3", "top1", src, s, dst, batches)


def build(nc, inputs, layers, batches):
    arrays, dram = {}, {}
    host = {**constants(), **layouts(inputs), "x": inputs["L0_attn_x"]}
    for name, a in host.items():
        arrays[f"in_{name}"] = np.ascontiguousarray(a)
        dram[name] = nc.dram_tensor(f"in_{name}", a.shape, mybir.dt.from_np(a.dtype), kind="ExternalInput").ap()
    out = nc.dram_tensor("out", (batches, T, D), F32, kind="ExternalOutput").ap()
    program(nc, dram, dram["x"], out, layers, batches)
    return arrays


def kernel(**inputs):
    import concourse.bacc as bacc
    from concourse.bass_utils import run_bass_kernel_spmd

    nc = bacc.Bacc("TRN2", target_bir_lowering=False, num_devices=1)
    a = {name: np.asarray(value) for name, value in inputs.items()}
    arrays = build(nc, a, [0, 1, 2, 3], NB)
    r = run_bass_kernel_spmd(nc, [arrays], core_ids=[0])
    return r.results[0]["out"]
```

```python
import math
from contextlib import ExitStack

import numpy as np

import concourse.bass as bass
from concourse import mybir

F32 = mybir.dt.float32
BF16 = mybir.dt.bfloat16
ALU = mybir.AluOpType
ACT = mybir.ActivationFunctionType
AX = mybir.AxisListType

P = 128
D = 128
T = 512
NC = T // P
NB = 16
EPS = 1e-5
NEG_BIG = -1.0e30
NEG_BAND = -1.0e20
MASK_NEG = -9000000000000000.0


class Chain:

    def __init__(self, eng, sem):
        self.eng, self.sem, self.n = eng, sem, 0

    def restart(self):
        self.eng.sem_clear(self.sem)
        self.n = 0

    def __call__(self, ins):
        self.n += 1
        ins.then_inc(self.sem, 1)
        self.eng.wait_ge(self.sem, self.n)


class Rows:

    def __init__(self, nc, ctx, tag, x_dram):
        def sb(name, shape, dt=F32):
            return ctx.enter_context(nc.sbuf_tensor(f"{tag}_{name}", shape, dt))

        def sem(name):
            return nc.alloc_semaphore(f"{tag}_{name}")

        self.nc = nc
        self.x_dram = x_dram.rearrange("b (c p) d -> b p c d", p=P)
        self.x = sb("x", [P, NC, D])
        self.stats = sb("stats", [P, NC, 6])
        self.moments = sb("moments", [P, NC, 2])
        self.var_eps = sb("var_eps", [P, NC])
        self.rstd = sb("rstd", [P, NC])
        self.half = sb("half", [P, NC])
        self.xn = sb("xn", [P, NC, D])
        self.xT = sb("xT", [D, T])
        self.x_loaded = sem("x_loaded")
        self.x_free = sem("x_free")
        self.half_ready = sem("half_ready")
        self.var_ready = sem("var_ready")
        self.rstd_ready = sem("rstd_ready")
        self.xn_ready = sem("xn_ready")
        self.xn_turned = sem("xn_turned")
        self.xT_ready = sem("xT_ready")

    def load(self, sp, b, at):
        sp.wait_ge(self.x_free, b + 1)
        sp.dma_start(self.x[:], self.x_dram[at]).then_inc(self.x_loaded, 16)

    def before_loop(self, dve):
        dve.memset(self.half[:], -0.5).then_inc(self.half_ready, 1)
        dve.memset(self.stats[:], 0.0).then_inc(self.x_free, 1)

    def root(self, pool, b):
        pool.wait_ge(self.half_ready, 1)
        pool.wait_ge(self.var_ready, b + 1)
        pool.tensor_tensor(self.rstd[:], self.var_eps[:], self.half[:], ALU.pow).then_inc(self.rstd_ready, 1)

    def moments_of(self, dve, chain, b):
        dve.wait_ge(self.x_loaded, b * 16 + 16)
        for c in range(NC):
            last = dve.bn_stats(self.stats[:, c, :], self.x[:, c, :])
        chain(last)
        for c in range(NC):
            last = dve.bn_aggr(self.moments[:, c, :], self.stats[:, c, :])
        chain(last)
        dve.tensor_scalar(self.var_eps[:], self.moments[:, :, 1], EPS, None, ALU.add).then_inc(self.var_ready, 1)

    def normalise(self, dve, b):
        dve.wait_ge(self.rstd_ready, b + 1)
        for c in range(NC):
            last = dve.tensor_scalar(self.xn[:, c, :], self.x[:, c, :], self.moments[:, c, 0:1],
                                     self.rstd[:, c:c + 1], ALU.subtract, ALU.mult)
            last.then_inc(self.xn_ready, 1)
        dve.wait_ge(self.xn_ready, b * NC + NC)
        dve.sem_inc(self.x_free, 1)

    def turn(self, pe, bank, ident, b):
        pe.wait_ge(self.xn_ready, b * NC + NC)
        for c in range(NC):
            last = pe.transpose(bank[:, c * P:(c + 1) * P], self.xn[:, c, :], ident[:])
        last.then_inc(self.xn_turned, 1)

    def keep_turned(self, act, bank, b):
        act.wait_ge(self.xn_turned, b + 1)
        act.activation(self.xT[:], bank[:], ACT.Copy).then_inc(self.xT_ready, 1)


def attention_phase(nc, dram, tag, kind, x_dram, s_dram, batches):
    H = 1 if kind == "triu" else 16
    DH = D // H
    U = NC * H
    causal, mixed, triu = kind == "causal", kind == "mixed", kind == "triu"

    with nc.cleanup_on_exit(), ExitStack() as ctx:
        def sb(name, shape, dt=F32):
            return ctx.enter_context(nc.sbuf_tensor(f"{tag}_{name}", shape, dt))

        def sem(name):
            return nc.alloc_semaphore(f"{tag}_{name}")

        def ps(name):
            return ctx.enter_context(nc.psum_tensor(f"{tag}_{name}_ps", [P, 512], F32))

        rows = Rows(nc, ctx, tag, x_dram)
        ident = sb("ident", [P, P])
        n_w = {"causal": 3, "mixed": 5, "triu": 3}[kind]
        w_in = sb("w_in", [D, n_w, D])
        qT, kT = sb("qT", [D, T]), sb("kT", [D, T])
        v = sb("v", [P, NC, H, 32] if causal else [P, NC, D])
        NS = 3 if causal else 2
        probs = sb("probs", [P, NS, T])
        RT = 8 if causal else 2
        probsT = sb("probsT", [P, RT, T])
        neg_max = sb("neg_max", [P, NS])
        row_sum = sb("row_sum", [P, U])
        inv_sum = sb("inv_sum", [P, U])
        o = sb("o", [P, NC, D])
        s_out = sb("s_out", [P, NC, D])
        if not triu:
            w_out = sb("w_out", [D, D])
            oT = sb("oT", [D, T])
            head_scale = sb("head_scale", [D, H])
            q_head = sb("q_head", [D, 4, P])
        if causal:
            ident16 = sb("ident16", [P, P], BF16)
            mask16, mask = sb("mask16", [P, P], BF16), sb("mask", [P, P])
            outT = sb("outT", [P, NC, P])
        if mixed:
            b_in = sb("b_in", [D, 4])
            b_v = sb("b_v", [P, D])
            b_out = sb("b_out", [P, D])
            cos, sin = sb("cos", [D, T]), sb("sin", [D, T])
            cos_part, sin_part = sb("cos_part", [D, T]), sb("sin_part", [D, T])
            post = sb("post", [P, H, D])
            v_post = sb("v_post", [P, H, NC, D])
        if triu:
            keep = sb("keep", [P, NC, T])
            masked = sb("masked", [P, 2, T])
            is_zero = sb("is_zero", [P, T])
        scores_ps = [ps(f"scores{n}") for n in range(NS)]
        turned_ps = [ps("turned0"), ps("turned1")]
        out_ps = [ps("out0"), ps("out1")]
        a_ps = ps("a")
        b_ps = a_ps if causal else ps("b")
        q_ps, k_ps = (scores_ps[0], scores_ps[1]) if causal else (b_ps, a_ps)

        weights = sem("weights")
        pads = sem("pads")
        mask_ready = sem("mask_ready")
        projected = sem("projected")
        q_ready, k_ready, v_ready = sem("q_ready"), sem("k_ready"), sem("v_ready")
        v_post_ready = sem("v_post_ready")
        q_head_ready = sem("q_head_ready")
        scores_ready = sem("scores_ready")
        max_ready = sem("max_ready")
        probs_ready = sem("probs_ready")
        probs_turned = sem("probs_turned")
        probsT_ready = sem("probsT_ready")
        out_ready = sem("out_ready")
        outT_kept, out_turned = sem("outT_kept"), sem("out_turned")
        o_taken = sem("o_taken")
        o_turned = sem("o_turned")
        oT_ready = sem("oT_ready")
        y_ready = sem("y_ready")
        s_ready = sem("s_ready")
        s_stored = sem("s_stored")
        s_free = sem("s_free")
        dve_chain = sem("dve_chain")

        loads = [(ident[:], dram["ident"])]
        if causal:
            loads += [(w_in[:], dram["L0_w_in"].rearrange("i n o -> i n o")), (w_out[:], dram["L0_WoT"]),
                      (head_scale[:], dram["L0_head_scale"]), (mask[:], dram["causal"])]
        if mixed:
            loads += [(w_in[:], dram["L2_w_in"]), (w_out[:], dram["L2_WoutT"]),
                      (head_scale[:], dram["L2_pre"]), (b_in[:], dram["L2_b_in"]),
                      (b_v[:], dram["L2_b_v"].partition_broadcast(P)),
                      (b_out[:], dram["L2_attn_bout"].partition_broadcast(P)),
                      (cos[:], dram["L2_cos"]), (sin[:], dram["L2_sin"]),
                      (post[:], dram["L2_post"].partition_broadcast(P))]
        if triu:
            loads += [(w_in[:], dram["L3_w_in"]), (keep[:], dram["keep_triu"])]
        SCORE_SCALE = 1.0 / math.sqrt(DH)
        MOMENTS, NORMALISE, TURN = (1, 2, 2) if triu else (U - 24, U - 20, U - 16)
        TURN_BEFORE = (TURN - 8) // H

        NG = U // 4
        s_rows = s_dram.rearrange("b (c p) d -> b p c d", p=P)
        used = (lambda c: (c + 1) * P) if causal else (lambda c: T)

        block = ctx.enter_context(nc.Block())

        @block.sync
        def _(sp):
            for dst, src in loads:
                sp.dma_start(dst, src).then_inc(weights, 16)
            rows.load(sp, 0, 0)
            with sp.Fori(0, batches) as b:
                rows.load(sp, b + 1, (b + 1) % batches)
                sp.wait_ge(s_ready, b + 1)
                sp.dma_start(s_rows[b], s_out[:]).then_inc(s_stored, 16)
                sp.wait_ge(s_stored, b * 16 + 16)
                sp.sem_inc(s_free, 1)

        @block.gpsimd
        def _(pool):
            pool.sem_inc(s_free, 1)
            pool.wait_ge(weights, 16 * len(loads))
            rows.root(pool, 0)
            with pool.Fori(0, batches) as b:
                if not triu:
                    pool.wait_ge(q_ready, b + 1)
                    if mixed:
                        pool.wait_ge(v_ready, b + 1)
                    for u in range(U):
                        c, h = divmod(u, H)
                        if u == MOMENTS + 2:
                            rows.root(pool, b + 1)
                        if u >= 4:
                            pool.wait_ge(scores_ready, b * U + (u - 3))
                        pool.tensor_tensor(q_head[:, u % 4, :], qT[:, c * P:(c + 1) * P],
                                           head_scale[:, h:h + 1].to_broadcast([D, P]),
                                           ALU.mult).then_inc(q_head_ready, 1)
                        if mixed and c == 0:
                            pool.tensor_tensor(v_post[:, h, :, :], v[:],
                                               post[:, h:h + 1, :].to_broadcast([P, NC, D]),
                                               ALU.mult).then_inc(v_post_ready, 1)
                if triu:
                    rows.root(pool, b + 1)

        @block.scalar
        def _(act):
            def keep_projections(b):
                act.wait_ge(projected, b * 3 + 1)
                act.activation(qT[:], q_ps[:], ACT.Copy,
                               scale=(SCORE_SCALE if triu else 1.0)).then_inc(q_ready, 1)
                act.wait_ge(projected, b * 3 + 2)
                act.activation(kT[:], k_ps[:], ACT.Copy).then_inc(k_ready, 1)
                act.wait_ge(projected, b * 3 + 3)
                if causal:
                    act.activation(v[:, :, :, 0:DH], out_ps[0][:].rearrange("p (c h d) -> p c h d", c=NC, h=H),
                                   ACT.Copy).then_inc(v_ready, 1)
                else:
                    act.activation(v[:].rearrange("p c d -> p (c d)"), out_ps[0][:], ACT.Copy).then_inc(v_ready, 1)

            rows.keep_turned(act, a_ps, 0)
            if causal:
                act.wait_ge(pads, 1)
            if not mixed:
                keep_projections(0)
            with act.Fori(0, batches) as b:
                def exps(u):
                    c, h = divmod(u, H)
                    act.wait_ge(max_ready, b * U + (u + 1))
                    if u >= NS:
                        act.wait_ge(probs_turned, b * U + (u - NS + 1))
                    src = masked[:, u % 2, :] if triu else scores_ps[u % NS][:, 0:used(c)]
                    act.activation(probs[:, u % NS, 0:used(c)], src, ACT.Exp, bias=neg_max[:, u % NS:u % NS + 1],
                                   scale=1.0, accum_out=row_sum[:, u:u + 1]).then_inc(probs_ready, 1)

                def keep_probsT(u):
                    act.wait_ge(probs_turned, b * U + (u + 1))
                    if u >= 2:
                        act.wait_ge(out_ready, b * U + (u - 1))
                    act.activation(probsT[:, u % 2, :], turned_ps[u % 2][:], ACT.Copy).then_inc(probsT_ready, 1)

                for i in range(U + 1):
                    if i < U:
                        exps(i)
                    if i >= 1 and not causal:
                        keep_probsT(i - 1)
                    if i == TURN:
                        rows.keep_turned(act, a_ps, b + 1)
                if not mixed:
                    keep_projections(b + 1)
                if not triu:
                    act.wait_ge(o_turned, b + 1)
                    act.activation(oT[:], turned_ps[0][:], ACT.Copy).then_inc(oT_ready, 1)
                if causal:
                    act.wait_ge(y_ready, b + 1)
                    act.wait_ge(s_free, b + 1)
                    act.activation(s_out[:].rearrange("p c d -> p (c d)"), turned_ps[1][:],
                                   ACT.Copy).then_inc(s_ready, 1)

        @block.vector
        def _(dve):
            chain = Chain(dve, dve_chain)
            rows.before_loop(dve)
            dve.wait_ge(weights, 16 * len(loads))
            if causal:
                dve.tensor_copy(ident16[:], ident[:]).then_inc(mask_ready, 1)
                dve.tensor_copy(mask16[:], mask[:]).then_inc(mask_ready, 1)
                dve.memset(v[:], 0.0).then_inc(pads, 1)

            def rotate_projections(b):
                for n, (plain, swapped, dst, ready) in enumerate(
                        [(b_ps, scores_ps[0], qT, q_ready), (a_ps, scores_ps[1], kT, k_ready)]):
                    dve.wait_ge(projected, b * 5 + 2 * n + 1)
                    dve.scalar_tensor_tensor(cos_part[:], plain[:], b_in[:, 2 * n:2 * n + 1], cos[:],
                                             ALU.add, ALU.mult)
                    dve.wait_ge(projected, b * 5 + 2 * n + 2)
                    chain(dve.scalar_tensor_tensor(sin_part[:], swapped[:], b_in[:, 2 * n + 1:2 * n + 2],
                                                   sin[:], ALU.add, ALU.mult))
                    dve.tensor_tensor(dst[:], cos_part[:], sin_part[:], ALU.add).then_inc(ready, 1)
                    dve.wait_ge(ready, b + 1)
                dve.wait_ge(projected, b * 5 + 5)
                dve.tensor_tensor(v[:], out_ps[0][:].rearrange("p (c d) -> p c d", c=NC),
                                  b_v[:].unsqueeze(1).to_broadcast([P, NC, D]),
                                  ALU.add).then_inc(v_ready, 1)

            rows.moments_of(dve, chain, 0)
            rows.normalise(dve, 0)
            if mixed:
                rotate_projections(0)
            with dve.Fori(0, batches) as b:
                chain.restart()
                def row_max(u):
                    c, h = divmod(u, H)
                    dve.wait_ge(scores_ready, b * U + (u + 1))
                    if u >= NS:
                        dve.wait_ge(probs_ready, b * U + (u - NS + 1))
                    src = scores_ps[u % NS][:, 0:used(c)]
                    if triu:
                        m = masked[:, u % 2, :]
                        chain(dve.tensor_tensor(m, src, keep[:, c, :], ALU.mult))
                        chain(dve.tensor_scalar(is_zero[:], m, 0.0, MASK_NEG, ALU.is_equal, ALU.mult))
                        chain(dve.tensor_tensor(m, m, is_zero[:], ALU.add))
                        src = m
                    dve.tensor_reduce(neg_max[:, u % NS:u % NS + 1], src, AX.X, ALU.max,
                                      negate=True).then_inc(max_ready, 1)

                def keep_probsT(u):
                    c = u // H
                    dve.wait_ge(probs_turned, b * U + (u + 1))
                    if u >= RT:
                        dve.wait_ge(out_ready, b * NG + (u // 4 - 1))
                    dve.tensor_copy(probsT[:, u % RT, 0:used(c)],
                                    turned_ps[u % 2][:, 0:used(c)]).then_inc(probsT_ready, 1)

                def keep_outT(c):
                    dve.wait_ge(out_ready, b * NG + (c + 1) * 4)
                    if c >= 1:
                        dve.wait_ge(out_turned, b * NC + c)
                    dve.tensor_copy(outT[:].rearrange("p g t -> p (g t)"), out_ps[c % 2][:]).then_inc(outT_kept, 1)

                def take_chunk(c):
                    heads = slice(c * H, (c + 1) * H)
                    chain(dve.reciprocal(inv_sum[:, heads], row_sum[:, heads]))
                    dve.wait_ge(out_turned, b * NC + (c + 1))
                    dve.tensor_tensor(o[:, c, :].rearrange("p (h d) -> p h d", h=H),
                                      b_ps[:].rearrange("p (h d) -> p h d", h=H)[:, :, 0:DH],
                                      inv_sum[:, heads].unsqueeze(2).to_broadcast([P, H, DH]),
                                      ALU.mult).then_inc(o_taken, 1)

                def take_unit(u):
                    c, h = divmod(u, H)
                    dve.wait_ge(out_ready, b * U + (u + 1))
                    chain(dve.reciprocal(inv_sum[:, u:u + 1], row_sum[:, u:u + 1]))
                    dst = s_out if triu else o
                    if h == 0:
                        if triu and c == 0:
                            dve.wait_ge(s_free, b + 1)
                        dve.tensor_scalar(dst[:, c, :], out_ps[u % 2][:, 0:D], inv_sum[:, u:u + 1], None,
                                          ALU.mult).then_inc(o_taken, 1)
                    else:
                        dve.wait_ge(o_taken, b * U + u)
                        dve.scalar_tensor_tensor(o[:, c, :], out_ps[u % 2][:, 0:D], inv_sum[:, u:u + 1],
                                                 o[:, c, :], ALU.mult, ALU.add).then_inc(o_taken, 1)

                for i in range(U + (9 if causal else 2)):
                    if i < U:
                        row_max(i)
                    if causal and 2 <= i <= U + 1:
                        keep_probsT(i - 2)
                    if causal and i >= 22 and i % H == 6:
                        keep_outT((i - 22) // H)
                    if causal and i >= 24 and i % H == 8:
                        take_chunk((i - 24) // H)
                    if not causal and i >= 2:
                        take_unit(i - 2)
                    if i == MOMENTS:
                        rows.moments_of(dve, chain, b + 1)
                    if i == NORMALISE:
                        rows.normalise(dve, b + 1)
                if mixed:
                    rotate_projections(b + 1)
                    dve.wait_ge(y_ready, b + 1)
                    dve.wait_ge(s_free, b + 1)
                    dve.tensor_tensor(s_out[:], turned_ps[1][:].rearrange("p (c d) -> p c d", c=NC),
                                      b_out[:].unsqueeze(1).to_broadcast([P, NC, D]),
                                      ALU.add).then_inc(s_ready, 1)
                if triu:
                    dve.wait_ge(o_taken, b * U + U)
                    dve.sem_inc(s_ready, 1)

        @block.tensor
        def _(pe):
            pe.wait_ge(weights, 16 * len(loads))
            if causal:
                pe.wait_ge(mask_ready, 2)
            n_taken = NC if causal else U

            def project(b):
                pe.wait_ge(rows.xT_ready, b + 1)
                banks = [(0, b_ps), (3, scores_ps[0]), (1, a_ps), (4, scores_ps[1])] if mixed else \
                    [(0, q_ps), (1, k_ps)]
                for n, bank in banks:
                    pe.matmul(bank[:], w_in[:, n, :], rows.xT[:], start=True, stop=True).then_inc(projected, 1)
                for c in range(NC):
                    last = pe.matmul(out_ps[0][:, c * D:(c + 1) * D], rows.xT[:, c * P:(c + 1) * P], w_in[:, 2, :],
                                     start=True, stop=True)
                last.then_inc(projected, 1)

            rows.turn(pe, a_ps, ident, 0)
            project(0)
            with pe.Fori(0, batches) as b:
                pe.wait_ge(k_ready, b + 1)
                if triu:
                    pe.wait_ge(q_ready, b + 1)
                    pe.wait_ge(v_ready, b + 1)

                def scores(u):
                    c, h = divmod(u, H)
                    if not triu:
                        pe.wait_ge(q_head_ready, b * U + (u + 1))
                    if u >= NS:
                        pe.wait_ge(probs_ready, b * U + (u - NS + 1))
                    q = qT[:, c * P:(c + 1) * P] if triu else q_head[:, u % 4, :]
                    if causal:
                        pe.matmul(scores_ps[u % NS][:, c * P:(c + 1) * P], ident16[:], mask16[:],
                                  start=True, stop=False, skip_group_check=True)
                    pe.matmul(scores_ps[u % NS][:, 0:used(c)], q, kT[:, 0:used(c)], start=not causal, stop=True,
                              skip_group_check=causal).then_inc(scores_ready, 1)

                def turn_probs(u):
                    c = u // H
                    pe.wait_ge(probs_ready, b * U + (u + 1))
                    if u >= 2:
                        pe.wait_ge(probsT_ready, b * U + (u - 1))
                    for j in range(used(c) // P):
                        last = pe.transpose(turned_ps[u % 2][:, j * P:(j + 1) * P],
                                            probs[:, u % NS, j * P:(j + 1) * P], ident[:])
                    last.then_inc(probs_turned, 1)

                def products(u):
                    c, h = divmod(u, H)
                    pe.wait_ge(probsT_ready, b * U + (u + 1))
                    if u == 0 and mixed:
                        pe.wait_ge(v_ready, b + 1)
                    if u >= 2:
                        pe.wait_ge(o_taken, b * U + (u - 1))
                    if mixed and c == 0:
                        pe.wait_ge(v_post_ready, b * H + (h + 1))
                    dst = out_ps[u % 2][:, 0:D]
                    n = used(c) // P
                    for j in range(n):
                        rhs = v_post[:, h, j, :] if mixed else v[:, j, :]
                        last = pe.matmul(dst, probsT[:, u % 2, j * P:(j + 1) * P], rhs,
                                         start=(j == 0), stop=(j == n - 1))
                    last.then_inc(out_ready, 1)

                def group_products(n, j):
                    c, four = divmod(n, H // 4)
                    if j == 0:
                        pe.wait_ge(probsT_ready, b * U + (4 * n + 4))
                        if n == 0:
                            pe.wait_ge(v_ready, b + 1)
                        if four == 0 and c >= 2:
                            pe.wait_ge(outT_kept, b * NC + (c - 1))
                    for k in range(4):
                        last = pe.matmul(out_ps[c % 2][32 * k:32 * k + 32, four * P:(four + 1) * P],
                                         v[:, j, 4 * four + k, :],
                                         probsT[:, (4 * n + k) % RT, j * P:(j + 1) * P], start=(j == 0),
                                         stop=(j == c))
                    if j == c:
                        last.then_inc(out_ready, 1)

                def turn_out(c):
                    pe.wait_ge(outT_kept, b * NC + (c + 1))
                    if c >= 1:
                        pe.wait_ge(o_taken, b * NC + c)
                    if c == TURN_BEFORE:
                        pe.wait_ge(rows.xT_ready, b + 2)
                    for k in range(NC):
                        last = pe.transpose(b_ps[:, k * P:(k + 1) * P], outT[:, k, :], ident[:])
                    last.then_inc(out_turned, 1)

                for i in range(U + (8 if causal else 2)):
                    if i < U:
                        scores(i)
                    if causal:
                        if 2 <= i <= U + 1:
                            turn_probs(i - 2)
                        n, j = divmod(i - 6, 4)
                        if 0 <= n < NG and j <= n // (H // 4):
                            group_products(n, j)
                        if i == U + 5:
                            pe.wait_ge(probs_ready, b * U + U)
                            pe.wait_ge(outT_kept, b * NC + (NC - 1))
                            project(b + 1)
                        if i >= 23 and i % H == 7:
                            turn_out((i - 23) // H)
                    else:
                        if 1 <= i <= U:
                            turn_probs(i - 1)
                        if i >= 2:
                            products(i - 2)
                    if i == TURN:
                        if causal:
                            pe.wait_ge(o_taken, b * NC + TURN_BEFORE)
                        rows.turn(pe, a_ps, ident, b + 1)
                if not causal:
                    pe.wait_ge(o_taken, b * n_taken + (n_taken - 1))
                    project(b + 1)
                pe.wait_ge(o_taken, b * n_taken + n_taken)
                if not triu:
                    for c in range(NC):
                        last = pe.transpose(turned_ps[0][:, c * P:(c + 1) * P], o[:, c, :], ident[:])
                    last.then_inc(o_turned, 1)
                    pe.wait_ge(oT_ready, b + 1)
                    for c in range(NC):
                        last = pe.matmul(turned_ps[1][:, c * D:(c + 1) * D], oT[:, c * P:(c + 1) * P], w_out[:],
                                         start=True, stop=True)
                    last.then_inc(y_ready, 1)
                    pe.wait_ge(s_ready, b + 1)


class Gate:

    def __init__(self, nc, ctx, tag, x_dram, s_dram, out_dram):
        def sb(name):
            return ctx.enter_context(nc.sbuf_tensor(f"{tag}_{name}", [P, NC, D], F32))

        def sem(name):
            return nc.alloc_semaphore(f"{tag}_{name}")

        self.x_rows, self.s_rows, self.out_rows = (
            a.rearrange("b (c p) d -> b p c d", p=P) for a in (x_dram, s_dram, out_dram))
        self.x, self.s, self.y, self.e, self.out = sb("gx"), sb("gs"), sb("y"), sb("ge"), sb("gout")
        self.loaded = sem("gate_loaded")
        self.free = sem("gate_free")
        self.neg_abs_ready = sem("neg_abs_ready")
        self.exp_ready = sem("exp_ready")
        self.out_full = sem("out_full")
        self.stored = sem("stored")
        self.out_free = sem("out_free")

    def load(self, sp, b):
        sp.wait_ge(self.free, b + 1)
        sp.dma_start(self.x[:], self.x_rows[b]).then_inc(self.loaded, 16)
        sp.dma_start(self.s[:], self.s_rows[b]).then_inc(self.loaded, 16)

    def exp(self, act, b):
        act.wait_ge(self.neg_abs_ready, b + 1)
        act.activation(self.e[:], self.e[:], ACT.Exp).then_inc(self.exp_ready, 1)

    def finish(self, dve, chain, b):
        self.finish_first(dve, b)
        self.finish_rest(dve, chain, b)

    def finish_first(self, dve, b):
        dve.scalar_tensor_tensor(self.e[:], self.y[:], -1.0, self.y[:], ALU.mult,
                                 ALU.min).then_inc(self.neg_abs_ready, 1)

    def finish_rest(self, dve, chain, b):
        dve.wait_ge(self.loaded, b * 32 + 32)
        chain(dve.tensor_tensor(self.s[:], self.s[:], self.y[:], ALU.mult))
        dve.wait_ge(self.exp_ready, b + 1)
        chain(dve.scalar_tensor_tensor(self.y[:], self.y[:], 0.0, self.e[:], ALU.is_ge, ALU.max))
        dve.tensor_scalar(self.e[:], self.e[:], 1.0, None, ALU.add)
        chain(dve.tensor_tensor(self.s[:], self.s[:], self.y[:], ALU.mult))
        chain(dve.reciprocal(self.e[:], self.e[:]))
        chain(dve.tensor_tensor(self.s[:], self.s[:], self.e[:], ALU.mult))
        dve.wait_ge(self.out_free, b + 1)
        dve.tensor_tensor(self.out[:], self.s[:], self.x[:], ALU.add).then_inc(self.out_full, 1)
        dve.wait_ge(self.out_full, b + 1)
        dve.sem_inc(self.free, 1)

    def before_loop(self, pool):
        pool.sem_inc(self.free, 1)
        pool.sem_inc(self.out_free, 1)

    def store(self, sp, b):
        sp.wait_ge(self.out_full, b + 1)
        sp.dma_start(self.out_rows[b], self.out[:]).then_inc(self.stored, 16)
        sp.wait_ge(self.stored, b * 16 + 16)
        sp.sem_inc(self.out_free, 1)


def experts_phase(nc, dram, tag, kind, x_dram, s_dram, out_dram, batches):
    E = 8
    capacity, lora, top1 = kind == "capacity", kind == "lora", kind == "top1"
    I = {"capacity": 256, "lora": 64, "top1": 512}[kind]
    PAIR = max(1, P // I)
    K = max(1, I // P)
    G = E // PAIR
    CAPACITY = NB * T // E
    GR = 16

    with nc.cleanup_on_exit(), ExitStack() as ctx:
        def sb(name, shape, dt=F32):
            return ctx.enter_context(nc.sbuf_tensor(f"{tag}_{name}", shape, dt))

        def sem(name):
            return nc.alloc_semaphore(f"{tag}_{name}")

        def ps(name):
            return ctx.enter_context(nc.psum_tensor(f"{tag}_{name}_ps", [P, 512], F32))

        rows = Rows(nc, ctx, tag, x_dram)
        gate = Gate(nc, ctx, tag, x_dram, s_dram, out_dram)
        ident = sb("ident", [P, P])
        rank = sb("rank", [P, NC, E])
        w_gate = sb("w_gate", [D, GR if top1 else E])
        w1 = sb("w1", [D, G * K, P])
        w2 = sb("w2", [P, E * K, D])
        hidden = sb("hidden", [P, 2, K, T])
        logits = sb("logits", [P, NC, E])
        eq = sb("eq", [P, NC, E])
        first = sb("first", [P, NC, E])
        second = sb("second", [P, NC, E])
        top = sb("top", [P, NC])
        top_rank = sb("top_rank", [P, NC])
        top2 = sb("top2", [P, NC])
        diff = sb("diff", [P, NC, E] if top1 else [P, NC])
        weight = sb("weight", [P, NC])
        weight2 = sb("weight2", [P, NC])
        gates = sb("gates", [P, NC, E])
        gates_now = sb("gates_now", [P, NC, E])
        xT_next = sb("xT_next", [D, T])
        gatesT = sb("gatesT", [E, T])
        if capacity:
            picked, zeros, count = sb("picked", [E, T]), sb("zeros", [E, T]), sb("count", [E, T])
            carry = sb("carry", [E, 1])
            capped = sb("capped", [P, NC, E])
        if lora:
            b_gate = sb("b_gate", [P, E])
        if top1:
            b1 = sb("b1", [P, E * K])
            b2 = sb("b2", [E, D])
            wg, wg_sq, wg_norm = sb("wg", [E, GR]), sb("wg_sq", [E, GR]), sb("wg_norm", [E, 1])
            wg_half = sb("wg_half", [E, 1])
            wg_unit = sb("wg_unit", [E, GR])
            wg_unitT = sb("wg_unitT", [GR, E])
            reducedT = sb("reducedT", [GR, T])
        hidden_ps = [ps("hidden0"), ps("hidden1")]
        y_ps = [ps("y0"), ps("y1")]
        a_ps, router_ps, gatesT_ps, extra_ps = ps("a"), ps("router"), ps("gatesT"), ps("extra")

        weights = sem("weights")
        gate_weights = sem("gate_weights")
        reduced_done, reduced_ready = sem("reduced_done"), sem("reduced_ready")
        next_ready = sem("next_ready")
        logits_done = sem("logits_done")
        diff_ready, weight_ready = sem("diff_ready"), sem("weight_ready")
        gates_ready = sem("gates_ready")
        gates_turned, gatesT_ready = sem("gates_turned"), sem("gatesT_ready")
        back_turned = sem("back_turned")
        bias_done = sem("bias_done")
        hidden_done, hidden_ready = sem("hidden_done"), sem("hidden_ready")
        y_done, y_taken = sem("y_done"), sem("y_taken")
        dve_chain = sem("dve_chain")

        pre = {"capacity": "L0", "lora": "L2f", "top1": "L3f"}[kind]
        loads = [(ident[:], dram["ident"]), (rank[:], dram["rank"]), (w_gate[:], dram[f"{pre}_w_gate"]),
                 (w1[:], dram[f"{pre}_w1"]), (w2[:], dram[f"{pre}_w2"])]
        if lora:
            loads += [(b_gate[:], dram["L2_ffn_bg"].partition_broadcast(P))]
        if top1:
            loads += [(b1[:], dram["L3f_b1"]), (b2[:], dram["L3_ffn_b2"]), (wg[:], dram["L3_ffn_wg"])]
        act_fn = ACT.Relu if capacity else ACT.Gelu
        TURN = 2

        block = ctx.enter_context(nc.Block())

        @block.sync
        def _(sp):
            for dst, src in loads:
                sp.dma_start(dst, src).then_inc(weights, 16)
            rows.load(sp, 0, 0)
            with sp.Fori(0, batches) as b:
                gate.load(sp, b)
                rows.load(sp, b + 1, (b + 1) % batches)
                gate.store(sp, b)

        @block.gpsimd
        def _(pool):
            gate.before_loop(pool)
            if top1:
                pool.wait_ge(gate_weights, 2)
                pool.tensor_tensor(wg_norm[:], wg_norm[:], wg_half[:], ALU.pow).then_inc(gate_weights, 1)
            rows.root(pool, 0)
            with pool.Fori(0, batches) as b:
                rows.root(pool, b + 1)

        @block.scalar
        def _(act):
            act.wait_ge(weights, 16 * len(loads))
            if top1:
                act.wait_ge(gate_weights, 5)
                act.activation(wg_unitT[:], a_ps[0:GR, 0:E], ACT.Copy).then_inc(gate_weights, 1)

            def keep_next(r):
                act.wait_ge(rows.xn_turned, r + 1)
                act.activation(xT_next[:], a_ps[:], ACT.Copy).then_inc(next_ready, 1)

            def keep_reduced(r):
                act.wait_ge(reduced_done, r + 1)
                act.activation(reducedT[:], gatesT_ps[0:GR, :], ACT.Copy).then_inc(reduced_ready, 1)

            def exp_diff(r):
                act.wait_ge(diff_ready, r + 1)
                act.activation(diff[:], diff[:], ACT.Exp).then_inc(weight_ready, 1)

            keep_next(0)
            rows.keep_turned(act, a_ps, 0)
            if top1:
                keep_reduced(0)
            exp_diff(0)
            with act.Fori(0, batches) as b:
                for g in range(G):
                    if g >= 2:
                        act.wait_ge(y_done, b * E + (g - 1) * PAIR)
                    for k in range(K):
                        n = g * K + k
                        act.wait_ge(hidden_done, b * G * K + (n + 1))
                        bias = b1[:, n:n + 1] if top1 else 0.0
                        act.activation(hidden[:, g % 2, k, :], hidden_ps[n % 2][:], act_fn,
                                       bias=bias).then_inc(hidden_ready, 1)
                    if g == TURN // PAIR + 1:
                        keep_next(b + 1)
                    if top1 and g == TURN + 2:
                        keep_reduced(b + 1)
                rows.keep_turned(act, a_ps, b + 1)
                exp_diff(b + 1)
                gate.exp(act, b)

        @block.vector
        def _(dve):
            chain = Chain(dve, dve_chain)
            rows.before_loop(dve)
            dve.wait_ge(weights, 16 * len(loads))
            if capacity:
                dve.memset(zeros[:], 0.0)
                chain(dve.memset(carry[:], 0.0))
            if top1:
                chain(dve.tensor_tensor(wg_sq[:], wg[:], wg[:], ALU.mult))
                dve.memset(wg_half[:], 0.5).then_inc(gate_weights, 1)
                dve.tensor_reduce(wg_norm[:], wg_sq[:], AX.X, ALU.add).then_inc(gate_weights, 1)
                dve.wait_ge(gate_weights, 3)
                chain(dve.tensor_scalar(wg_norm[:], wg_norm[:], 1e-4, None, ALU.max))
                chain(dve.reciprocal(wg_norm[:], wg_norm[:]))
                dve.tensor_scalar(wg_unit[:], wg[:], wg_norm[:], None, ALU.mult).then_inc(gate_weights, 1)

            def wide(a):
                return a[:].unsqueeze(2).to_broadcast([P, NC, E])

            def one_hot(dst, top_value):
                chain(dve.tensor_reduce(top_value[:], logits[:], AX.X, ALU.max))
                chain(dve.tensor_tensor(eq[:], logits[:], wide(top_value), ALU.is_equal))
                chain(dve.tensor_tensor(eq[:], eq[:], rank[:], ALU.mult))
                chain(dve.tensor_reduce(top_rank[:], eq[:], AX.X, ALU.max))
                chain(dve.tensor_tensor(dst[:], eq[:], wide(top_rank), ALU.is_equal))

            def route_first(r):
                dve.wait_ge(logits_done, r + 1)
                src = router_ps[:, 0:NC * E].rearrange("p (c e) -> p c e", c=NC)
                if lora:
                    chain(dve.tensor_tensor(logits[:], src, b_gate[:].unsqueeze(1).to_broadcast([P, NC, E]), ALU.add))
                else:
                    chain(dve.tensor_copy(logits[:], src))
                one_hot(first, top)

            def route_second(r):
                if top1:
                    dve.tensor_tensor(diff[:], logits[:], wide(top), ALU.subtract).then_inc(diff_ready, 1)
                else:
                    chain(dve.scalar_tensor_tensor(logits[:], first[:], -3.0e38, logits[:], ALU.mult, ALU.add))
                    one_hot(second, top2)
                    dve.tensor_tensor(diff[:], top2[:], top[:], ALU.subtract).then_inc(diff_ready, 1)

            def weigh(r):
                dve.wait_ge(weight_ready, r + 1)
                if top1:
                    chain(dve.tensor_reduce(weight[:], diff[:], AX.X, ALU.add))
                    chain(dve.reciprocal(weight[:], weight[:]))
                    dve.tensor_tensor(gates[:], first[:], wide(weight), ALU.mult).then_inc(gates_ready, 1)
                else:
                    chain(dve.tensor_scalar(weight[:], diff[:], 1.0, None, ALU.add))
                    chain(dve.reciprocal(weight[:], weight[:]))
                    if lora:
                        chain(dve.tensor_scalar(weight[:], weight[:], 2.0, None, ALU.mult))
                    chain(dve.tensor_tensor(weight2[:], diff[:], weight[:], ALU.mult))
                    dve.tensor_tensor(first[:], first[:], wide(weight), ALU.mult)
                    chain(dve.tensor_tensor(second[:], second[:], wide(weight2), ALU.mult))
                    dve.tensor_tensor(gates[:], first[:], second[:], ALU.add).then_inc(gates_ready, 1)
                dve.wait_ge(gates_ready, r + 1)

            def turned_gates(r):
                if not lora:
                    dve.wait_ge(gates_turned, r + 1)
                if capacity:
                    chain(dve.tensor_copy(gatesT[:], gatesT_ps[0:E, :]))
                    chain(dve.tensor_scalar(picked[:], gatesT[:], 0.0, None, ALU.is_gt))
                    chain(dve.tensor_tensor_scan(count[:], picked[:], zeros[:], carry[:], ALU.add, ALU.add))
                    dve.tensor_copy(carry[:], count[:, T - 1:T])
                    chain(dve.scalar_tensor_tensor(gatesT[:], count[:], float(CAPACITY), gatesT[:],
                                                   ALU.is_le, ALU.mult))
                    dve.sem_inc(gatesT_ready, 1)
                if top1:
                    dve.tensor_copy(gatesT[:], gatesT_ps[0:E, :]).then_inc(gatesT_ready, 1)

            rows.moments_of(dve, chain, 0)
            rows.normalise(dve, 0)
            dve.sem_inc(y_taken, 2)
            for part in (route_first, route_second, weigh, turned_gates):
                part(0)
            with dve.Fori(0, batches) as b:
                chain.restart()
                if capacity:
                    dve.wait_ge(back_turned, b + 1)
                    chain(dve.tensor_copy(gates_now[:], router_ps[:, 64:64 + NC * E].rearrange("p (c e) -> p c e", c=NC)))
                else:
                    chain(dve.tensor_copy(gates_now[:], gates[:]))
                if top1:
                    dve.wait_ge(bias_done, b + 1)
                    chain(dve.tensor_copy(gate.y[:], extra_ps[:].rearrange("p (c d) -> p c d", c=NC)))
                for e in range(E):
                    dve.wait_ge(y_done, b * E + (e + 1))
                    for c in range(NC):
                        src = y_ps[e % 2][:, c * D:(c + 1) * D]
                        if e == 0 and not top1:
                            last = dve.tensor_scalar(gate.y[:, c, :], src, gates_now[:, c, e:e + 1], None, ALU.mult)
                        else:
                            last = dve.scalar_tensor_tensor(gate.y[:, c, :], src, gates_now[:, c, e:e + 1],
                                                            gate.y[:, c, :], ALU.mult, ALU.add)
                    last.then_inc(y_taken, 1)
                    dve.wait_ge(y_taken, b * E + (e + 3))
                    if e == TURN - 2:
                        rows.moments_of(dve, chain, b + 1)
                    if e == TURN - 1:
                        rows.normalise(dve, b + 1)
                    if e == TURN + 2:
                        route_first(b + 1)
                    if e == TURN + 3:
                        route_second(b + 1)
                    if e == TURN + 4:
                        weigh(b + 1)
                gate.finish(dve, chain, b)
                turned_gates(b + 1)

        @block.tensor
        def _(pe):
            pe.wait_ge(weights, 16 * len(loads))
            if top1:
                pe.wait_ge(gate_weights, 4)
                pe.transpose(a_ps[0:GR, 0:E], wg_unit[:], ident[0:E, 0:E]).then_inc(gate_weights, 1)
                pe.wait_ge(gate_weights, 6)

            def reduce_rows(r):
                pe.wait_ge(next_ready, r + 1)
                pe.matmul(gatesT_ps[0:GR, :], w_gate[:], xT_next[:], start=True, stop=True).then_inc(reduced_done, 1)

            def router(r):
                pe.wait_ge(reduced_ready if top1 else next_ready, r + 1)
                for c in range(NC):
                    lhsT = (reducedT if top1 else xT_next)[:, c * P:(c + 1) * P]
                    last = pe.matmul(router_ps[:, c * E:(c + 1) * E], lhsT, (wg_unitT if top1 else w_gate)[:],
                                     start=True, stop=True)
                last.then_inc(logits_done, 1)

            def turn_gates(r):
                pe.wait_ge(gates_ready, r + 1)
                for c in range(NC):
                    last = pe.transpose(gatesT_ps[0:E, c * P:(c + 1) * P], gates[:, c, :], ident[:])
                last.then_inc(gates_turned, 1)

            rows.turn(pe, a_ps, ident, 0)
            if top1:
                reduce_rows(0)
            router(0)
            if not lora:
                turn_gates(0)
            with pe.Fori(0, batches) as b:
                pe.wait_ge(rows.xT_ready, b + 1)

                def hidden_tiles(g):
                    for k in range(K):
                        n = g * K + k
                        if n >= 2:
                            pe.wait_ge(hidden_ready, b * G * K + (n - 1))
                        pe.matmul(hidden_ps[n % 2][:], w1[:, n, :], rows.xT[:], start=True,
                                  stop=True).then_inc(hidden_done, 1)

                def outputs(g):
                    pe.wait_ge(hidden_ready, b * G * K + (g + 1) * K)
                    for e in range(g * PAIR, (g + 1) * PAIR):
                        pe.wait_ge(y_taken, b * E + (e + 1))
                        for c in range(NC):
                            for k in range(K):
                                last = pe.matmul(y_ps[e % 2][:, c * D:(c + 1) * D],
                                                 hidden[:, g % 2, k, c * P:(c + 1) * P],
                                                 w2[:, e * K + k, :], start=(k == 0), stop=(k == K - 1))
                        last.then_inc(y_done, 1)
                        if e == TURN:
                            rows.turn(pe, a_ps, ident, b + 1)
                        if top1 and e == TURN + 1:
                            reduce_rows(b + 1)
                        if e == (TURN + 2 if top1 else TURN + 1):
                            router(b + 1)

                hidden_tiles(0)
                hidden_tiles(1)
                outputs(0)
                if not lora:
                    pe.wait_ge(gatesT_ready, b + 1)
                hidden_tiles(2)
                if not lora:
                    for c in range(NC):
                        if capacity:
                            last = pe.transpose(router_ps[:, 64 + c * E:64 + (c + 1) * E],
                                                gatesT[:, c * P:(c + 1) * P], ident[0:E, 0:E])
                        else:
                            last = pe.matmul(extra_ps[:, c * D:(c + 1) * D], gatesT[:, c * P:(c + 1) * P], b2[:],
                                             start=True, stop=True)
                    last.then_inc(back_turned if capacity else bias_done, 1)
                outputs(1)
                for g in range(3, G):
                    hidden_tiles(g)
                    outputs(g - 1)
                outputs(G - 1)
                if not lora:
                    turn_gates(b + 1)


def grouped_attention_phase(nc, dram, tag, x_dram, s_dram, batches):
    G, S, W = 8, 8, 64
    R2 = S // 2
    U = R2 * G
    DV = D // S
    NP = R2 + S

    with nc.cleanup_on_exit(), ExitStack() as ctx:
        def sb(name, shape, dt=F32):
            return ctx.enter_context(nc.sbuf_tensor(f"{tag}_{name}", shape, dt))

        def sem(name):
            return nc.alloc_semaphore(f"{tag}_{name}")

        def ps(name):
            return ctx.enter_context(nc.psum_tensor(f"{tag}_{name}_ps", [P, 512], F32))

        rows = Rows(nc, ctx, tag, x_dram)
        ident = sb("ident", [P, P])
        wq, wk, wv = sb("wq", [D, S * W]), sb("wk", [D, S, 2, W]), sb("wv", [D, D])
        qT = sb("qT", [P, G, S, T // G])
        kT = sb("kT", [P, G, S, T // G])
        xT_twice = sb("xT_twice", [D, G, 2, T // G])
        v = sb("v", [P, R2, G, 32])
        probs = sb("probs", [P, 2, G, S, T // G])
        neg_max = sb("neg_max", [P, 3])
        col_sum = sb("col_sum", [P, U])
        inv_sum = sb("inv_sum", [P, U])
        outT = sb("outT", [P, 2, T])
        s_out = sb("s_out", [P, NC, D])
        scores_ps = [ps("scores0"), ps("scores1"), ps("scores2")]
        out_ps = [ps("out0"), ps("out1")]
        a_ps = ps("a")
        v_ps = [ps("v0"), ps("v1")]

        weights = sem("weights")
        pads = sem("pads")
        projected = sem("projected")
        q_kept, k_kept = sem("q_kept"), sem("k_kept")
        twice_ready = sem("twice_ready")
        v_projected, v_ready = sem("v_projected"), sem("v_ready")
        scores_ready, max_ready, probs_ready = sem("scores_ready"), sem("max_ready"), sem("probs_ready")
        scaled = sem("scaled")
        out_ready, outT_kept, out_turned = sem("out_ready"), sem("outT_kept"), sem("out_turned")
        o_taken = sem("o_taken")
        s_free, s_stored = sem("s_free"), sem("s_stored")
        dve_chain = sem("dve_chain")

        loads = [(ident[:], dram["ident"]), (wq[:], dram["L1_Mq"]), (wv[:], dram["L1_Mv"])]
        loads += [(wk[:, :, twice, :], dram["L1_Mk"].rearrange("d (s w) -> d s w", s=S)) for twice in range(2)]
        MOMENTS, NORMALISE, TURN = 8, 12, 14
        s_rows = s_dram.rearrange("b (c p) d -> b p c d", p=P)
        banks = scores_ps + [a_ps]

        def grouped(bank):
            return bank[:].rearrange("p (g t) -> p g t", g=G)

        block = ctx.enter_context(nc.Block())

        @block.sync
        def _(sp):
            for dst, src in loads:
                sp.dma_start(dst, src).then_inc(weights, 16)
            rows.load(sp, 0, 0)
            with sp.Fori(0, batches) as b:
                rows.load(sp, b + 1, (b + 1) % batches)
                sp.wait_ge(o_taken, b * 2 + 4)
                sp.dma_start(s_rows[b], s_out[:]).then_inc(s_stored, 16)
                sp.wait_ge(s_stored, b * 16 + 16)
                sp.sem_inc(s_free, 1)

        @block.gpsimd
        def _(pool):
            pool.sem_inc(s_free, 1)
            rows.root(pool, 0)
            with pool.Fori(0, batches) as b:
                rows.root(pool, b + 1)

        @block.scalar
        def _(act):
            def keep_twice(b):
                rows.keep_turned(act, a_ps, b)
                act.activation(xT_twice[:], grouped(a_ps).unsqueeze(2)
                               .to_broadcast([D, G, 2, T // G]), ACT.Copy).then_inc(twice_ready, 1)

            def keep_q(b, m):
                act.wait_ge(projected, b * NP + (3 * m + 1))
                bank = grouped(banks[3 * m % 4])
                act.activation(qT[0:W, :, 2 * m, :], bank[0:W], ACT.Copy, scale=1.0 / math.sqrt(W))
                act.activation(qT[W:P, :, 2 * m + 1, :], bank[W:P], ACT.Copy,
                               scale=1.0 / math.sqrt(W)).then_inc(q_kept, 1)

            keep_twice(0)
            act.wait_ge(pads, 1)
            for m in range(R2):
                keep_q(0, m)
            with act.Fori(0, batches) as b:
                for u in range(U):
                    r, g = divmod(u, G)
                    act.wait_ge(max_ready, b * U + (u + 1))
                    if g == 0 and r >= 2:
                        act.wait_ge(out_ready, b * R2 + (r - 1))
                    act.activation(probs[:, r % 2, g].rearrange("p s t -> p (s t)"), scores_ps[u % 3][:], ACT.Exp,
                                   bias=neg_max[:, u % 3:u % 3 + 1],
                                   accum_out=col_sum[:, u:u + 1]).then_inc(probs_ready, 1)
                    if u == TURN:
                        act.wait_ge(v_projected, b + 1)
                        keep_twice(b + 1)
                keep_q(b + 1, 0)
                keep_q(b + 1, 1)
                act.wait_ge(out_ready, b * R2 + R2)
                act.activation(outT[:, 0, :], out_ps[0][:], ACT.Copy).then_inc(outT_kept, 1)
                keep_q(b + 1, 2)
                keep_q(b + 1, 3)

        @block.vector
        def _(dve):
            chain = Chain(dve, dve_chain)
            rows.before_loop(dve)
            dve.memset(v[:], 0.0)
            chain(dve.memset(qT[:], 0.0))
            dve.sem_inc(pads, 1)
            dve.sem_inc(o_taken, 2)

            def keep_k(b, n):
                j = 3 * (n // 2) + 1 + n % 2
                dve.wait_ge(projected, b * NP + (j + 1))
                dve.tensor_copy(kT[:, :, n, :], grouped(banks[j % 4])).then_inc(k_kept, 1)

            rows.moments_of(dve, chain, 0)
            rows.normalise(dve, 0)
            for n in range(S):
                keep_k(0, n)
            with dve.Fori(0, batches) as b:
                chain.restart()

                def keep_v():
                    dve.wait_ge(v_projected, b + 1)
                    for half in range(2):
                        for n in range(2):
                            lo = half * 64
                            src = v_ps[n][lo:lo + 64, :].rearrange("p (g r two d) -> p r g two d", g=4, r=R2, two=2)
                            dve.tensor_copy(v[lo:lo + 64, :, n * 4:n * 4 + 4, 0:DV],
                                            src[:, :, :, half, :]).then_inc(v_ready, 1)

                def col_max(u):
                    dve.wait_ge(scores_ready, b * U + (u + 1))
                    if u >= 3:
                        dve.wait_ge(probs_ready, b * U + (u - 2))
                    dve.tensor_reduce(neg_max[:, u % 3:u % 3 + 1], scores_ps[u % 3][:], AX.X, ALU.max,
                                      negate=True).then_inc(max_ready, 1)

                def divide(u):
                    r, g = divmod(u, G)
                    dve.wait_ge(probs_ready, b * U + (u + 1))
                    chain(dve.reciprocal(inv_sum[:, u:u + 1], col_sum[:, u:u + 1]))
                    unit = probs[:, r % 2, g].rearrange("p s t -> p (s t)")
                    dve.tensor_scalar(unit, unit, inv_sum[:, u:u + 1], None, ALU.mult).then_inc(scaled, 1)

                for i in range(U + 2):
                    if i < U:
                        col_max(i)
                    if i >= 2:
                        divide(i - 2)
                    if i == 4:
                        keep_v()
                    if i == MOMENTS:
                        rows.moments_of(dve, chain, b + 1)
                    if i == NORMALISE:
                        rows.normalise(dve, b + 1)
                for n in range(4):
                    keep_k(b + 1, n)
                dve.wait_ge(out_ready, b * R2 + R2)
                dve.tensor_copy(outT[:, 1, :], out_ps[1][:]).then_inc(outT_kept, 1)
                for n in range(4, S):
                    keep_k(b + 1, n)
                dve.wait_ge(out_turned, b + 1)
                dve.wait_ge(s_free, b + 1)
                for n in range(2):
                    dve.tensor_copy(s_out[:, :, n * 64:(n + 1) * 64].rearrange("p c (s d) -> p c s d", s=4),
                                    v_ps[n][:].rearrange("p (c s d) -> p c s d", c=NC, s=4)[:, :, :, 0:DV]
                                    ).then_inc(o_taken, 1)

        @block.tensor
        def _(pe):
            pe.wait_ge(weights, 16 * len(loads))

            def project(b, n):
                m, kind = divmod(n, 3)
                if n == 3:
                    pe.wait_ge(twice_ready, b + 1)
                if n >= 4:
                    mm, kk = divmod(n - 4, 3)
                    if kk == 0:
                        pe.wait_ge(q_kept, b * R2 + (mm + 1))
                    else:
                        pe.wait_ge(k_kept, b * S + (2 * mm + kk))
                lhsT = wq[:, 2 * m * W:2 * (m + 1) * W] if kind == 0 else \
                    wk[:, 2 * m + kind - 1].rearrange("d a w -> d (a w)")
                pe.matmul(banks[n % 4][:], lhsT, rows.xT[:], start=True, stop=True).then_inc(projected, 1)

            rows.turn(pe, a_ps, ident, 0)
            pe.wait_ge(rows.xT_ready, 1)
            for n in range(NP):
                project(0, n)
            with pe.Fori(0, batches) as b:
                pe.wait_ge(q_kept, b * R2 + R2)
                pe.wait_ge(k_kept, b * S + S)

                def scores(u):
                    r, g = divmod(u, G)
                    if u >= 3:
                        pe.wait_ge(probs_ready, b * U + (u - 2))
                    pe.matmul(scores_ps[u % 3][:], kT[:, g, 2 * r:2 * r + 2, :].rearrange("p a t -> p (a t)"),
                              qT[:, g, :, :].rearrange("p s t -> p (s t)"), start=True,
                              stop=True).then_inc(scores_ready, 1)

                def project_v():
                    pe.wait_ge(o_taken, b * 2 + 2)
                    for g in range(G):
                        last = pe.matmul(v_ps[g // 4][:, (g % 4) * D:(g % 4 + 1) * D],
                                         xT_twice[:, g, :, :].rearrange("p a t -> p (a t)"), wv[:],
                                         start=True, stop=True)
                    last.then_inc(v_projected, 1)

                def products(r, four):
                    if four == 0:
                        pe.wait_ge(scaled, b * U + (r + 1) * G)
                        if r == 0:
                            pe.wait_ge(v_ready, b * 4 + 4)
                    for k in range(4):
                        n = 4 * four + k
                        last = pe.matmul(out_ps[four][32 * k:32 * k + 32, :], v[:, r, n, :],
                                         probs[:, r % 2, :, n, :], start=(r == 0), stop=(r == R2 - 1))
                    if four == 1:
                        last.then_inc(out_ready, 1)

                for i in range(U):
                    scores(i)
                    if i == 2:
                        project_v()
                    if i >= G + 3 and i % G in (3, 5):
                        products(i // G - 1, (i % G - 3) // 2)
                    if i == TURN:
                        rows.turn(pe, a_ps, ident, b + 1)
                pe.wait_ge(probs_ready, b * U + U)
                pe.wait_ge(rows.xT_ready, b + 2)
                for n in range(6):
                    project(b + 1, n)
                products(R2 - 1, 0)
                products(R2 - 1, 1)
                for n in range(6, NP):
                    project(b + 1, n)
                pe.wait_ge(outT_kept, b * 2 + 2)
                for n in range(2):
                    for c in range(NC):
                        last = pe.transpose(v_ps[n][:, c * P:(c + 1) * P], outT[:, n, c * P:(c + 1) * P], ident[:])
                last.then_inc(out_turned, 1)


def local_transformer_phase(nc, dram, tag, x_dram, s_dram, out_dram, batches):
    L, H, W = 2, 8, 64
    HP = H // 2
    HID = 341
    HK = [128, 128, 85]
    N_ROT = 2 * NC
    N_PAIR = NC * HP
    KEYS = P + W

    with nc.cleanup_on_exit(), ExitStack() as ctx:
        def sb(name, shape, dt=F32):
            return ctx.enter_context(nc.sbuf_tensor(f"{tag}_{name}", shape, dt))

        def sem(name):
            return nc.alloc_semaphore(f"{tag}_{name}")

        def ps(name):
            return ctx.enter_context(nc.psum_tensor(f"{tag}_{name}_ps", [P, 512], F32))

        rows = Rows(nc, ctx, tag, x_dram)
        gate = Gate(nc, ctx, tag, x_dram, s_dram, out_dram)
        x = gate.y
        ident, ident16 = sb("ident", [P, P]), sb("ident16", [P, P], BF16)
        band16, band = sb("band16", [P, KEYS], BF16), sb("band", [P, KEYS])
        rotary = sb("rotary", [P, 4, NC, W])
        scale = sb("scale", [P, 2, L, W])
        turnings = sb("turnings", [P, L, 2, 2, NC, W])
        w_qkv = sb("w_qkv", [D, L, 3 * H * W])
        w_o = sb("w_o", [P, L, 4, D])
        ln_g, ln_b = sb("ln_g", [D, L]), sb("ln_b", [D, L])
        w1, w2 = sb("w1", [D, L, 2 * HID]), sb("w2", [P, L, 3, D])
        b1, b2 = sb("b1", [P, L, 2, 3]), sb("b2", [P, L, D])
        hT = sb("hT", [D, T])
        hnT = sb("hnT", [D, T])
        squares = sb("squares", [P, 2, T])
        sums = sb("sums", [P, 2, H])
        norms = sb("norms", [P, 2, H])
        q_norms = sb("q_norms", [P, NC, H])
        neg_half = sb("neg_half", [P, H])
        cos_part, sin_part = sb("cos_part", [P, 2, T]), sb("sin_part", [P, 2, T])
        turned_rows = sb("turned_rows", [P, 2, T])
        qT, kT = sb("qT", [P, 2, HP, T]), sb("kT", [P, HP, T])
        v = sb("v", [P, NC, H * W])
        probs = sb("probs", [P, 3, 2, 2 * P])
        probsT = sb("probsT", [P, 2, 4 * P])
        row_max, neg_max = sb("row_max", [P, 3, 2]), sb("neg_max", [P, 3, 2])
        row_sum, inv_sum = sb("row_sum", [P, NC * H]), sb("inv_sum", [P, NC * H])
        neg_one = sb("neg_one", [P, 2])
        oT = sb("oT", [P, 2, 4, P])
        stats, moments = sb("lstats", [P, NC, 6]), sb("lmoments", [P, NC, 2])
        var_eps, rstd = sb("lvar_eps", [P, NC]), sb("lrstd", [P, NC])
        hn = sb("hn", [P, NC, D])
        gelu = sb("gelu", [P, 2, T])
        mixed = sb("mixed", [P, 3, T])
        a_ps, b_ps = ps("a"), ps("b")
        s_ps, t_ps, o_ps = [ps("s0"), ps("s1")], [ps("t0"), ps("t1")], [ps("o0"), ps("o1")]
        score_banks = [s_ps[0], s_ps[1], a_ps]
        qkv_banks = [[o_ps[0], o_ps[1]], [s_ps[0], s_ps[1], o_ps[0], o_ps[1]]]
        up_banks = [[t_ps[0], s_ps[0], t_ps[1], s_ps[1]], [s_ps[0], s_ps[1], a_ps]]

        weights = sem("weights")
        tables = sem("tables")
        x_ready = sem("x_ready")
        x_turned, hT_ready = sem("x_turned"), sem("hT_ready")
        qkv_done = sem("qkv_done")
        k_rotated = sem("k_rotated")
        squares_ready, sums_ready, rotated = sem("squares_ready"), sem("sums_ready"), sem("rotated")
        rows_turned, rowsT_kept = sem("rows_turned"), sem("rowsT_kept")
        v_kept = sem("v_kept")
        scores_ready, max_ready, probs_ready = sem("scores_ready"), sem("max_ready"), sem("probs_ready")
        probs_scaled = sem("probs_scaled")
        probs_turned, probsT_ready, out_ready = sem("probs_turned"), sem("probsT_ready"), sem("out_ready")
        oT_ready = sem("oT_ready")
        wo_done = sem("wo_done")
        h_back, lvar_ready, lrstd_ready = sem("h_back"), sem("lvar_ready"), sem("lrstd_ready")
        hn_ready, hn_turned, hnT_ready = sem("hn_ready"), sem("hn_turned"), sem("hnT_ready")
        up_done, gelu_ready, mixed_ready = sem("up_done"), sem("gelu_ready"), sem("mixed_ready")
        down_done = sem("down_done")
        pads = sem("pads")
        dve_chain, pool_chain = sem("dve_chain"), sem("pool_chain")

        loads = [(ident[:], dram["ident"]), (band[:], dram["band"]),
                 (rotary[:], dram["L1_rotary"]), (scale[:, 0], dram["L1_q_scale"].partition_broadcast(P)),
                 (scale[:, 1], dram["L1_k_scale"].partition_broadcast(P)),
                 (b2[:], dram["L1_b2"].partition_broadcast(P))]
        for l in range(L):
            loads += [(w_qkv[:, l, :], dram["L1_wqkv"][l]), (w_o[:, l], dram["L1_wo"][l]),
                      (ln_g[:, l:l + 1], dram["L1_ln_g"][l]), (ln_b[:, l:l + 1], dram["L1_ln_b"][l]),
                      (w1[:, l, :], dram["L1_w1"][l])]
            for k, n in enumerate(HK):
                loads += [(w2[0:n, l, k, :], dram["L1_w2"][l, k * P:k * P + n, :])]
                for half in range(2):
                    loads += [(b1[0:n, l, half, k:k + 1],
                               dram["L1_b1"][l, half * HID + k * P:half * HID + k * P + n, :])]

        def heads(ap):
            return ap.rearrange("p (h w) -> p h w", h=H)

        block = ctx.enter_context(nc.Block())

        @block.sync
        def _(sp):
            for dst, src in loads:
                sp.dma_start(dst, src).then_inc(weights, 16)
            rows.load(sp, 0, 0)
            with sp.Fori(0, batches) as b:
                gate.load(sp, b)
                rows.load(sp, b + 1, (b + 1) % batches)
                gate.store(sp, b)

        @block.gpsimd
        def _(pool):
            gate.before_loop(pool)
            chain = Chain(pool, pool_chain)
            pool.wait_ge(pads, 1)

            def rotate_rows(b, l):
                for n in range(N_ROT):
                    pool.wait_ge(sums_ready, b * L * N_ROT + (l * N_ROT + n + 1))
                    if n % 2 == 0:
                        pool.tensor_tensor(q_norms[:, n // 2, :], sums[:, n % 2, :], neg_half[:], ALU.pow)
                        if n >= 2:
                            pool.wait_ge(rows_turned, b * L * N_ROT + (l * N_ROT + n - 1))
                        pool.tensor_tensor(turned_rows[:, n % 2, :], cos_part[:, n % 2, :],
                                           sin_part[:, n % 2, :], ALU.add).then_inc(rotated, 1)
                        continue
                    chain(pool.tensor_tensor(norms[:, n % 2, :], sums[:, n % 2, :], neg_half[:], ALU.pow))
                    pool.wait_ge(k_rotated, b * L * NC + (l * NC + n // 2 + 1))
                    if n >= 2:
                        pool.wait_ge(rows_turned, b * L * N_ROT + (l * N_ROT + n - 1))
                    pool.tensor_tensor(heads(turned_rows[:, n % 2, :]), heads(cos_part[:, n % 2, :]),
                                       norms[:, n % 2, :].unsqueeze(2).to_broadcast([P, H, W]),
                                       ALU.mult).then_inc(rotated, 1)

            rows.root(pool, 0)
            rotate_rows(0, 0)
            with pool.Fori(0, batches) as b:
                chain.restart()
                for l in range(L):
                    if l:
                        rotate_rows(b, l)
                    for i in range(N_PAIR):
                        lo = P if i // HP == 0 else W
                        pool.wait_ge(probs_ready, b * L * N_PAIR + (l * N_PAIR + i + 1))
                        p = probs[:, i % 3, :, lo:2 * P]
                        s = inv_sum[:, 2 * i:2 * i + 2]
                        chain(pool.tensor_tensor(s, row_sum[:, 2 * i:2 * i + 2], neg_one[:], ALU.pow))
                        pool.tensor_tensor(p, p, s.unsqueeze(2).to_broadcast([P, 2, 2 * P - lo]),
                                           ALU.mult).then_inc(probs_scaled, 1)
                        if l == L - 1 and i == 8:
                            rows.root(pool, b + 1)
                    pool.wait_ge(lvar_ready, b * L + (l + 1))
                    pool.tensor_tensor(rstd[:], var_eps[:], neg_half[:, 0:NC], ALU.pow).then_inc(lrstd_ready, 1)
                rotate_rows(b + 1, 0)

        @block.scalar
        def _(act):
            act.wait_ge(weights, 16 * len(loads))
            act.wait_ge(pads, 1)

            def shift(src):
                act.activation(hT[0:W, :], src[0:W, :], ACT.Copy)
                return act.activation(hT[W:D, 1:T], src[W:D, 0:T - 1], ACT.Copy)

            def first(b, l, j):
                c, kind = divmod(j, 3)
                bank = qkv_banks[l][j % len(qkv_banks[l])]
                act.wait_ge(qkv_done, b * L * 3 * NC + (l * 3 * NC + j + 1))
                if kind < 2:
                    n = 2 * c + kind
                    if n >= 2:
                        act.wait_ge(sums_ready, b * L * N_ROT + (l * N_ROT + n - 1))
                    act.activation(squares[:, n % 2, :], bank[:], ACT.Square).then_inc(squares_ready, 1)
                else:
                    act.activation(v[:, c, :], bank[:], ACT.Copy).then_inc(v_kept, 1)

            def keep(b, l, j):
                c, kind = divmod(j, 3)
                if kind < 2:
                    n = 2 * c + kind
                    act.wait_ge(rows_turned, b * L * N_ROT + (l * N_ROT + n + 1))
                    turned = t_ps[n % 2][:].rearrange("p (h t) -> p h t", h=HP)
                    if kind == 0:
                        act.activation(qT[0:W, 0, :, c * P:(c + 1) * P], turned[0:W], ACT.Copy)
                        last = act.activation(qT[W:P, 1, :, c * P:(c + 1) * P], turned[W:P], ACT.Copy)
                    else:
                        last = act.activation(kT[:, :, c * P:(c + 1) * P], turned, ACT.Copy)
                    last.then_inc(rowsT_kept, 1)

            def project_slot(b, l, i):
                if i < 3 * NC:
                    first(b, l, i)
                if i >= 4:
                    keep(b, l, i - 4)

            def gelu_tile(b, l, k):
                m = HK[k]
                act.wait_ge(up_done, b * L * 3 + (l * 3 + k + 1))
                if k >= 2:
                    act.wait_ge(mixed_ready, b * L * 3 + (l * 3 + k - 1))
                act.activation(gelu[0:m, k % 2, :], up_banks[l][(2 * k + 1) % len(up_banks[l])][0:m, :], ACT.Gelu,
                               bias=b1[0:m, l, 1, k:k + 1]).then_inc(gelu_ready, 1)

            act.wait_ge(x_turned, 1)
            shift(t_ps[0]).then_inc(hT_ready, 1)
            for i in range(3 * NC + 4):
                project_slot(0, 0, i)
            with act.Fori(0, batches) as b:
                for l in range(L):
                    if l:
                        act.wait_ge(x_turned, b * 2 * L + (2 * l + 1))
                        shift(a_ps).then_inc(hT_ready, 1)

                    if l:
                        for i in range(3 * NC + 4):
                            project_slot(b, l, i)

                    def exps(i):
                        c = i // HP
                        lo = 0 if c else W
                        act.wait_ge(max_ready, b * L * N_PAIR + (l * N_PAIR + i + 1))
                        if i >= 3:
                            act.wait_ge(probs_turned, b * L * N_PAIR + (l * N_PAIR + i - 2))
                        for hh in range(2):
                            h = (i % HP) * 2 + hh
                            last = act.activation(probs[:, i % 3, hh, W + lo:2 * P],
                                                  score_banks[i % 3][:, hh * KEYS + lo:(hh + 1) * KEYS], ACT.Exp,
                                                  bias=neg_max[:, i % 3, hh:hh + 1],
                                                  scale=q_norms[:, c, h:h + 1],
                                                  accum_out=row_sum[:, c * H + h:c * H + h + 1])
                        last.then_inc(probs_ready, 1)

                    def keep_oT(c):
                        act.wait_ge(out_ready, b * L * N_PAIR + (l * N_PAIR + (c + 1) * HP))
                        if c >= 2:
                            act.wait_ge(wo_done, b * L * NC + (l * NC + c - 1))
                        act.activation(oT[:, c % 2].rearrange("p k t -> p (k t)"), o_ps[c % 2][:],
                                       ACT.Copy).then_inc(oT_ready, 1)

                    for i in range(N_PAIR + 4):
                        if i < N_PAIR:
                            exps(i)
                        if i >= 7 and i % HP == 3:
                            keep_oT((i - 7) // HP)
                    act.wait_ge(x_turned, b * 2 * L + (2 * l + 2))
                    shift(a_ps).then_inc(hT_ready, 1)
                    if l < L - 1:
                        for k in range(3):
                            gelu_tile(b, l, k)
                act.wait_ge(h_back, b * L + L)
                act.wait_ge(x_turned, b * 2 * L + (2 * L + 1))
                shift(t_ps[0]).then_inc(hT_ready, 1)
                for i in range(3 * NC + 4):
                    project_slot(b + 1, 0, i)
                    if i in (3, 5, 7):
                        gelu_tile(b, L - 1, (i - 3) // 2)
                    if i == 9:
                        gate.exp(act, b)

        @block.vector
        def _(dve):
            chain = Chain(dve, dve_chain)
            rows.before_loop(dve)
            dve.memset(neg_half[:], -0.5)
            dve.memset(neg_one[:], -1.0)
            dve.memset(hT[W:D, 0:1], 0.0)
            dve.memset(qT[:], 0.0)
            chain(dve.memset(probs[:], 0.0))
            dve.sem_inc(pads, 1)
            dve.wait_ge(weights, 16 * len(loads))
            for l in range(L):
                for kind in range(2):
                    s = scale[:, kind, l, :].unsqueeze(1)
                    HW = W // 2
                    t = turnings[:, l, kind]
                    dve.tensor_tensor(t[:, 0], rotary[:, 2 * kind], s.to_broadcast([P, NC, W]), ALU.mult)
                    for dst, src in ((0, HW), (HW, 0)):
                        last = dve.tensor_tensor(t[:, 1, :, dst:dst + HW], rotary[:, 2 * kind + 1, :, dst:dst + HW],
                                                 s[:, :, src:src + HW].to_broadcast([P, NC, HW]), ALU.mult)
            chain(last)
            dve.tensor_copy(ident16[:], ident[:]).then_inc(tables, 1)
            dve.tensor_copy(band16[:], band[:]).then_inc(tables, 1)

            def rotate(b, l, n):
                c, kind = divmod(n, 2)
                j = 3 * c + kind
                bank = heads(qkv_banks[l][j % len(qkv_banks[l])][:])
                t = turnings[:, l, kind]
                HW = W // 2
                dve.wait_ge(squares_ready, b * L * N_ROT + (l * N_ROT + n + 1))
                if n >= 2:
                    dve.wait_ge(rotated, b * L * N_ROT + (l * N_ROT + n - 1))
                dve.tensor_tensor(heads(cos_part[:, n % 2, :]), bank,
                                  t[:, 0, c, :].unsqueeze(1).to_broadcast([P, H, W]), ALU.mult)
                for dst, src in ((0, HW), (HW, 0)):
                    dve.tensor_tensor(heads(sin_part[:, n % 2, :])[:, :, dst:dst + HW],
                                      bank[:, :, src:src + HW],
                                      t[:, 1, c, dst:dst + HW].unsqueeze(1).to_broadcast([P, H, HW]),
                                      ALU.mult)
                chain(dve.tensor_reduce(sums[:, n % 2, :], heads(squares[:, n % 2, :]), AX.X, ALU.add))
                dve.tensor_scalar(sums[:, n % 2, :], sums[:, n % 2, :], 1e-24, None,
                                  ALU.max).then_inc(sums_ready, 1)
                if kind:
                    dve.tensor_tensor(cos_part[:, n % 2, :], cos_part[:, n % 2, :],
                                      sin_part[:, n % 2, :], ALU.add).then_inc(k_rotated, 1)

            def mix(b, l, k):
                m = HK[k]
                dve.wait_ge(gelu_ready, b * L * 3 + (l * 3 + k + 1))
                dve.scalar_tensor_tensor(mixed[0:m, k, :], up_banks[l][2 * k % len(up_banks[l])][0:m, :],
                                         b1[0:m, l, 0, k:k + 1], gelu[0:m, k % 2, :], ALU.add,
                                         ALU.mult).then_inc(mixed_ready, 1)

            def add_down(b, l):
                dve.wait_ge(down_done, b * L + (l + 1))
                chain(dve.tensor_tensor(x[:], x[:], b_ps[:].rearrange("p (c d) -> p c d", c=NC), ALU.add))

            rows.moments_of(dve, chain, 0)
            rows.normalise(dve, 0)
            for n in range(N_ROT):
                rotate(0, 0, n)
            with dve.Fori(0, batches) as b:
                chain.restart()
                for l in range(L):
                    if l:
                        for n in range(N_ROT):
                            rotate(b, l, n)

                    def pair_max(i):
                        lo = 0 if i // HP else W
                        dve.wait_ge(scores_ready, b * L * N_PAIR + (l * N_PAIR + i + 1))
                        src = score_banks[i % 3][:, 0:2 * KEYS].rearrange("p (a k) -> p a k", a=2)
                        chain(dve.tensor_reduce(row_max[:, i % 3, :], src[:, :, lo:KEYS], AX.X, ALU.max, negate=True))
                        if i >= 3:
                            dve.wait_ge(probs_ready, b * L * N_PAIR + (l * N_PAIR + i - 2))
                        c, hp = divmod(i, HP)
                        dve.tensor_tensor(neg_max[:, i % 3, :], row_max[:, i % 3, :],
                                          q_norms[:, c, 2 * hp:2 * hp + 2], ALU.mult).then_inc(max_ready, 1)

                    def keep_probsT(i):
                        n = 4 * P if i // HP else 2 * P
                        dve.wait_ge(probs_turned, b * L * N_PAIR + (l * N_PAIR + i + 1))
                        if i >= 2:
                            dve.wait_ge(out_ready, b * L * N_PAIR + (l * N_PAIR + i - 1))
                        dve.tensor_copy(probsT[:, i % 2, 0:n], t_ps[i % 2][:, 0:n]).then_inc(probsT_ready, 1)

                    for i in range(N_PAIR + 2):
                        if i < N_PAIR:
                            pair_max(i)
                        if i >= 2:
                            keep_probsT(i - 2)
                        if l == L - 1 and i == 6:
                            rows.moments_of(dve, chain, b + 1)
                        if l == L - 1 and i == 10:
                            rows.normalise(dve, b + 1)
                    dve.wait_ge(wo_done, b * L * NC + (l + 1) * NC)
                    chain(dve.tensor_tensor(x[:], x[:] if l else rows.xn[:], b_ps[:].rearrange("p (c d) -> p c d", c=NC), ALU.add))
                    dve.sem_inc(x_ready, 1)

                    dve.wait_ge(h_back, b * L + (l + 1))
                    for c in range(NC):
                        last = dve.bn_stats(stats[:, c, :], b_ps[:, c * D:(c + 1) * D])
                    chain(last)
                    for c in range(NC):
                        last = dve.bn_aggr(moments[:, c, :], stats[:, c, :])
                    chain(last)
                    dve.tensor_scalar(var_eps[:], moments[:, :, 1], EPS, None, ALU.add).then_inc(lvar_ready, 1)
                    dve.wait_ge(lrstd_ready, b * L + (l + 1))
                    for c in range(NC):
                        last = dve.tensor_scalar(hn[:, c, :], b_ps[:, c * D:(c + 1) * D], moments[:, c, 0:1],
                                                 rstd[:, c:c + 1], ALU.subtract, ALU.mult)
                    last.then_inc(hn_ready, 1)
                    if l == L - 1:
                        rotate(b + 1, 0, 0)
                    dve.wait_ge(hn_turned, b * L + (l + 1))
                    dve.tensor_scalar(hnT[:], a_ps[:], ln_g[:, l:l + 1], ln_b[:, l:l + 1], ALU.mult,
                                      ALU.add).then_inc(hnT_ready, 1)
                    chain(dve.tensor_tensor(x[:], x[:], b2[:, l:l + 1, :].to_broadcast([P, NC, D]), ALU.add))
                    if l < L - 1:
                        for k in range(3):
                            mix(b, l, k)
                        add_down(b, l)
                        dve.sem_inc(x_ready, 1)
                rotate(b + 1, 0, 1)
                for k in range(3):
                    rotate(b + 1, 0, k + 2)
                    mix(b, L - 1, k)
                rotate(b + 1, 0, 5)
                add_down(b, L - 1)
                gate.finish_first(dve, b)
                for n in range(6, N_ROT):
                    rotate(b + 1, 0, n)
                gate.finish_rest(dve, chain, b)

        @block.tensor
        def _(pe):
            pe.wait_ge(weights, 16 * len(loads))
            pe.wait_ge(tables, 2)

            def turn(src):
                for c in range(NC):
                    last = pe.transpose(a_ps[:, c * P:(c + 1) * P], src[:, c, :], ident[:])
                return last

            def turn_first(b):
                pe.wait_ge(rows.xn_ready, b * NC + NC)
                for c in range(NC):
                    last = pe.transpose(t_ps[0][:, c * P:(c + 1) * P], rows.xn[:, c, :], ident[:])
                last.then_inc(x_turned, 1)

            def project(b, l, j):
                ring = qkv_banks[l]
                c, kind = divmod(j, 3)
                if j >= len(ring):
                    cc, kk = divmod(j - len(ring), 3)
                    if kk < 2:
                        pe.wait_ge(sums_ready, b * L * N_ROT + (l * N_ROT + 2 * cc + kk + 1))
                    else:
                        pe.wait_ge(v_kept, b * L * NC + (l * NC + cc + 1))
                pe.matmul(ring[j % len(ring)][:], hT[:, c * P:(c + 1) * P],
                          w_qkv[:, l, kind * H * W:(kind + 1) * H * W], start=True,
                          stop=True).then_inc(qkv_done, 1)

            def turn_rows(b, l, j):
                c, kind = divmod(j, 3)
                if kind < 2:
                    n = 2 * c + kind
                    pe.wait_ge(rotated, b * L * N_ROT + (l * N_ROT + n + 1))
                    if n >= 2:
                        pe.wait_ge(rowsT_kept, b * L * N_ROT + (l * N_ROT + n - 1))
                    for k in range(HP):
                        last = pe.transpose(t_ps[n % 2][:, k * P:(k + 1) * P],
                                            turned_rows[:, n % 2, k * P:(k + 1) * P], ident[:])
                    last.then_inc(rows_turned, 1)

            def project_slot(b, l, i):
                if i < 3 * NC:
                    project(b, l, i)
                if i >= 4:
                    turn_rows(b, l, i - 4)

            def up(b, l, k):
                m, ring = HK[k], up_banks[l]
                for j in (2 * k, 2 * k + 1):
                    if j >= len(ring):
                        before = j - len(ring)
                        pe.wait_ge(gelu_ready if before % 2 else mixed_ready, b * L * 3 + (l * 3 + before // 2 + 1))
                    first = (j % 2) * HID + k * P
                    last = pe.matmul(ring[j % len(ring)][0:m, :], w1[:, l, first:first + m], hnT[:], start=True,
                                     stop=True)
                last.then_inc(up_done, 1)

            def down(b, l):
                pe.wait_ge(mixed_ready, b * L * 3 + (l + 1) * 3)
                for c in range(NC):
                    for k, m in enumerate(HK):
                        last = pe.matmul(b_ps[:, c * D:(c + 1) * D], mixed[0:m, k, c * P:(c + 1) * P],
                                         w2[0:m, l, k, :], start=(k == 0), stop=(k == 2))
                last.then_inc(down_done, 1)

            turn_first(0)
            pe.wait_ge(hT_ready, 1)
            for i in range(3 * NC + 4):
                project_slot(0, 0, i)
            with pe.Fori(0, batches) as b:
                for l in range(L):
                    if l:
                        pe.wait_ge(x_ready, b * (2 * L - 1) + 2 * l)
                        turn(x).then_inc(x_turned, 1)
                        pe.wait_ge(hT_ready, b * 2 * L + (2 * l + 1))
                        for i in range(3 * NC + 4):
                            project_slot(b, l, i)
                    pe.wait_ge(rowsT_kept, b * L * N_ROT + (l + 1) * N_ROT)
                    pe.wait_ge(v_kept, b * L * NC + (l + 1) * NC)

                    def scores(i):
                        c, hp = divmod(i, HP)
                        lo = 0 if c else W
                        if i >= 3:
                            pe.wait_ge(probs_ready, b * L * N_PAIR + (l * N_PAIR + i - 2))
                        for hh in range(2):
                            dst = score_banks[i % 3][:, hh * KEYS + lo:(hh + 1) * KEYS]
                            pe.matmul(dst, ident16[:], band16[:, lo:KEYS], start=True, stop=False)
                            last = pe.matmul(dst, qT[:, hh, hp, c * P:(c + 1) * P],
                                             kT[:, hp, c * P - W + lo:(c + 1) * P], start=False, stop=True)
                        last.then_inc(scores_ready, 1)

                    def turn_probs(i):
                        c = i // HP
                        pe.wait_ge(probs_scaled, b * L * N_PAIR + (l * N_PAIR + i + 1))
                        if i >= 2:
                            pe.wait_ge(probsT_ready, b * L * N_PAIR + (l * N_PAIR + i - 1))
                        n = 0
                        for hh in range(2):
                            for part in ((0, 1) if c else (1,)):
                                last = pe.transpose(t_ps[i % 2][:, n * P:(n + 1) * P],
                                                    probs[:, i % 3, hh, part * P:(part + 1) * P], ident[:])
                                n += 1
                        last.then_inc(probs_turned, 1)

                    def products(i):
                        c, hp = divmod(i, HP)
                        pe.wait_ge(probsT_ready, b * L * N_PAIR + (l * N_PAIR + i + 1))
                        if hp == 0 and c >= 2:
                            pe.wait_ge(oT_ready, b * L * NC + (l * NC + c - 1))
                        parts = (c - 1, c) if c else (c,)
                        for n, cc in enumerate(parts):
                            for hh in range(2):
                                h, at = 2 * hp + hh, hh * len(parts) + n
                                last = pe.matmul(o_ps[c % 2][hh * W:(hh + 1) * W, hp * P:(hp + 1) * P],
                                                 v[:, cc, h * W:(h + 1) * W], probsT[:, i % 2, at * P:(at + 1) * P],
                                                 start=(cc == parts[0]), stop=(cc == c))
                        last.then_inc(out_ready, 1)

                    def project_o(c):
                        pe.wait_ge(oT_ready, b * L * NC + (l * NC + c + 1))
                        for k in range(4):
                            last = pe.matmul(b_ps[:, c * D:(c + 1) * D], oT[:, c % 2, k, :], w_o[:, l, k, :],
                                             start=(k == 0), stop=(k == 3))
                        last.then_inc(wo_done, 1)

                    for i in range(N_PAIR + 5):
                        if i < N_PAIR:
                            scores(i)
                        if 2 <= i <= N_PAIR + 1:
                            turn_probs(i - 2)
                        if 3 <= i <= N_PAIR + 2:
                            products(i - 3)
                        if i >= 8 and i % HP == 0:
                            project_o((i - 8) // HP)

                    pe.wait_ge(x_ready, b * (2 * L - 1) + (2 * l + 1))
                    turn(x).then_inc(x_turned, 1)
                    pe.wait_ge(hT_ready, b * 2 * L + (2 * l + 2))
                    for c in range(NC):
                        last = pe.transpose(b_ps[:, c * D:(c + 1) * D], hT[:, c * P:(c + 1) * P], ident[:])
                    last.then_inc(h_back, 1)
                    if l == L - 1:
                        turn_first(b + 1)
                        pe.wait_ge(hT_ready, b * 2 * L + (2 * L + 1))
                        project_slot(b + 1, 0, 0)
                        project_slot(b + 1, 0, 1)
                    pe.wait_ge(hn_ready, b * L + (l + 1))
                    turn(hn).then_inc(hn_turned, 1)
                    if l == L - 1:
                        project_slot(b + 1, 0, 2)
                        project_slot(b + 1, 0, 3)
                    pe.wait_ge(hnT_ready, b * L + (l + 1))
                    if l < L - 1:
                        for k in range(3):
                            up(b, l, k)
                        down(b, l)
                for k in range(3):
                    up(b, L - 1, k)
                    if k < 2:
                        project_slot(b + 1, 0, 4 + 2 * k)
                        project_slot(b + 1, 0, 5 + 2 * k)
                down(b, L - 1)
                for i in range(8, 3 * NC + 4):
                    project_slot(b + 1, 0, i)


def constants():
    out = {}
    out["ident"] = np.eye(P, dtype=np.float32)
    i, j = np.arange(P)[:, None], np.arange(P)[None, :]
    out["causal"] = np.where(j > i, NEG_BIG, 0.0).astype(np.float32)
    tok = np.arange(T).reshape(NC, P).T
    out["keep_triu"] = (np.arange(T)[None, None, :] >= tok[:, :, None]).astype(np.float32)
    out["rank"] = np.broadcast_to(8.0 - np.arange(8), (P, NC, 8)).astype(np.float32).copy()
    f = np.arange(D)
    out["L0_head_scale"] = ((f[:, None] // 8 == np.arange(16)[None, :]) / math.sqrt(8)).astype(np.float32)
    inv = 1.0 / 10000.0 ** (np.arange(0, 8, 2) / 8)
    ang = (np.arange(T)[None, :].astype(np.float32) * inv.astype(np.float32)[f % 4][:, None]).astype(np.float64)
    root = 8.0 ** -0.25
    out["L2_cos"] = (np.cos(ang) * root).astype(np.float32)
    out["L2_sin"] = (np.sin(ang) * np.where(f % 8 < 4, -1.0, 1.0)[:, None] * root).astype(np.float32)
    k = np.arange(192)[None, :] - 64
    out["band"] = np.where((k > i) | (k < i - 64), NEG_BAND, 0.0).astype(np.float32)
    half = np.arange(0, 64, 2).astype(np.float32)
    inv = (1.0 / 10000.0 ** (half / 64)).astype(np.float32)
    t = np.arange(T).astype(np.float32)
    fr = np.concatenate([t[:, None] * inv[None, :]] * 2, axis=1).astype(np.float32).astype(np.float64)
    base = ((half + 0.4 * 64) / (1.4 * 64)).astype(np.float64)
    power = (t - T // 2) / 32.0
    sc = np.concatenate([base[None, :] ** power[:, None]] * 2, axis=1)
    sign = np.where(np.arange(64) < 32, -1.0, 1.0)[None, :]
    tabs = [np.cos(fr) * sc * 8.0, np.sin(fr) * sc * sign * 8.0, np.cos(fr) / sc, np.sin(fr) / sc * sign]
    out["L1_rotary"] = np.stack(tabs).reshape(4, NC, P, 64).transpose(2, 0, 1, 3).astype(np.float32).copy()
    return out


def layouts(a):
    out = {}
    out["L0_w_in"] = np.stack([a["L0_attn_Wq"].T, a["L0_attn_Wk"].T, a["L0_attn_Wv"].T], axis=1)
    out["L0_WoT"] = a["L0_attn_Wo"].T
    out["L0_w_gate"] = a["L0_ffn_expert_embeddings"].T
    out["L0_w1"] = a["L0_ffn_first_linear"].reshape(16, 128, 128).transpose(2, 0, 1)
    out["L0_w2"] = a["L0_ffn_second_linear"].transpose(0, 2, 1).reshape(16, 128, 128).transpose(1, 0, 2)
    out["L1_Mq"], out["L1_Mk"], out["L1_Mv"] = a["L1_attn_Mq"], a["L1_attn_Mk"], a["L1_attn_Mv"]
    out["L1_wqkv"] = a["L1_ffn_wqkv"]
    out["L1_q_scale"], out["L1_k_scale"] = a["L1_ffn_q_scale"], a["L1_ffn_k_scale"]
    out["L1_wo"] = a["L1_ffn_wo"].reshape(2, 4, 128, 128).transpose(0, 2, 1, 3)
    out["L1_ln_g"], out["L1_ln_b"] = a["L1_ffn_ln_g"].reshape(2, 128, 1), a["L1_ffn_ln_b"].reshape(2, 128, 1)
    out["L1_w1"] = a["L1_ffn_w1"]
    out["L1_b1"] = a["L1_ffn_b1"].reshape(2, 682, 1)
    out["L1_w2"] = a["L1_ffn_w2"]
    out["L1_b2"] = a["L1_ffn_b2"]
    swap = (np.arange(128) // 8) * 8 + (np.arange(128) + 4) % 8
    w, bias = a["L2_attn_Wqkv"], a["L2_attn_bqkv"]
    out["L2_w_in"] = np.stack([w[0:128].T, w[128:256].T, w[256:384].T, w[0:128][swap].T, w[128:256][swap].T], axis=1)
    out["L2_b_in"] = np.stack([bias[0:128], bias[0:128][swap], bias[128:256], bias[128:256][swap]], axis=1)
    out["L2_b_v"] = bias[256:384]
    out["L2_pre"] = np.repeat(a["L2_attn_Wpre"].T, 8, axis=0)
    out["L2_post"] = np.repeat(a["L2_attn_Wpost"].T, 8, axis=1)
    out["L2_WoutT"] = a["L2_attn_Wout"].T
    out["L2_attn_bout"] = a["L2_attn_bout"]
    out["L2f_w_gate"] = a["L2_ffn_Wg"].T
    out["L2_ffn_bg"] = a["L2_ffn_bg"]
    out["L2f_w1"] = a["L2_ffn_W1"].reshape(4, 128, 128).transpose(2, 0, 1)
    w2 = np.zeros((128, 8, 128), a["L2_ffn_W2"].dtype)
    w2[0:64, 0::2] = a["L2_ffn_W2"][0::2].transpose(2, 0, 1)
    w2[64:128, 1::2] = a["L2_ffn_W2"][1::2].transpose(2, 0, 1)
    out["L2f_w2"] = w2
    out["L3_w_in"] = a["L3_attn_W"].reshape(128, 3, 128)
    out["L3f_w_gate"] = a["L3_ffn_wg_red"].T
    out["L3_ffn_wg"] = a["L3_ffn_wg"]
    out["L3f_w1"] = a["L3_ffn_w1"].transpose(1, 0, 2).reshape(128, 32, 128)
    out["L3f_w2"] = a["L3_ffn_w2"].reshape(32, 128, 128).transpose(1, 0, 2)
    out["L3f_b1"] = a["L3_ffn_b1"].reshape(32, 128).T
    out["L3_ffn_b2"] = a["L3_ffn_b2"]
    return out


def program(nc, dram, x_in, x_out, layers, batches):
    scratch = [nc.dram_tensor(f"x_after_{n}", (batches, T, D), F32, kind="Internal").ap() for n in layers[:-1]]
    xs = [x_in] + scratch + [x_out]
    s = nc.dram_tensor("attention_out", (batches, T, D), F32, kind="Internal").ap()
    for n, layer in enumerate(layers):
        src, dst = xs[n], xs[n + 1]
        if layer == 0:
            attention_phase(nc, dram, "a0", "causal", src, s, batches)
            experts_phase(nc, dram, "f0", "capacity", src, s, dst, batches)
        elif layer == 1:
            grouped_attention_phase(nc, dram, "a1", src, s, batches)
            local_transformer_phase(nc, dram, "f1", src, s, dst, batches)
        elif layer == 2:
            attention_phase(nc, dram, "a2", "mixed", src, s, batches)
            experts_phase(nc, dram, "f2", "lora", src, s, dst, batches)
        else:
            attention_phase(nc, dram, "a3", "triu", src, s, batches)
            experts_phase(nc, dram, "f3", "top1", src, s, dst, batches)


def build(nc, inputs, layers, batches):
    arrays, dram = {}, {}
    host = {**constants(), **layouts(inputs), "x": inputs["L0_attn_x"]}
    for name, a in host.items():
        arrays[f"in_{name}"] = np.ascontiguousarray(a)
        dram[name] = nc.dram_tensor(f"in_{name}", a.shape, mybir.dt.from_np(a.dtype), kind="ExternalInput").ap()
    out = nc.dram_tensor("out", (batches, T, D), F32, kind="ExternalOutput").ap()
    program(nc, dram, dram["x"], out, layers, batches)
    return arrays


def kernel(**inputs):
    import concourse.bacc as bacc
    from concourse.bass_utils import run_bass_kernel_spmd

    nc = bacc.Bacc("TRN2", target_bir_lowering=False, num_devices=1)
    a = {name: np.asarray(value) for name, value in inputs.items()}
    arrays = build(nc, a, [0, 1, 2, 3], NB)
    r = run_bass_kernel_spmd(nc, [arrays], core_ids=[0])
    return r.results[0]["out"]
```
